# Optimizing a Trainium2 kernel written in Bass

```python
import numpy as np
import jax
import jax.numpy as jnp

def _softmax(x, axis=-1):
    return jax.nn.softmax(x, axis=axis)

def _gelu(x):
    return jax.nn.gelu(x, approximate=True)

def _silu(x):
    return jax.nn.silu(x)

def _sigmoid(x):
    return jax.nn.sigmoid(x)

def _layernorm(x, axis=-1, eps=1e-05):
    m = jnp.mean(x, axis=axis, keepdims=True)
    v = jnp.var(x, axis=axis, keepdims=True)
    return (x - m) / jnp.sqrt(v + eps)

def _scatter_add(tgt, idx, src, axis=0):
    return tgt.at[idx].add(src)

def _segment_sum(src, seg, n):
    return jax.ops.segment_sum(src, seg, n)
kernel_name = 'mk_vit_tower_postln_d1_tok_img2048_r4_60be21'

def setup_inputs(seed: int=0):
    np.random.seed(seed)
    _w = jnp.asarray

    def _rec_inputs():
        import jax
        import jax.numpy as jnp
        _rk = jax.random.key(seed)
        x = -0.00340659 + 1.00146 * jax.random.normal(jax.random.fold_in(_rk, 1), (8, 256, 64, 2), jnp.float32)
        return x
    x = _rec_inputs()

    def _L0_tok_setup():
        import jax, jax.numpy as jnp
        import numpy as np
        CH, H, N, N_SSM, SEQ_L = (1, 256, 64, 256, 512)

        def _kernel(C_ri, log_dt, B_ri, inv_A_real, A_imag, L):
            C = C_ri[..., 0] + 1j * C_ri[..., 1]
            B = B_ri[..., 0] + 1j * B_ri[..., 1]
            A = -jnp.exp(inv_A_real) + 1j * A_imag
            rep = log_dt.shape[0] // inv_A_real.shape[0]
            B = jnp.tile(B, (rep, 1))
            A = jnp.tile(A, (rep, 1))
            dt = jnp.exp(log_dt)
            dtA = A * dt[:, None]
            Ct = B[None] * C / (1.0 - dtA / 2) * dt[:, None]
            dA = (1.0 + dtA / 2) / (1.0 - dtA / 2)
            dA_log = jnp.log(dA)
            l = jnp.arange(L, dtype=jnp.float32)
            V = jnp.exp(dA_log[:, :, None] * l)
            K = 2.0 * jnp.einsum('chn,hnl->chl', Ct, V).real
            return K
        key = jax.random.key(seed)
        ks = jax.random.split(key, 5)
        return {'C_ri': jax.random.normal(ks[0], (CH, H, N, 2), dtype=jnp.float32), 'log_dt': jax.random.normal(ks[1], (H,), dtype=jnp.float32), 'B_ri': jax.random.normal(ks[2], (N_SSM, N, 2), dtype=jnp.float32), 'inv_A_real': jax.random.normal(ks[3], (N_SSM, N), dtype=jnp.float32), 'A_imag': jax.random.normal(ks[4], (N_SSM, N), dtype=jnp.float32), 'L': SEQ_L}
    _L0_tok_all = _L0_tok_setup()
    _L0_tok_in = {k: v for k, v in _L0_tok_all.items() if k in ('log_dt', 'B_ri', 'inv_A_real', 'A_imag')}
    del _L0_tok_all

    def _L0_attn_setup():
        import jax, jax.numpy as jnp
        import numpy as np
        B_, S_, E_ = (1, 512, 512)
        NH, P_, N_, G_, K_, CS = (64, 64, 128, 1, 4, 64)
        INTER = NH * P_
        CONV_DIM = INTER + 2 * G_ * N_
        PROJ = INTER + CONV_DIM + NH
        EPS = 1e-05

        def segsum(x):
            L = x.shape[-1]
            i = jnp.arange(L)
            strict = i[:, None] > i[None, :]
            X = jnp.where(strict, x[..., :, None], 0.0)
            S = jnp.cumsum(X, axis=-2)
            return jnp.where(i[:, None] >= i[None, :], S, -jnp.inf)
        key = jax.random.key(seed)
        ks = jax.random.split(key, 6)
        return {'input_states': jax.random.normal(ks[0], (B_, S_, E_), dtype=jnp.float32), 'mask': jnp.ones((B_, 1, S_), dtype=jnp.int32), 'W_in': jax.random.normal(ks[1], (PROJ, E_), dtype=jnp.float32) * 0.02, 'conv_w': jax.random.normal(ks[2], (CONV_DIM, K_), dtype=jnp.float32) * 0.2, 'conv_b': jnp.zeros((CONV_DIM,), dtype=jnp.float32), 'dt_bias': jnp.ones((NH,), dtype=jnp.float32), 'A_log': jnp.log(jnp.arange(1, NH + 1, dtype=jnp.float32)), 'D': jnp.ones((NH,), dtype=jnp.float32), 'norm_w': jnp.ones((INTER,), dtype=jnp.float32), 'W_out': jax.random.normal(ks[3], (E_, INTER), dtype=jnp.float32) * 0.02}
    _L0_attn_all = _L0_attn_setup()
    _L0_attn_in = {k: v for k, v in _L0_attn_all.items() if k in ('mask', 'W_in', 'conv_w', 'conv_b', 'dt_bias', 'A_log', 'D', 'norm_w', 'W_out')}
    del _L0_attn_all

    def _L0_ffn_setup():
        import jax, jax.numpy as jnp
        import numpy as np
        DIM_IN = 512
        DIM_HIDDEN = 2048
        key = jax.random.key(seed)
        k_x, k_g, k_u, k_d = jax.random.split(key, 4)
        s_in = 1.0 / np.sqrt(DIM_IN)
        s_hid = 1.0 / np.sqrt(DIM_HIDDEN)
        x = jax.random.normal(k_x, (4, 512, DIM_IN), dtype=jnp.float32)
        w_gate = jax.random.uniform(k_g, (DIM_HIDDEN, DIM_IN), jnp.float32, -s_in, s_in)
        w_up = jax.random.uniform(k_u, (DIM_HIDDEN, DIM_IN), jnp.float32, -s_in, s_in)
        w_down = jax.random.uniform(k_d, (DIM_IN, DIM_HIDDEN), jnp.float32, -s_hid, s_hid)
        return {'x': x, 'w_gate': w_gate, 'w_up': w_up, 'w_down': w_down}
    _L0_ffn_all = _L0_ffn_setup()
    _L0_ffn_in = {k: v for k, v in _L0_ffn_all.items() if k in ('w_gate', 'w_up', 'w_down')}
    del _L0_ffn_all
    return {'x': x, 'L0_tok_log_dt': _L0_tok_in['log_dt'], 'L0_tok_B_ri': _L0_tok_in['B_ri'], 'L0_tok_inv_A_real': _L0_tok_in['inv_A_real'], 'L0_tok_A_imag': _L0_tok_in['A_imag'], 'L0_attn_mask': _L0_attn_in['mask'], 'L0_attn_W_in': _L0_attn_in['W_in'], 'L0_attn_conv_w': _L0_attn_in['conv_w'], 'L0_attn_conv_b': _L0_attn_in['conv_b'], 'L0_attn_dt_bias': _L0_attn_in['dt_bias'], 'L0_attn_A_log': _L0_attn_in['A_log'], 'L0_attn_D': _L0_attn_in['D'], 'L0_attn_norm_w': _L0_attn_in['norm_w'], 'L0_attn_W_out': _L0_attn_in['W_out'], 'L0_ffn_w_gate': _L0_ffn_in['w_gate'], 'L0_ffn_w_up': _L0_ffn_in['w_up'], 'L0_ffn_w_down': _L0_ffn_in['w_down']}

def reference(x, L0_tok_log_dt, L0_tok_B_ri, L0_tok_inv_A_real, L0_tok_A_imag, L0_attn_mask, L0_attn_W_in, L0_attn_conv_w, L0_attn_conv_b, L0_attn_dt_bias, L0_attn_A_log, L0_attn_D, L0_attn_norm_w, L0_attn_W_out, L0_ffn_w_gate, L0_ffn_w_up, L0_ffn_w_down):
    import jax
    import jax.numpy as jnp

    def _L0_tok_ref(C_ri, log_dt, B_ri, inv_A_real, A_imag, L):
        import jax, jax.numpy as jnp
        import numpy as np
        CH, H, N, N_SSM, SEQ_L = (1, 256, 64, 256, 512)

        def _kernel(C_ri, log_dt, B_ri, inv_A_real, A_imag, L):
            C = C_ri[..., 0] + 1j * C_ri[..., 1]
            B = B_ri[..., 0] + 1j * B_ri[..., 1]
            A = -jnp.exp(inv_A_real) + 1j * A_imag
            rep = log_dt.shape[0] // inv_A_real.shape[0]
            B = jnp.tile(B, (rep, 1))
            A = jnp.tile(A, (rep, 1))
            dt = jnp.exp(log_dt)
            dtA = A * dt[:, None]
            Ct = B[None] * C / (1.0 - dtA / 2) * dt[:, None]
            dA = (1.0 + dtA / 2) / (1.0 - dtA / 2)
            dA_log = jnp.log(dA)
            l = jnp.arange(L, dtype=jnp.float32)
            V = jnp.exp(dA_log[:, :, None] * l)
            K = 2.0 * jnp.einsum('chn,hnl->chl', Ct, V).real
            return K
        return _kernel(C_ri, log_dt, B_ri, inv_A_real, A_imag, L)

    def _L0_attn_ref(input_states, mask, W_in, conv_w, conv_b, dt_bias, A_log, D, norm_w, W_out):
        import jax, jax.numpy as jnp
        import numpy as np
        B_, S_, E_ = (1, 512, 512)
        NH, P_, N_, G_, K_, CS = (64, 64, 128, 1, 4, 64)
        INTER = NH * P_
        CONV_DIM = INTER + 2 * G_ * N_
        PROJ = INTER + CONV_DIM + NH
        EPS = 1e-05

        def segsum(x):
            L = x.shape[-1]
            i = jnp.arange(L)
            strict = i[:, None] > i[None, :]
            X = jnp.where(strict, x[..., :, None], 0.0)
            S = jnp.cumsum(X, axis=-2)
            return jnp.where(i[:, None] >= i[None, :], S, -jnp.inf)
        B, S, E = input_states.shape
        proj = input_states @ W_in.T
        gate = proj[..., :INTER]
        h_BC = proj[..., INTER:INTER + CONV_DIM]
        dt = proj[..., INTER + CONV_DIM:]
        xpad = jnp.pad(h_BC, ((0, 0), (K_ - 1, 0), (0, 0)))
        conv = conv_b
        for i in range(K_):
            conv = conv + xpad[:, i:i + S, :] * conv_w[:, i]
        h_BC = jax.nn.silu(conv)
        hidden = h_BC[..., :INTER]
        Bm = h_BC[..., INTER:INTER + G_ * N_]
        Cm = h_BC[..., INTER + G_ * N_:]
        A = -jnp.exp(A_log)
        dt = jnp.clip(jax.nn.softplus(dt + dt_bias), 0.0)
        Hs = hidden.reshape(B, S, NH, P_).astype(jnp.float32)
        Bm = jnp.tile(Bm.reshape(B, S, G_, N_).astype(jnp.float32), (1, 1, NH // G_, 1))
        Cm = jnp.tile(Cm.reshape(B, S, G_, N_).astype(jnp.float32), (1, 1, NH // G_, 1))
        D_resid = D[None, None, :, None] * Hs
        Hdt = Hs * dt[..., None]
        At = A * dt
        C_ = S // CS
        Hc = Hdt.reshape(B, C_, CS, NH, P_)
        Ac = At.reshape(B, C_, CS, NH)
        Bc = Bm.reshape(B, C_, CS, NH, N_)
        Cc = Cm.reshape(B, C_, CS, NH, N_)
        Ap = jnp.transpose(Ac, (0, 3, 1, 2))
        A_cum = jnp.cumsum(Ap, axis=-1)
        L_tri = jnp.exp(segsum(Ap))
        Gm = jnp.einsum('bclhn,bcshn->bclsh', Cc, Bc)
        M = Gm * jnp.transpose(L_tri, (0, 2, 3, 4, 1))
        Yd = jnp.einsum('bclsh,bcshp->bclhp', M, Hc)
        decay = jnp.exp(A_cum[..., -1:] - A_cum)
        Bd = Bc * jnp.transpose(decay, (0, 2, 3, 1))[..., None]
        states = jnp.einsum('bclhn,bclhp->bchpn', Bd, Hc)
        Sd = jnp.transpose(jnp.exp(A_cum), (0, 2, 3, 1))
        Yoff = jnp.einsum('bclhn,bchpn->bclhp', Cc, states) * Sd[..., None]
        y = (Yd + Yoff).reshape(B, S, NH, P_) + D_resid
        y = y.reshape(B, S, INTER)
        yf = y.astype(jnp.float32) * jax.nn.silu(gate.astype(jnp.float32))
        var = jnp.mean(yf * yf, axis=-1, keepdims=True)
        yn = norm_w * (yf * jax.lax.rsqrt(var + EPS))
        return yn @ W_out.T

    def _L0_ffn_ref(x, w_gate, w_up, w_down):
        import jax, jax.numpy as jnp
        import numpy as np
        DIM_IN = 512
        DIM_HIDDEN = 2048
        gate = jnp.einsum('bsd,hd->bsh', x, w_gate)
        up = jnp.einsum('bsd,hd->bsh', x, w_up)
        gated = jax.nn.silu(gate) * up
        return jnp.einsum('bsh,dh->bsd', gated, w_down)
    h = _L0_tok_ref(x, L0_tok_log_dt, L0_tok_B_ri, L0_tok_inv_A_real, L0_tok_A_imag, 512)
    h = _layernorm(h + _L0_attn_ref(h, L0_attn_mask, L0_attn_W_in, L0_attn_conv_w, L0_attn_conv_b, L0_attn_dt_bias, L0_attn_A_log, L0_attn_D, L0_attn_norm_w, L0_attn_W_out), axis=-1)
    h = _layernorm(h + _L0_ffn_ref(h, L0_ffn_w_gate, L0_ffn_w_up, L0_ffn_w_down), axis=-1)
    return h

_drawn_inputs = setup_inputs


def setup_inputs(seed=0):
    import zlib

    import numpy as np

    out = dict(_drawn_inputs(seed))
    spreads = {'L0_attn_conv_b': (0.0, 0.1),
     'L0_attn_dt_bias': (1.0, 0.6),
     'L0_attn_D': (1.0, 0.2),
     'L0_attn_norm_w': (1.0, 0.2)}
    factors = {'L0_attn_A_log': 5.031}
    for name, (base, spread) in spreads.items():
        noise = np.random.default_rng([zlib.crc32(name.encode()), seed]).standard_normal(out[name].shape)
        drawn = base * np.exp(spread * noise) if base else spread * noise
        out[name] = jnp.asarray(drawn.astype(out[name].dtype))
    for name, factor in factors.items():
        out[name] = (out[name] * factor).astype(out[name].dtype)
    return out
```

```python
from contextlib import ExitStack

import concourse.bass as bass
from concourse import mybir

F32 = mybir.dt.float32
F32R = mybir.dt.float32r
ALU = mybir.AluOpType
ACT = mybir.ActivationFunctionType

P = 128
NB, H, NS = 8, 256, 64
E = 512
TOK = NB * H
KE = E // P
INTER, HEADS, HD = 4096, 64, 64
NJ = INTER // P
TAPS = 4
CHUNK = 64
TBW = 512
NT = TOK // TBW
CP = TBW // P
TT = TOK // P
NM = 2048 // P
NPAR = 8
EPS = 1e-5
A_LO, A_HI, LB = 4, 4, 32


UNITS = NJ * NT
FUNITS = NM * NT
BODY = 8


class Shared:
    pass


def count(i, k, per=1, more=0):
    if isinstance(i, int):
        return per * (BODY * i + k) + more
    return i * (per * BODY) + (per * k + more)


def wait(eng, sem, value):
    if isinstance(value, int) and value <= 0:
        return
    eng.wait_ge(sem, value)


def values(eng, *v):
    return [x if isinstance(x, int) else eng.snap(x) for x in v]


def alive(i, k, units):
    return not isinstance(i, int) or 0 <= BODY * i + k < units


def steps(eng, step, units, tail):
    bodies = units // BODY
    for k in range(BODY):
        step(0, k)
    with eng.Fori(1, bodies - 1) as i:
        for k in range(BODY):
            step(i, k)
    for k in range(BODY):
        step(bodies - 1, k)
    for k in range(tail):
        step(bodies, k)


def phase_token(nc, d, g):
    with ExitStack() as ctx:
        def sb(name, shape, dt=F32):
            return ctx.enter_context(nc.sbuf_tensor(name, shape, dt))

        def sem(name):
            return ctx.enter_context(nc.semaphore(name))

        x = sb("x", [P, H, NB])
        V1 = sb("V1", [P, H, LB])
        V2 = sb("V2", [P, H, LB])
        Q = sb("Q", [P, 2, H, A_LO, A_HI])
        HG = 8
        T = sb("T", [P, 2, 2, HG, A_LO * A_HI, NB])
        X2 = sb("X2", [P, 2, 2 * HG, A_HI, NB])
        Vs = sb("Vs", [P, 2, 2, 2 * HG, LB])
        Y = sb("Y", [P, 2, 4, P])
        par = Vs[:].rearrange("p a r h b -> p (a r h b)")[:, 0:5 * H].rearrange("p (k h) -> p k h", h=H)
        w_lo = Y[:].rearrange("p a m c -> p (a m c)").rearrange("p (k h) -> p k h", h=H)
        w_hi = X2[:].rearrange("p a h k c -> p (a h k c)").rearrange("p (k h) -> p k h", h=H)
        W = lambda i: w_lo[:, i, :] if i < 4 else w_hi[:, i - 4, :]
        ps = [ctx.enter_context(nc.psum_tensor(f"tok_ps{i}", [P, 4, P], F32)) for i in range(2)]
        pt = [ctx.enter_context(nc.psum_tensor(f"tok_pt{i}", [P, 2 * HG, LB], F32)) for i in range(2)]
        s_vs = sem("tok_vs")
        s_y = sem("tok_y")
        s_tr = sem("tok_tr")
        s_in = sem("tok_in")
        s_exp = sem("tok_exp")
        s_dv = sem("tok_dv")
        s_v = sem("tok_v")
        s_T = sem("tok_T")
        s_mm = sem("tok_mm")
        s_x2 = sem("tok_x2")
        s_hi = sem("tok_hi")
        s_lo = sem("tok_lo")
        block = ctx.enter_context(nc.Block())
        flat = T[:].rearrange("p a b h m c -> p (a b h m c)")

        @block.sync
        def _(sp):
            sp.dma_start(par[:, 0, :], d["log_dt"].partition_broadcast(P)).then_inc(s_in, 16)
            for half in range(2):
                rows = slice(64 * half, 64 * half + 64)
                sp.dma_start(par[rows, 1:5, :], d["tokpar"]).then_inc(s_in, 16)
            sp.dma_start(x[:], d["x"]).then_inc(s_in, 16)

        @block.scalar
        def _(act):
            act.wait_ge(s_in, 64)
            nc.scalar.activation(W(0), par[:, 0, :], ACT.Exp).then_inc(s_exp, 1)
            nc.scalar.activation(W(1), par[:, 1, :], ACT.Exp).then_inc(s_exp, 1)

            def copy_v(n, slot, first):
                if not first:
                    act.wait_ge(s_mm, 2 * n - 2)
                h = bass.ds(n * (2 * HG), 2 * HG)
                nc.scalar.activation(Vs[:, slot, 0], V1[:, h, :], ACT.Copy).then_inc(s_vs, 1)
                nc.scalar.activation(Vs[:, slot, 1], V2[:, h, :], ACT.Copy).then_inc(s_vs, 1)

            def take(n, slot, first):
                act.wait_ge(s_mm, 2 * n + 2)
                if not first:
                    act.wait_ge(s_tr, n - 1)
                nc.scalar.activation(Y[:, slot], ps[slot][:], ACT.Copy).then_inc(s_y, 1)

            def high(n, slot):
                act.wait_ge(s_x2, n + 1)
                nc.scalar.activation(
                    g.hhi[:].rearrange("p k (c h) -> p k c h", c=NB)[:, :, :, bass.ds(n * (2 * HG), 2 * HG)],
                    X2[:, slot].rearrange("p h k c -> p k c h"), ACT.Copy).then_inc(s_hi, 1)

            act.wait_ge(s_v, 1)
            last = H // (2 * HG)
            copy_v(0, 0, True)
            copy_v(1, 1, True)
            take(0, 0, True)
            copy_v(2, 0, False)
            take(1, 1, True)
            high(0, 0)
            with act.Fori(1, last // 2 - 1) as i:
                for k in range(2):
                    copy_v(i * 2 + (k + 1), 1 - k, False)
                    take(i * 2 + k, k, False)
                    high(i * 2 + k - 1 if k else i * 2 - 1, 1 - k)
            copy_v(last - 1, 1, False)
            take(last - 2, 0, False)
            high(last - 3, 1)
            take(last - 1, 1, False)
            high(last - 2, 0)
            high(last - 1, 1)

        @block.vector
        def _(dve):
            chain = [0]

            def after(ins):
                chain[0] += 1
                ins.then_inc(s_dv, 1)
                dve.wait_ge(s_dv, chain[0])

            tt = nc.vector.tensor_tensor
            ts = nc.vector.tensor_scalar
            stt = nc.vector.scalar_tensor_tensor
            dve.wait_ge(s_exp, 2)
            after(stt(W(2), W(1), -0.5, W(0), ALU.mult, ALU.mult))
            after(stt(W(3), par[:, 2, :], 0.5, W(0), ALU.mult, ALU.mult))
            after(ts(W(4), W(2), -1.0, 1.0, ALU.mult, ALU.add))
            after(tt(W(5), W(3), W(3), ALU.mult))
            after(tt(W(6), W(4), W(4), ALU.mult))
            after(tt(W(6), W(6), W(5), ALU.add))
            after(nc.vector.reciprocal(W(6), W(6)))
            after(stt(W(0), W(0), 2.0, W(6), ALU.mult, ALU.mult))
            after(tt(W(1), par[:, 3, :], W(4), ALU.mult))
            after(tt(W(7), par[:, 4, :], W(3), ALU.mult))
            after(tt(W(1), W(1), W(7), ALU.subtract))
            after(tt(Q[:, 0, :, 0, 0], W(1), W(0), ALU.mult))
            after(tt(W(1), par[:, 3, :], W(3), ALU.mult))
            after(tt(W(7), par[:, 4, :], W(4), ALU.mult))
            after(tt(W(1), W(1), W(7), ALU.add))
            after(tt(Q[:, 1, :, 0, 0], W(1), W(0), ALU.mult))
            after(stt(W(1), W(2), 1.0, W(4), ALU.add, ALU.mult))
            after(tt(W(1), W(1), W(5), ALU.subtract))
            after(tt(W(0), W(1), W(6), ALU.mult))
            after(stt(W(1), W(3), 2.0, W(6), ALU.mult, ALU.mult))
            mr, mi, nr, ni = 0, 1, 2, 3

            def square(mr, mi, nr, ni):
                after(tt(W(4), W(mr), W(mr), ALU.mult))
                after(tt(W(5), W(mi), W(mi), ALU.mult))
                after(tt(W(nr), W(4), W(5), ALU.subtract))
                after(stt(W(ni), W(mr), 2.0, W(mi), ALU.mult, ALU.mult))

            after(nc.vector.memset(V1[0:64, :, 0], 1.0))
            after(nc.vector.memset(V1[64:128, :, 0], 0.0))
            after(nc.vector.memset(V2[0:64, :, 0], 0.0))
            after(nc.vector.memset(V2[64:128, :, 0], -1.0))

            def grow(re, im, out_re, out_im, n, sign):
                dims = [int(v) for v in re.shape[1:]]
                size = dims[0] * (dims[1] if len(dims) > 1 else 1)
                t0 = flat[:, 0:size].rearrange("p (h b) -> p h b", h=dims[0])
                t1 = flat[:, 2048:2048 + size].rearrange("p (h b) -> p h b", h=dims[0])
                r = W(mr)[:, n].unsqueeze(2).to_broadcast([P] + dims)
                i = W(mi)[:, n].unsqueeze(2).to_broadcast([P] + dims)
                tt(out_re, re, r, ALU.mult).then_inc(s_dv, 1)
                tt(t0, im, i, ALU.mult).then_inc(s_dv, 1)
                tt(out_im, im, r, ALU.mult).then_inc(s_dv, 1)
                chain[0] += 3
                after(tt(t1, re, i, ALU.mult))
                tt(out_re, out_re, t0, ALU.add if sign > 0 else ALU.subtract).then_inc(s_dv, 1)
                chain[0] += 1
                after(tt(out_im, out_im, t1, ALU.subtract if sign > 0 else ALU.add))

            b = 1
            while b < LB:
                step = min(H, 2048 // b)
                for h0 in range(0, H, step):
                    hs = slice(h0, h0 + step)
                    grow(V1[:, hs, 0:b], V2[:, hs, 0:b], V1[:, hs, b:2 * b], V2[:, hs, b:2 * b], hs, 1)
                square(mr, mi, nr, ni)
                mr, mi, nr, ni = nr, ni, mr, mi
                b *= 2
            al = slice(0, H)
            grow(Q[:, 0, :, 0, 0:1], Q[:, 1, :, 0, 0:1], Q[:, 0, :, 1, 0:1], Q[:, 1, :, 1, 0:1], al, -1)
            square(mr, mi, nr, ni)
            mr, mi, nr, ni = nr, ni, mr, mi
            grow(Q[:, 0, :, 0:2, 0], Q[:, 1, :, 0:2, 0], Q[:, 0, :, 2:4, 0], Q[:, 1, :, 2:4, 0], al, -1)
            square(mr, mi, nr, ni)
            mr, mi, nr, ni = nr, ni, mr, mi
            grow(Q[:, 0, :, :, 0], Q[:, 1, :, :, 0], Q[:, 0, :, :, 1], Q[:, 1, :, :, 1], al, -1)
            square(mr, mi, nr, ni)
            mr, mi, nr, ni = nr, ni, mr, mi
            for hi_ in range(2):
                grow(Q[:, 0, :, :, hi_], Q[:, 1, :, :, hi_], Q[:, 0, :, :, 2 + hi_], Q[:, 1, :, :, 2 + hi_], al, -1)
            nc.vector.memset(W(7)[:, 0:1], 0.0).then_inc(s_v, 1)

            Qm = Q[:].rearrange("p r h a b -> p r h (a b)")

            def products(n, slot, first):
                if not first:
                    dve.wait_ge(s_mm, n - 1)
                h = bass.ds(n * HG, HG)
                for r in range(2):
                    tt(T[:, slot, r], x[:, h, :].unsqueeze(2).to_broadcast([P, HG, 16, NB]),
                       Qm[:, r, h, :].unsqueeze(3).to_broadcast([P, HG, 16, NB]), ALU.mult).then_inc(s_T, 1)

            def finish(n, slot, first):
                dve.wait_ge(s_tr, n + 1)
                if not first:
                    dve.wait_ge(s_hi, n - 1)
                    dve.wait_ge(s_lo, n - 1)
                nc.vector.transpose(X2[:, slot].rearrange("p h k c -> p h (k c)"), pt[slot][:]).then_inc(s_x2, 1)
                dve.wait_ge(s_hi, n + 1)
                h = bass.ds(n * (2 * HG), 2 * HG)
                for_c = lambda t: t.rearrange("p k (c h) -> p k c h", c=NB)[:, :, :, h]
                tt(for_c(g.hlo[:]), X2[:, slot].rearrange("p h k c -> p k c h"), for_c(g.hhi[:].bitcast(F32)),
                   ALU.subtract).then_inc(s_lo, 1)

            last = H // (2 * HG)
            for n in range(4):
                products(n, n % 2, n < 2)
            finish(0, 0, True)
            products(4, 0, False)
            products(5, 1, False)
            finish(1, 1, True)
            with dve.Fori(1, last // 2 - 1) as i:
                for k in range(2):
                    products(i * 4 + (2 * k + 2), 0, False)
                    products(i * 4 + (2 * k + 3), 1, False)
                    finish(i * 2 + k, k, False)
            products(2 * last - 2, 0, False)
            products(2 * last - 1, 1, False)
            finish(last - 2, 0, False)
            finish(last - 1, 1, False)

        @block.tensor
        def _(pe):
            def sums(n, slot, first):
                pe.wait_ge(s_vs, 2 * n + 2)
                if not first:
                    pe.wait_ge(s_y, n - 1)
                for half in range(2):
                    pe.wait_ge(s_T, 4 * n + (2 * half + 2))
                    for m in range(HG):
                        at = half * HG + m
                        q = at % 4
                        for r in range(2):
                            mm = nc.tensor.matmul(ps[slot][32 * q:32 * q + 32, at // 4, :], Vs[:, slot, r, at, :],
                                                  T[:, half, r, m].rearrange("p a c -> p (a c)"),
                                                  start=(r == 0), stop=(r == 1), skip_group_check=True)
                    mm.then_inc(s_mm, 1)

            def turn(n, slot, first):
                pe.wait_ge(s_y, n + 1)
                if not first:
                    pe.wait_ge(s_x2, n - 1)
                for m in range(4):
                    mm = nc.tensor.transpose(pt[slot][:, 4 * m:4 * m + 4, :].rearrange("p h b -> p (h b)"), Y[:, slot, m, :], g.ident[:])
                mm.then_inc(s_tr, 1)

            last = H // (2 * HG)
            sums(0, 0, True)
            sums(1, 1, True)
            turn(0, 0, True)
            sums(2, 0, False)
            turn(1, 1, True)
            with pe.Fori(1, last // 2 - 1) as i:
                for k in range(2):
                    sums(i * 2 + (k + 1), 1 - k, False)
                    turn(i * 2 + k, k, False)
            sums(last - 1, 1, False)
            turn(last - 2, 0, False)
            turn(last - 1, 1, False)



def phase_constants(nc, d, g):
    with ExitStack() as ctx:
        s_in = ctx.enter_context(nc.semaphore("const_in"))
        s_r = ctx.enter_context(nc.semaphore("const_r"))
        block = ctx.enter_context(nc.Block())

        @block.sync
        def _(sp):
            sp.dma_start(g.ident[:], d["ident"]).then_inc(s_in, 16)
            sp.wait_ge(s_in, 16)

        @block.scalar
        def _(act):
            act.wait_ge(s_in, 16)
            nc.scalar.activation(g.identr[:], g.ident[:], ACT.Copy).then_inc(s_r, 1)


def split_matmuls(nc, out, whi, wlo, g, w_of, h_of):
    for k in range(KE):
        mm = None
        for n, (w, h) in enumerate(((whi, g.hhi), (whi, g.hlo), (wlo, g.hhi))):
            mm = nc.tensor.matmul(out, w_of(w, k), h_of(h, k), start=(k == 0 and n == 0),
                                  stop=(k == KE - 1 and n == 2))
    return mm


def phase_decays(nc, d, g):
    with ExitStack() as ctx:
        def sb(name, shape, dt=F32):
            return ctx.enter_context(nc.sbuf_tensor(name, shape, dt))

        def sem(name):
            return ctx.enter_context(nc.semaphore(name))

        w = sb("bc_w", [P, 2 * E + HEADS * KE])
        whi = sb("bc_whi", [P, 2 * E + HEADS * KE], F32R)
        wlo = sb("bc_wlo", [P, 2 * E + HEADS * KE], F32R)
        par = sb("bc_par", [P, 2, NPAR])
        hd = sb("hd_par", [P, 2, HEADS])
        msk = sb("msk", [P, P + 1])
        names = ["xb", "ex", "un", "ln", "dt", "a", "z0"]
        t = {n: sb("dc_" + n, [P, TT, HEADS]) for n in names}
        packed = sb("packed", [P, NJ, 2, NT, 2, CP])
        eT = sb("eT", [HEADS, 2, NT, CP, CHUNK])
        raw = sb("bc_raw", [P, 2, 3 + H])
        cv = sb("bc_cv", [P, 2, H])
        BC = sb("BC", [P, 2, TOK])
        pd = [ctx.enter_context(nc.psum_tensor(f"pd{i}", [P, 8, HEADS], F32)) for i in range(2)]
        ph = [ctx.enter_context(nc.psum_tensor(f"pb{i}", [P, TBW], F32)) for i in range(2)]
        pm = [ctx.enter_context(nc.psum_tensor(f"pm{i}", [P, 8, HEADS], F32)) for i in range(2)]
        pe_t = [ctx.enter_context(nc.psum_tensor(f"pet{i}", [P, TBW], F32)) for i in range(2)]
        s_w = sem("bc_in_w")
        s_in = sem("bc_in")
        s_hi = sem("bc_hi")
        s_lo = sem("bc_lo")
        s_pd = sem("bc_pd")
        s_ph = sem("bc_ph")
        s_raw = sem("bc_raw_s")
        s_pad = sem("bc_pad")
        s_cv0 = sem("bc_cv0")
        s_conv = sem("bc_conv")
        s_bc = sem("bc_bc")
        s_d = sem("bc_d")
        s_x = sem("bc_x")
        s_pm = sem("bc_pm")
        s_pt = sem("bc_pt")
        s_eT = sem("bc_eT")
        s_neg = sem("bc_neg")
        s_zero = sem("bc_zero")
        s_G = sem("bc_G")
        s_Gc = sem("bc_Gc")
        s_out = sem("bc_out")
        block = ctx.enter_context(nc.Block())
        wk = lambda x, i, k: x[:, E * i + P * k:E * i + P * (k + 1)]
        wd = lambda x, k: x[:, 2 * E + HEADS * k:2 * E + HEADS * (k + 1)]

        @block.sync
        def _(sp):
            sp.dma_start(w[:], d["w_bc"]).then_inc(s_w, 16)
            sp.dma_start(par[:], d["par_bc"]).then_inc(s_in, 16)
            sp.dma_start(hd[:, 0, :], d["A_log"].partition_broadcast(P)).then_inc(s_in, 16)
            sp.dma_start(hd[:, 1, :], d["dt_bias"].partition_broadcast(P)).then_inc(s_in, 16)
            sp.dma_start(msk[:], d["mask"]).then_inc(s_in, 16)
            sp.wait_ge(s_zero, 1)
            for h2 in range(2):
                for q in range(2):
                    sp.dma_start(d["decay"][:, q, :, h2, :], eT[h2:HEADS:2, q].rearrange("j t c l -> j t (c l)")).then_inc(s_out, 16)
            sp.wait_ge(s_d, 14)
            sp.dma_start(d["dtz"].rearrange("j p n -> p j n"), packed[:].rearrange("p j a t h c -> p j (a t h c)")).then_inc(s_out, 16)
            sp.wait_ge(s_out, 80)

        @block.scalar
        def _(act):
            act.wait_ge(s_w, 16)
            nc.scalar.activation(whi[:], w[:], ACT.Copy).then_inc(s_hi, 1)
            act.wait_ge(s_in, 64)
            nc.scalar.activation(hd[:, 0, :], hd[:, 0, :], ACT.Exp).then_inc(s_x, 1)
            act.wait_ge(s_d, 3)
            nc.scalar.activation(t["ex"][:], t["un"][:], ACT.Exp).then_inc(s_x, 1)
            act.wait_ge(s_d, 4)
            nc.scalar.activation(t["ln"][:], t["un"][:], ACT.Ln).then_inc(s_x, 1)
            act.wait_ge(s_d, 10)
            nc.scalar.activation(t["ex"][:], t["a"][:], ACT.Exp).then_inc(s_x, 1)
            for n in range(2):
                act.wait_ge(s_pm, n + 1)
                nc.scalar.activation(t["z0"][:, 8 * n:8 * n + 8, :], pm[n][:], ACT.Exp).then_inc(s_x, 1)
            for tb in range(NT):
                act.wait_ge(s_pt, tb + 1)
                nc.scalar.activation(eT[:, :, tb], pe_t[tb % 2][0:HEADS, :].rearrange("p (c q l) -> p q c l", c=CP, q=2),
                                     ACT.Copy).then_inc(s_eT, 1)
            act.wait_ge(s_pad, 1)
            for n in range(2 * NT):
                i, tb = n // NT, n % NT
                act.wait_ge(s_ph, n + 1)
                if n:
                    act.wait_ge(s_conv, 3 * n)
                nc.scalar.activation(raw[:, :, 3:], ph[n % 2][:].rearrange("p (c h) -> p c h", c=2), ACT.Copy).then_inc(s_raw, 1)
                if n:
                    act.wait_ge(s_bc, n)
                nc.scalar.activation(cv[:].rearrange("p c h -> p (c h)"), ph[n % 2][:], ACT.Identity,
                                     bias=par[:, i, 4:5], scale=par[:, i, 3:4]).then_inc(s_cv0, 1)
                act.wait_ge(s_conv, 3 * n + 3)
                nc.scalar.activation(BC[:, i, TBW * tb:TBW * tb + TBW], cv[:].rearrange("p c h -> p (c h)"), ACT.Silu).then_inc(s_bc, 1)

        @block.vector
        def _(dve):
            tt = nc.vector.tensor_tensor
            stt = nc.vector.scalar_tensor_tensor
            ts = nc.vector.tensor_scalar
            nc.vector.memset(raw[:, :, 0:3], 0.0).then_inc(s_pad, 1)
            nc.vector.memset(g.G[:], 0.0).then_inc(s_pad, 1)
            dve.wait_ge(s_hi, 1)
            tt(wlo[:], w[:], whi[:].bitcast(F32), ALU.subtract).then_inc(s_lo, 1)
            dve.wait_ge(s_in, 64)
            for n in range(2):
                dve.wait_ge(s_pd, n + 1)
                tt(t["xb"][:, 8 * n:8 * n + 8, :], pd[n][:], hd[:, 1:2, :].to_broadcast([P, 8, HEADS]), ALU.add).then_inc(s_d, 1)
            dve.wait_ge(s_x, 1)
            ts(hd[:, 0, :], hd[:, 0, :], -1.0, None, ALU.mult).then_inc(s_neg, 1)
            dve.wait_ge(s_d, 2)
            stt(t["un"][:], t["xb"][:], -1.0, t["xb"][:], ALU.mult, ALU.min).then_inc(s_d, 1)
            dve.wait_ge(s_x, 2)
            ts(t["un"][:], t["ex"][:], 1.0, None, ALU.add).then_inc(s_d, 1)
            dve.wait_ge(s_d, 4)
            stt(t["dt"][:], t["un"][:], -1.0, t["ex"][:], ALU.add, ALU.subtract).then_inc(s_d, 1)
            dve.wait_ge(s_x, 3)
            nc.vector.reciprocal(t["un"][:], t["un"][:]).then_inc(s_d, 1)
            dve.wait_ge(s_d, 6)
            tt(t["dt"][:], t["dt"][:], t["un"][:], ALU.mult).then_inc(s_d, 1)
            dve.wait_ge(s_d, 7)
            tt(t["ln"][:], t["ln"][:], t["dt"][:], ALU.subtract).then_inc(s_d, 1)
            dve.wait_ge(s_d, 8)
            stt(t["dt"][:], t["xb"][:], 0.0, t["ln"][:], ALU.max, ALU.add).then_inc(s_d, 1)
            dve.wait_ge(s_d, 9)
            dve.wait_ge(s_neg, 1)
            stt(t["a"][:], t["dt"][:], 0.0,
                hd[:, 0:1, :].to_broadcast([P, TT, HEADS]), ALU.max, ALU.mult).then_inc(s_d, 1)
            for h2 in range(2):
                ts(packed[:, :, 0, :, h2, :], t["dt"][:].rearrange("p (t c) (j h) -> p j t c h", t=NT, h=2)[:, :, :, :, h2],
                   0.0, None, ALU.max).then_inc(s_d, 1)
            dve.wait_ge(s_x, 6)
            for h2 in range(2):
                ts(packed[:, :, 1, :, h2, :], t["z0"][:].rearrange("p (t c) (j h) -> p j t c h", t=NT, h=2)[:, :, :, :, h2],
                   msk[:, P:P + 1], None, ALU.add).then_inc(s_d, 1)
            dve.wait_ge(s_eT, NT)
            nc.vector.memset(eT[:, :, :, :, 0], 0.0).then_inc(s_zero, 1)
            for n in range(2 * NT):
                i = n // NT
                dve.wait_ge(s_raw, n + 1)
                dve.wait_ge(s_cv0, n + 1)
                for tap in range(3):
                    if tap:
                        dve.wait_ge(s_conv, 3 * n + tap)
                    stt(cv[:], raw[:, :, tap:tap + H], par[:, i, tap:tap + 1], cv[:], ALU.mult, ALU.add).then_inc(s_conv, 1)
            dve.wait_ge(s_pad, 2)
            for n in range(CP):
                dve.wait_ge(s_G, n + 1)
                for q in range(2):
                    rows = slice(64 * q, 64 * q + 64)
                    nc.vector.tensor_copy(g.G[rows, CP * n:CP * n + CP, q, :],
                                          ph[n % 2][:].rearrange("p (c m) -> p c m", c=CP)[rows, :, 64 * q:64 * q + 64]).then_inc(s_Gc, 1)

        @block.tensor
        def _(pe):
            pe.wait_ge(s_hi, 1)
            pe.wait_ge(s_lo, 1)
            for n in range(TT):
                for k in range(KE):
                    for m, (h, x) in enumerate(((g.hhi, whi), (g.hlo, whi), (g.hhi, wlo))):
                        mm = nc.tensor.matmul(pd[n // 8][:, n % 8, :], h[:, k, P * n:P * n + P], wd(x, k),
                                              start=(k == 0 and m == 0), stop=(k == KE - 1 and m == 2))
                if n % 8 == 7:
                    mm.then_inc(s_pd, 1)

            def project(n):
                i, tb = n // NT, n % NT
                if n >= 2:
                    pe.wait_ge(s_cv0, n - 1)
                    pe.wait_ge(s_raw, n - 1)
                split_matmuls(nc, ph[n % 2][:], whi, wlo, g, lambda x, k: wk(x, i, k),
                              lambda h, k: h[:, k, TBW * tb:TBW * tb + TBW]).then_inc(s_ph, 1)

            project(0)
            project(1)
            pe.wait_ge(s_d, 10)
            pe.wait_ge(s_in, 64)
            for n in range(2):
                nc.tensor.matmul(pm[n][:].rearrange("p t h -> p (t h)"), msk[:, 0:P],
                                 t["a"][:, 8 * n:8 * n + 8, :].rearrange("p t h -> p (t h)"), start=True, stop=True).then_inc(s_pm, 1)
            pe.wait_ge(s_x, 4)
            for tb in range(NT):
                if tb >= 2:
                    pe.wait_ge(s_eT, tb - 1)
                for c in range(CP):
                    mm = nc.tensor.transpose(pe_t[tb % 2][0:HEADS, P * c:P * c + P], t["ex"][:, CP * tb + c, :], g.ident[:])
                mm.then_inc(s_pt, 1)
            for n in range(2, 2 * NT):
                project(n)
            pe.wait_ge(s_bc, 2 * NT)
            for n in range(CP):
                if n >= 2:
                    pe.wait_ge(s_Gc, 2 * n - 2)
                for c in range(CP):
                    at = slice(P * (CP * n + c), P * (CP * n + c + 1))
                    mm = nc.tensor.matmul(ph[n % 2][:, P * c:P * c + P], BC[:, 0, at], BC[:, 1, at], start=True, stop=True)
                mm.then_inc(s_G, 1)


def phase_mixer(nc, d, g):
    with ExitStack() as ctx:
        def sb(name, shape, dt=F32):
            return ctx.enter_context(nc.sbuf_tensor(name, shape, dt))

        def sem(name):
            return ctx.enter_context(nc.semaphore(name))

        def bank(name):
            return ctx.enter_context(nc.psum_tensor(name, [P, TBW], F32))

        wst = sb("wst", [P, 2 * E + NPAR])
        whi = sb("whi", [P, 2, 2 * E], F32R)
        wlo = sb("wlo", [P, 2, 2 * E], F32R)
        par = sb("par_j", [P, 2, NPAR])
        wost = sb("wost", [P, 2, E])
        wohi = sb("wohi", [P, 2, E], F32R)
        wolo = sb("wolo", [P, 2, E], F32R)
        dtz = sb("dtz_j", [P, 2, 2, NT, 2 * CP])
        raw = sb("raw", [P, 2, 3 + H])
        cv = sb("cv", [P, 2, H])
        hs = sb("hs", [P, 2, TBW])
        sg = sb("sg", [P, 2, TBW])
        Hdt = sb("Hdt", [P, 2, CP, 2, HD])
        dec = sb("dec", [P, 2, TBW])
        one = sb("one", [P, 2 * CP, CHUNK])
        Z = sb("Z", [P, 2, CP, CHUNK])
        M = sb("M", [P, 2, CP, 2, CHUNK])
        y = sb("y", [P, 2, TBW])
        ye = [sb(f"ye{i}", [P, NT, TBW], F32R) for i in range(2)]
        yo = [sb(f"yo{i}", [P, 2, TBW], F32R) for i in range(2)]
        sq = sb("sq", [P, TBW])
        ph = [bank(f"ph{i}") for i in range(2)]
        pg = [bank(f"pg{i}") for i in range(2)]
        tr, Yp = bank("tr"), bank("Yp")
        po = [bank(f"po{i}") for i in range(2)]
        s = {n: sem("mx_" + n) for n in (
            "w", "wo", "dtz", "dec0", "dec1", "init", "whi", "wlo", "par", "wohi", "wolo", "Ah", "Ag", "raw", "cv0",
            "conv", "hs", "sg", "tr", "Hdt", "one", "Z", "M", "Y", "y", "yhi", "ylo", "sq", "sqa", "po", "acc", "pat")}
        block = ctx.enter_context(nc.Block())
        flat = lambda x: x.rearrange("p c h -> p (c h)")

        def y_of(k, part):
            return ye[part][:, k % NT, :] if (k // NT) % 2 == 0 else yo[part][:, k % 2, :]

        def y_free(i, k):
            tb = k % NT
            pair = i if k >= 0 else i - 1
            return count(pair, 0, 2, 4 * tb - (12 if (k // NT) % 2 == 0 else 4))

        @block.sync
        def _(sp):
            def load_w(j):
                sp.dma_start(wst[:], d["w_mix"][bass.ds(j, 1)].rearrange("a p n -> (a p) n")).then_inc(s["w"], 16)

            def load_dtz(j, slot):
                sp.dma_start(dtz[:, slot].rearrange("p a t n -> p (a t n)"), d["dtz"][bass.ds(j, 1)].rearrange("a p n -> (a p) n")).then_inc(s["dtz"], 16)

            def load_wo(pair):
                sp.dma_start(wost[:], d["w_out"][bass.ds(pair, 1)].rearrange("a m p n -> p (a m) n")).then_inc(s["wo"], 16)

            def load_dec(j, tb, slot):
                for q in range(2):
                    sp.dma_start(dec[64 * q:64 * q + 64, slot, :],
                                 d["decay"][bass.ds(j, 1), q, tb].rearrange("a h n -> a (h n)").to_broadcast([64, TBW])).then_inc(s[f"dec{slot}"], 16)

            sp.dma_start(one[:, 0, :], d["eye64"]).then_inc(s["pat"], 16)
            load_w(0)
            load_dtz(0, 0)
            load_dec(0, 0, 0)
            load_wo(0)

            def step(i, k):
                done, j, next_j, before, landed, pair = values(sp, count(i, k), i * 2 + (k + 1) // NT, i * 2 + (k // NT + 1),
                                                               count(i, k - 1), count(i, k - 1, 4, 16), i + 1)
                if alive(i, k + 1, UNITS):
                    wait(sp, s["Z"], done)
                    load_dec(j, (k + 1) % NT, (k + 1) % 2)
                if k % NT == 0 and alive(i, k + NT, UNITS):
                    sp.wait_ge(s["whi"], next_j)
                    sp.wait_ge(s["wlo"], next_j)
                    sp.wait_ge(s["par"], next_j)
                    load_w(next_j)
                if k % NT == 1 and alive(i, k + NT, UNITS):
                    wait(sp, s["dtz"], landed)
                    wait(sp, s["Hdt"], before)
                    wait(sp, s["Z"], before)
                    load_dtz(next_j, (k // NT + 1) % 2)
                if k == 4 and alive(i, BODY, UNITS):
                    both = values(sp, i * 2 + 2)[0]
                    sp.wait_ge(s["wohi"], both)
                    sp.wait_ge(s["wolo"], both)
                    load_wo(pair)

            steps(sp, step, UNITS, 0)

        @block.scalar
        def _(act):
            def split_w(j, slot):
                act.wait_ge(s["w"], j * 16 + 16)
                nc.scalar.activation(whi[:, slot], wst[:, 0:2 * E], ACT.Copy).then_inc(s["whi"], 1)
                nc.scalar.activation(par[:, slot], wst[:, 2 * E:], ACT.Copy).then_inc(s["par"], 1)

            split_w(0, 0)

            def step(i, k):
                u = k - 2
                if alive(i, u, UNITS):
                    wait(act, s["y"], count(i, u, 2, 2))
                    wait(act, s["po"], y_free(i, u))
                    nc.scalar.activation(y_of(u, 0), y[:, u % 2, :], ACT.Copy).then_inc(s["yhi"], 1)
                    wait(act, s["sqa"], count(i, u))
                    nc.scalar.activation(sq[:], y[:, u % 2, :], ACT.Square).then_inc(s["sq"], 1)
                if not alive(i, k, UNITS):
                    return
                wait(act, s["Ah"], count(i, k, 1, 1))
                wait(act, s["conv"], count(i, k, 3))
                if isinstance(i, int) and i == 0 and k == 0:
                    act.wait_ge(s["init"], 4)
                nc.scalar.activation(raw[:, :, 3:], ph[k % 2][:].rearrange("p (c h) -> p c h", c=2), ACT.Copy).then_inc(s["raw"], 1)
                wait(act, s["hs"], count(i, k))
                wait(act, s["par"], i * 2 + (k // NT + 1))
                nc.scalar.activation(flat(cv[:]), ph[k % 2][:], ACT.Identity, bias=par[:, k // NT, 4:5],
                                     scale=par[:, k // NT, 3:4]).then_inc(s["cv0"], 1)
                if k % NT == 1 and alive(i, k + NT, UNITS):
                    wait(act, s["Ag"], count(i, k - 1))
                    wait(act, s["y"], count(i, k - 1, 2))
                    split_w(i * 2 + (k // NT + 1), (k // NT + 1) % 2)
                if k in (2, 3):
                    act.wait_ge(s["wo"], i * 16 + 16)
                    wait(act, s["po"], count(i, 0, 2))
                    nc.scalar.activation(wohi[:, k - 2], wost[:, k - 2], ACT.Copy, scale=par[:, k - 2, 5:6]).then_inc(s["wohi"], 1)
                wait(act, s["conv"], count(i, k, 3, 3))
                wait(act, s["tr"], count(i, k, 1, -1))
                wait(act, s["y"], count(i, k, 2, -2))
                nc.scalar.activation(hs[:, k % 2, :], flat(cv[:]), ACT.Silu).then_inc(s["hs"], 1)
                wait(act, s["Ag"], count(i, k, 1, 1))
                nc.scalar.activation(sg[:, k % 2, :], pg[k % 2][:], ACT.Silu).then_inc(s["sg"], 1)

            steps(act, step, UNITS, 2)

        @block.vector
        def _(dve):
            tt = nc.vector.tensor_tensor
            stt = nc.vector.scalar_tensor_tensor
            nc.vector.memset(raw[:, :, 0:3], 0.0).then_inc(s["init"], 1)
            nc.vector.memset(g.acc[:], 0.0).then_inc(s["init"], 1)
            nc.vector.memset(g.sqa[:], 0.0).then_inc(s["init"], 1)
            dve.wait_ge(s["pat"], 16)
            nc.vector.tensor_copy(one[:, 1:, :], one[:, 0:1, :].to_broadcast([P, 2 * CP - 1, CHUNK])).then_inc(s["init"], 1)
            dve.wait_ge(s["init"], 4)

            def step(i, k):
                v = k - 1
                if alive(i, v, UNITS):
                    jv = v // NT
                    dve.wait_ge(s["dtz"], (i * 32 + (16 * jv + 16)))
                    wait(dve, s["Z"], count(i, v))
                    nc.vector.tensor_copy(one[:, :, 0], dtz[:, jv % 2, 1, v % NT, :]).then_inc(s["one"], 1)
                    dve.wait_ge(s[f"dec{v % 2}"], count(i, v - v % 2, 16, 32))
                    wait(dve, s["M"], count(i, v, 2))
                    dve.wait_ge(s["one"], count(i, v, 1, 1))
                    nc.vector.tensor_tensor_scan(Z[:].rearrange("p h c l -> p (h c l)"), dec[:, v % 2, :],
                                                 one[:].rearrange("p n l -> p (n l)"), 0.0, ALU.mult, ALU.add).then_inc(s["Z"], 1)
                    dve.wait_ge(s["tr"], count(i, v, 1, 1))
                    wait(dve, s["Y"], count(i, v, 1, -1))
                    tt(Hdt[:, v % 2], tr[:].rearrange("p (c h d) -> p c h d", c=CP, h=2),
                       dtz[:, jv % 2, 0, v % NT, :].rearrange("p (h c) -> p c h", h=2).unsqueeze(3).to_broadcast([P, CP, 2, HD]),
                       ALU.mult).then_inc(s["Hdt"], 1)
                u = k - 2
                if alive(i, u, UNITS):
                    dve.wait_ge(s["yhi"], count(i, u, 1, 1))
                    wait(dve, s["po"], y_free(i, u))
                    tt(y_of(u, 1), y[:, u % 2, :], y_of(u, 0).bitcast(F32), ALU.subtract).then_inc(s["ylo"], 1)
                if alive(i, k, UNITS):
                    dve.wait_ge(s["raw"], count(i, k, 1, 1))
                    dve.wait_ge(s["cv0"], count(i, k, 1, 1))
                    for tap in range(3):
                        if tap:
                            dve.wait_ge(s["conv"], count(i, k, 3, tap))
                        stt(cv[:], raw[:, :, tap:tap + H], par[:, k // NT, tap:tap + 1], cv[:], ALU.mult, ALU.add).then_inc(s["conv"], 1)
                if k in (2, 3) and alive(i, k, UNITS):
                    dve.wait_ge(s["wohi"], i * 2 + (k - 1))
                    wait(dve, s["po"], count(i, 0, 2))
                    stt(wolo[:, k - 2], wost[:, k - 2], par[:, k - 2, 5:6], wohi[:, k - 2].bitcast(F32),
                        ALU.mult, ALU.subtract).then_inc(s["wolo"], 1)
                if alive(i, v, UNITS):
                    dve.wait_ge(s["Y"], count(i, v, 1, 1))
                    wait(dve, s["yhi"], count(i, v, 1, -1))
                    wait(dve, s["sq"], count(i, v, 1, -1))
                    wait(dve, s["ylo"], count(i, v, 1, -1))
                    stt(y[:, v % 2, :], hs[:, v % 2, :], par[:, (v // NT) % 2, 6:7], Yp[:], ALU.mult, ALU.add).then_inc(s["y"], 1)
                    dve.wait_ge(s["sg"], count(i, v, 1, 1))
                    dve.wait_ge(s["y"], count(i, v, 2, 1))
                    tt(y[:, v % 2, :], y[:, v % 2, :], sg[:, v % 2, :], ALU.mult).then_inc(s["y"], 1)
                if alive(i, u, UNITS) and (u // NT) % 2 == 1:
                    pair = i if u >= 0 else i - 1
                    for m in range(CP):
                        n = 4 * (u % NT) + m
                        dve.wait_ge(s["po"], count(pair, 0, 2, n + 1))
                        wait(dve, s["acc"], count(pair, 0, 2, n - 7))
                        tt(g.acc[:, n, :], g.acc[:, n, :], po[n % 2][:], ALU.add).then_inc(s["acc"], 1)

            steps(dve, step, UNITS, 2)

        @block.gpsimd
        def _(pool):
            tt = nc.gpsimd.tensor_tensor

            def split_w(j, slot):
                pool.wait_ge(s["whi"], j + 1)
                tt(wlo[:, slot], wst[:, 0:2 * E], whi[:, slot].bitcast(F32), ALU.subtract).then_inc(s["wlo"], 1)

            split_w(0, 0)
            pool.wait_ge(s["init"], 4)

            def step(i, k):
                v = k - 1
                if alive(i, v, UNITS):
                    pool.wait_ge(s["Z"], count(i, v, 1, 1))
                    wait(pool, s["Y"], count(i, v))
                    for q in range(2):
                        tt(M[:, :, :, q, :], Z[:],
                           g.G[:, CP * (v % NT):CP * (v % NT) + CP, q, :].unsqueeze(1).to_broadcast([P, 2, CP, CHUNK]),
                           ALU.mult).then_inc(s["M"], 1)
                u = k - 2
                if alive(i, u, UNITS):
                    pool.wait_ge(s["sq"], count(i, u, 1, 1))
                    wait(pool, s["sqa"], count(i, u, 1, -3))
                    tt(g.sqa[:, u % NT, :], g.sqa[:, u % NT, :], sq[:], ALU.add).then_inc(s["sqa"], 1)
                if k % NT == 1 and alive(i, k + NT, UNITS) and alive(i, k, UNITS):
                    split_w(i * 2 + (k // NT + 1), (k // NT + 1) % 2)

            steps(pool, step, UNITS, 2)

        @block.tensor
        def _(pe):
            def project(i, k, part, out):
                tb, slot = k % NT, k // NT
                return split_matmuls(nc, out, whi, wlo, g, lambda x, c: x[:, slot, E * part + P * c:E * part + P * (c + 1)],
                                     lambda h, c: h[:, c, TBW * tb:TBW * tb + TBW])

            def step(i, k):
                if alive(i, k, UNITS):
                    if k % NT == 0:
                        pe.wait_ge(s["whi"], i * 2 + (k // NT + 1))
                        pe.wait_ge(s["wlo"], i * 2 + (k // NT + 1))
                    wait(pe, s["raw"], count(i, k, 1, -1))
                    wait(pe, s["cv0"], count(i, k, 1, -1))
                    project(i, k, 0, ph[k % 2][:]).then_inc(s["Ah"], 1)
                v = k - 1
                if alive(i, v, UNITS):
                    pe.wait_ge(s["hs"], count(i, v, 1, 1))
                    wait(pe, s["Hdt"], count(i, v))
                    for c in range(CP):
                        mm = nc.tensor.transpose(tr[:, P * c:P * c + P], hs[:, v % 2, P * c:P * c + P], g.ident[:])
                    mm.then_inc(s["tr"], 1)
                if alive(i, k, UNITS):
                    wait(pe, s["sg"], count(i, k, 1, -1))
                    project(i, k, 1, pg[k % 2][:]).then_inc(s["Ag"], 1)
                if alive(i, v, UNITS):
                    pe.wait_ge(s["Hdt"], count(i, v, 1, 1))
                    pe.wait_ge(s["M"], count(i, v, 2, 2))
                    wait(pe, s["y"], count(i, v, 2, -1))
                    for c in range(CP):
                        for h in range(2):
                            mm = nc.tensor.matmul(Yp[64 * h:64 * h + 64, P * c:P * c + P], Hdt[:, v % 2, c, h, :],
                                                  M[:, h, c].rearrange("p q l -> p (q l)"), start=True, stop=True)
                    mm.then_inc(s["Y"], 1)
                u = k - 2
                if alive(i, u, UNITS) and (u // NT) % 2 == 1:
                    pair = i if u >= 0 else i - 1
                    pe.wait_ge(s["yhi"], count(i, u, 1, 1))
                    pe.wait_ge(s["ylo"], count(i, u, 1, 1))
                    pe.wait_ge(s["wohi"], pair * 2 + 2)
                    pe.wait_ge(s["wolo"], pair * 2 + 2)
                    for m in range(CP):
                        n = 4 * (u % NT) + m
                        wait(pe, s["acc"], count(pair, 0, 2, n - 1))
                        mm = None
                        for tile in range(2):
                            kk = u - NT + NT * tile
                            cols = slice(P * m, P * m + P)
                            for a, b in ((0, wohi), (1, wohi), (0, wolo)):
                                mm = nc.tensor.matmul(po[n % 2][:], y_of(kk, a)[:, cols], b[:, tile, :],
                                                      start=(tile == 0 and a == 0 and b is wohi), stop=(tile == 1 and b is wolo))
                        mm.then_inc(s["po"], 1)

            steps(pe, step, UNITS, 2)


def phase_norm(nc, d, g):
    with ExitStack() as ctx:
        def sb(name, shape, dt=F32):
            return ctx.enter_context(nc.sbuf_tensor(name, shape, dt))

        def sem(name):
            return ctx.enter_context(nc.semaphore(name))

        ones = sb("nm_ones", [P, 2])
        var = sb("nm_var", [P, TT])
        root = sb("nm_root", [P, TT])
        inv = sb("nm_inv", [P, TT])
        st = sb("nm_st", [P, TT, 6])
        mv = sb("nm_mv", [P, TT, 2])
        rs = sb("nm_rs", [P, TT])
        mrs = sb("nm_mrs", [P, TT])
        pv = ctx.enter_context(nc.psum_tensor("nm_pv", [P, TT, 2], F32))
        ph = [ctx.enter_context(nc.psum_tensor(f"nm_h{i}", [P, E], F32)) for i in range(3)]
        pt = [ctx.enter_context(nc.psum_tensor(f"nm_t{i}", [P, KE, P], F32)) for i in range(3)]
        s_one, s_pv, s_rms, s_root, s_h, s_x, s_st, s_mv, s_c, s_n, s_t, s_hi, s_lo = [
            sem("nm_" + n) for n in ("one", "pv_s", "rms", "root_s", "h", "x", "st_s", "mv_s", "c", "n", "t", "hi", "lo")]
        block = ctx.enter_context(nc.Block())

        @block.tensor
        def _(pe):
            pe.wait_ge(s_one, 1)
            for n in range(TT):
                mm = nc.tensor.matmul(pv[:, n, :], g.sqa[:].rearrange("p t n -> p (t n)")[:, P * n:P * n + P], ones[:],
                                      start=True, stop=True)
            mm.then_inc(s_pv, 1)
            for n in range(TT):
                if n >= 3:
                    pe.wait_ge(s_x, n - 2)
                for k in range(KE):
                    for m, h in enumerate((g.hhi, g.hlo)):
                        mm = nc.tensor.matmul(ph[n % 3][:, P * k:P * k + P], h[:, k, P * n:P * n + P], g.identr[:],
                                              start=(m == 0), stop=(m == 1))
                mm.then_inc(s_h, 1)
            for n in range(TT):
                pe.wait_ge(s_n, n + 1)
                if n >= 3:
                    pe.wait_ge(s_hi, n - 2)
                    pe.wait_ge(s_lo, n - 2)
                for k in range(KE):
                    mm = nc.tensor.transpose(pt[n % 3][:, k, :], g.acc[:, n, P * k:P * k + P], g.ident[:])
                mm.then_inc(s_t, 1)

        @block.scalar
        def _(act):
            act.wait_ge(s_rms, 1)
            nc.scalar.activation(root[:], var[:], ACT.Sqrt).then_inc(s_root, 1)
            act.wait_ge(s_mv, TT + 1)
            nc.scalar.activation(root[:], var[:], ACT.Sqrt).then_inc(s_root, 1)
            for n in range(TT):
                act.wait_ge(s_t, n + 1)
                nc.scalar.activation(g.hhi[:, :, P * n:P * n + P], pt[n % 3][:], ACT.Copy).then_inc(s_hi, 1)

        @block.vector
        def _(dve):
            tt = nc.vector.tensor_tensor
            stt = nc.vector.scalar_tensor_tensor
            ts = nc.vector.tensor_scalar
            chain = [0]

            def after(ins):
                chain[0] += 1
                ins.then_inc(s_c, 1)
                dve.wait_ge(s_c, chain[0])

            def rsqrt(out):
                after(nc.vector.reciprocal(inv[:], root[:]))
                after(tt(inv[:], inv[:], var[:], ALU.mult))
                after(tt(inv[:], inv[:], root[:], ALU.add))
                after(ts(inv[:], inv[:], 0.5, None, ALU.mult))
                after(nc.vector.reciprocal(out, inv[:]))

            nc.vector.memset(ones[:], 1.0).then_inc(s_one, 1)
            dve.wait_ge(s_pv, 1)
            ts(var[:], pv[:, :, 0], 1.0 / INTER, EPS, ALU.mult, ALU.add).then_inc(s_rms, 1)
            dve.wait_ge(s_root, 1)
            rsqrt(rs[:])
            for n in range(TT):
                dve.wait_ge(s_h, n + 1)
                stt(g.acc[:, n, :], g.acc[:, n, :], rs[:, n:n + 1], ph[n % 3][:], ALU.mult, ALU.add).then_inc(s_x, 1)
                dve.wait_ge(s_x, n + 1)
                nc.vector.bn_stats(st[:, n, :], g.acc[:, n, :]).then_inc(s_st, 1)
                dve.wait_ge(s_st, n + 1)
                nc.vector.bn_aggr(mv[:, n, :], st[:, n, :]).then_inc(s_mv, 1)
            dve.wait_ge(s_mv, TT)
            ts(var[:], mv[:, :, 1], EPS, None, ALU.add).then_inc(s_mv, 1)
            dve.wait_ge(s_root, 2)
            rsqrt(rs[:])
            after(stt(mrs[:], mv[:, :, 0], -1.0, rs[:], ALU.mult, ALU.mult))
            for n in range(TT):
                ts(g.acc[:, n, :], g.acc[:, n, :], rs[:, n:n + 1], mrs[:, n:n + 1], ALU.mult, ALU.add).then_inc(s_n, 1)
                if n >= 2:
                    dve.wait_ge(s_hi, n - 1)
                    tt(g.hlo[:, :, P * (n - 2):P * (n - 1)], pt[(n - 2) % 3][:], g.hhi[:, :, P * (n - 2):P * (n - 1)].bitcast(F32),
                       ALU.subtract).then_inc(s_lo, 1)
            for n in range(TT - 2, TT):
                dve.wait_ge(s_hi, n + 1)
                tt(g.hlo[:, :, P * n:P * n + P], pt[n % 3][:], g.hhi[:, :, P * n:P * n + P].bitcast(F32),
                   ALU.subtract).then_inc(s_lo, 1)


def phase_ffn(nc, d, g):
    with ExitStack() as ctx:
        def sb(name, shape, dt=F32):
            return ctx.enter_context(nc.sbuf_tensor(name, shape, dt))

        def sem(name):
            return ctx.enter_context(nc.semaphore(name))

        def bank(name):
            return ctx.enter_context(nc.psum_tensor(name, [P, TBW], F32))

        wst = sb("f_wst", [P, 2 * E])
        whi = sb("f_whi", [P, 2, 2 * E], F32R)
        wlo = sb("f_wlo", [P, 2, 2 * E], F32R)
        wost = sb("f_wost", [P, 2, E])
        wohi = sb("f_wohi", [P, 2, E], F32R)
        wolo = sb("f_wolo", [P, 2, E], F32R)
        sg = sb("f_sg", [P, 2, TBW])
        y = sb("f_y", [P, 2, TBW])
        ye = [sb(f"f_ye{i}", [P, NT, TBW], F32R) for i in range(2)]
        yo = [sb(f"f_yo{i}", [P, 2, TBW], F32R) for i in range(2)]
        pg = [bank(f"f_pg{i}") for i in range(2)]
        pu = [bank(f"f_pu{i}") for i in range(2)]
        po = [bank(f"f_po{i}") for i in range(4)]
        s = {n: sem("ff_" + n) for n in ("w", "wo", "whi", "wlo", "wohi", "wolo", "Ag", "Au", "sg", "y", "yhi", "ylo", "po", "acc")}
        block = ctx.enter_context(nc.Block())

        def y_of(k, part):
            return ye[part][:, k % NT, :] if (k // NT) % 2 == 0 else yo[part][:, k % 2, :]

        def y_free(i, k):
            pair = i if k >= 0 else i - 1
            return count(pair, 0, 2, 4 * (k % NT) - (12 if (k // NT) % 2 == 0 else 4))

        @block.sync
        def _(sp):
            def load_w(m):
                sp.dma_start(wst[:], d["w_ffn"][bass.ds(m, 1)].rearrange("a p n -> (a p) n")).then_inc(s["w"], 16)

            def load_wo(pair):
                sp.dma_start(wost[:], d["w_down"][bass.ds(pair, 1)].rearrange("a m p n -> p (a m) n")).then_inc(s["wo"], 16)

            load_w(0)
            load_wo(0)

            def step(i, k):
                next_m, both, pair = values(sp, i * 2 + (k // NT + 1), i * 2 + 2, i + 1)
                if k % NT == 0 and alive(i, k + NT, FUNITS):
                    sp.wait_ge(s["whi"], next_m)
                    sp.wait_ge(s["wlo"], next_m)
                    load_w(next_m)
                if k == 4 and alive(i, BODY, FUNITS):
                    sp.wait_ge(s["wohi"], both)
                    sp.wait_ge(s["wolo"], both)
                    load_wo(pair)

            steps(sp, step, FUNITS, 0)

        @block.scalar
        def _(act):
            def split_w(m, slot):
                act.wait_ge(s["w"], m * 16 + 16)
                nc.scalar.activation(whi[:, slot], wst[:], ACT.Copy).then_inc(s["whi"], 1)

            split_w(0, 0)

            def step(i, k):
                u = k - 1
                if alive(i, u, FUNITS):
                    act.wait_ge(s["y"], count(i, u, 1, 1))
                    wait(act, s["po"], y_free(i, u))
                    nc.scalar.activation(y_of(u, 0), y[:, u % 2, :], ACT.Copy).then_inc(s["yhi"], 1)
                if not alive(i, k, FUNITS):
                    return
                if k % NT == 1 and alive(i, k + NT, FUNITS):
                    wait(act, s["Au"], count(i, k - 1))
                    split_w(i * 2 + (k // NT + 1), (k // NT + 1) % 2)
                if k in (2, 3):
                    act.wait_ge(s["wo"], i * 16 + 16)
                    wait(act, s["po"], count(i, 0, 2))
                    nc.scalar.activation(wohi[:, k - 2], wost[:, k - 2], ACT.Copy).then_inc(s["wohi"], 1)
                act.wait_ge(s["Ag"], count(i, k, 1, 1))
                wait(act, s["y"], count(i, k, 1, -1))
                nc.scalar.activation(sg[:, k % 2, :], pg[k % 2][:], ACT.Silu).then_inc(s["sg"], 1)

            steps(act, step, FUNITS, 2)

        @block.vector
        def _(dve):
            tt = nc.vector.tensor_tensor

            def step(i, k):
                v = k - 1
                if alive(i, v, FUNITS):
                    dve.wait_ge(s["yhi"], count(i, v, 1, 1))
                    wait(dve, s["po"], y_free(i, v))
                    tt(y_of(v, 1), y[:, v % 2, :], y_of(v, 0).bitcast(F32), ALU.subtract).then_inc(s["ylo"], 1)
                if k in (2, 3) and alive(i, k, FUNITS):
                    dve.wait_ge(s["wohi"], i * 2 + (k - 1))
                    wait(dve, s["po"], count(i, 0, 2))
                    tt(wolo[:, k - 2], wost[:, k - 2], wohi[:, k - 2].bitcast(F32), ALU.subtract).then_inc(s["wolo"], 1)
                if alive(i, k, FUNITS):
                    dve.wait_ge(s["Au"], count(i, k, 1, 1))
                    dve.wait_ge(s["sg"], count(i, k, 1, 1))
                    wait(dve, s["yhi"], count(i, k, 1, -1))
                    wait(dve, s["ylo"], count(i, k, 1, -1))
                    tt(y[:, k % 2, :], sg[:, k % 2, :], pu[k % 2][:], ALU.mult).then_inc(s["y"], 1)
                if alive(i, v, FUNITS) and (v // NT) % 2 == 1:
                    pair = i if v >= 0 else i - 1
                    for m in range(CP):
                        n = 4 * (v % NT) + m
                        dve.wait_ge(s["po"], count(pair, 0, 2, n + 1))
                        wait(dve, s["acc"], count(pair, 0, 2, n - 7))
                        tt(g.acc[:, n, :], g.acc[:, n, :], po[n % 4][:], ALU.add).then_inc(s["acc"], 1)

            steps(dve, step, FUNITS, 1)

        @block.gpsimd
        def _(pool):
            def split_w(m, slot):
                pool.wait_ge(s["whi"], m + 1)
                nc.gpsimd.tensor_tensor(wlo[:, slot], wst[:], whi[:, slot].bitcast(F32), ALU.subtract).then_inc(s["wlo"], 1)

            split_w(0, 0)

            def step(i, k):
                if k % NT == 1 and alive(i, k + NT, FUNITS) and alive(i, k, FUNITS):
                    split_w(i * 2 + (k // NT + 1), (k // NT + 1) % 2)

            steps(pool, step, FUNITS, 0)

        @block.tensor
        def _(pe):
            def project(i, k, part, out):
                tb, slot = k % NT, k // NT
                return split_matmuls(nc, out, whi, wlo, g, lambda x, c: x[:, slot, E * part + P * c:E * part + P * (c + 1)],
                                     lambda h, c: h[:, c, TBW * tb:TBW * tb + TBW])

            def step(i, k):
                if alive(i, k, FUNITS):
                    if k % NT == 0:
                        pe.wait_ge(s["whi"], i * 2 + (k // NT + 1))
                        pe.wait_ge(s["wlo"], i * 2 + (k // NT + 1))
                    wait(pe, s["sg"], count(i, k, 1, -1))
                    project(i, k, 0, pg[k % 2][:]).then_inc(s["Ag"], 1)
                    wait(pe, s["y"], count(i, k, 1, -1))
                    project(i, k, 1, pu[k % 2][:]).then_inc(s["Au"], 1)
                u = k - 1
                if alive(i, u, FUNITS) and (u // NT) % 2 == 1:
                    pair = i if u >= 0 else i - 1
                    pe.wait_ge(s["yhi"], count(i, u, 1, 1))
                    pe.wait_ge(s["ylo"], count(i, u, 1, 1))
                    pe.wait_ge(s["wohi"], pair * 2 + 2)
                    pe.wait_ge(s["wolo"], pair * 2 + 2)
                    for m in range(CP):
                        n = 4 * (u % NT) + m
                        wait(pe, s["acc"], count(pair, 0, 2, n - 3))
                        mm = None
                        for tile in range(2):
                            kk = u - NT + NT * tile
                            cols = slice(P * m, P * m + P)
                            for a, b in ((0, wohi), (1, wohi), (0, wolo)):
                                mm = nc.tensor.matmul(po[n % 4][:], y_of(kk, a)[:, cols], b[:, tile, :],
                                                      start=(tile == 0 and a == 0 and b is wohi), stop=(tile == 1 and b is wolo))
                        mm.then_inc(s["po"], 1)

            steps(pe, step, FUNITS, 1)


def phase_out(nc, d, g, out):
    with ExitStack() as ctx:
        def sb(name, shape, dt=F32):
            return ctx.enter_context(nc.sbuf_tensor(name, shape, dt))

        def sem(name):
            return ctx.enter_context(nc.semaphore(name))

        var = sb("o_var", [P, TT])
        root = sb("o_root", [P, TT])
        inv = sb("o_inv", [P, TT])
        st = sb("o_st", [P, TT, 6])
        mv = sb("o_mv", [P, TT, 2])
        rs = sb("o_rs", [P, TT])
        mrs = sb("o_mrs", [P, TT])
        s_st, s_mv, s_root, s_c, s_n, s_out = [sem("o_" + n) for n in ("st_s", "mv_s", "root_s", "c", "n", "out")]
        block = ctx.enter_context(nc.Block())

        @block.vector
        def _(dve):
            tt = nc.vector.tensor_tensor
            ts = nc.vector.tensor_scalar
            chain = [0]

            def after(ins):
                chain[0] += 1
                ins.then_inc(s_c, 1)
                dve.wait_ge(s_c, chain[0])

            for n in range(TT):
                nc.vector.bn_stats(st[:, n, :], g.acc[:, n, :]).then_inc(s_st, 1)
            for n in range(TT):
                dve.wait_ge(s_st, n + 1)
                nc.vector.bn_aggr(mv[:, n, :], st[:, n, :]).then_inc(s_mv, 1)
            dve.wait_ge(s_mv, TT)
            ts(var[:], mv[:, :, 1], EPS, None, ALU.add).then_inc(s_mv, 1)
            dve.wait_ge(s_root, 1)
            after(nc.vector.reciprocal(inv[:], root[:]))
            after(tt(inv[:], inv[:], var[:], ALU.mult))
            after(tt(inv[:], inv[:], root[:], ALU.add))
            after(ts(inv[:], inv[:], 0.5, None, ALU.mult))
            after(nc.vector.reciprocal(rs[:], inv[:]))
            after(nc.vector.scalar_tensor_tensor(mrs[:], mv[:, :, 0], -1.0, rs[:], ALU.mult, ALU.mult))
            for n in range(TT):
                ts(g.acc[:, n, :], g.acc[:, n, :], rs[:, n:n + 1], mrs[:, n:n + 1], ALU.mult, ALU.add).then_inc(s_n, 1)

        @block.scalar
        def _(act):
            act.wait_ge(s_mv, TT + 1)
            nc.scalar.activation(root[:], var[:], ACT.Sqrt).then_inc(s_root, 1)

        @block.sync
        def _(sp):
            o = out.rearrange("b (t p) e -> p (b t) e", p=P)
            for n in range(0, TT, 4):
                sp.wait_ge(s_n, n + 4)
                sp.dma_start(o[:, n:n + 4, :], g.acc[:, n:n + 4, :]).then_inc(s_out, 16)
            sp.wait_ge(s_out, 16 * (TT // 4))


def build(nc, d, out, stop=None):
    with ExitStack() as ctx:
        g = Shared()
        g.hhi = ctx.enter_context(nc.sbuf_tensor("hhi", [P, KE, TOK], F32R))
        g.hlo = ctx.enter_context(nc.sbuf_tensor("hlo", [P, KE, TOK], F32R))
        g.ident = ctx.enter_context(nc.sbuf_tensor("ident", [P, P], F32))
        g.identr = ctx.enter_context(nc.sbuf_tensor("identr", [P, P], F32R))
        phase_constants(nc, d, g)
        phase_token(nc, d, g)
        g.acc = ctx.enter_context(nc.sbuf_tensor("acc", [P, TT, E], F32))
        with ExitStack() as mixer:
            g.G = mixer.enter_context(nc.sbuf_tensor("G", [P, TT, 2, CHUNK], F32))
            phase_decays(nc, d, g)
            g.sqa = mixer.enter_context(nc.sbuf_tensor("sqa", [P, NT, TBW], F32))
            phase_mixer(nc, d, g)
            phase_norm(nc, d, g)
        phase_ffn(nc, d, g)
        phase_out(nc, d, g, out)


def kernel(**inputs):
    import numpy as np
    import concourse.bacc as bacc
    from concourse.bass_utils import run_bass_kernel_spmd

    a = {k: np.asarray(v) for k, v in inputs.items()}
    lay = np.ascontiguousarray

    def tiles(w):
        r = w.shape[0] // P
        return w.reshape(r, P, KE, P).transpose(0, 3, 2, 1).reshape(r, P, E)

    W_in = a["L0_attn_W_in"]
    gate, hidden, bc, dtw = W_in[:INTER], W_in[INTER:2 * INTER], W_in[2 * INTER:2 * INTER + 2 * P], W_in[2 * INTER + 2 * P:]
    cw, cb = a["L0_attn_conv_w"], a["L0_attn_conv_b"]
    par = np.zeros((NJ, P, NPAR), np.float32)
    par[:, :, 0:4] = cw[:INTER].reshape(NJ, P, TAPS)
    par[:, :, 4] = cb[:INTER].reshape(NJ, P)
    par[:, :, 5] = a["L0_attn_norm_w"].reshape(NJ, P)
    par[:, :, 6] = np.repeat(a["L0_attn_D"], HD).reshape(NJ, P)
    par_bc = np.zeros((P, 2, NPAR), np.float32)
    par_bc[:, :, 0:4] = cw[INTER:].reshape(2, P, TAPS).transpose(1, 0, 2)
    par_bc[:, :, 4] = cb[INTER:].reshape(2, P).T
    k, s_ = np.arange(P)[:, None], np.arange(P)[None, :]
    mask = np.zeros((P, P + 1), np.float32)
    mask[:, :P] = (k // CHUNK == s_ // CHUNK) & ((k > s_) | (k % CHUNK == 0))
    mask[:, P] = np.arange(P) % CHUNK == 0
    arrays = {
        "x": lay(a["x"].transpose(3, 2, 1, 0).reshape(P, H, NB)),
        "log_dt": a["L0_tok_log_dt"],
        "tokpar": lay(np.stack([a["L0_tok_inv_A_real"].T, a["L0_tok_A_imag"].T, a["L0_tok_B_ri"][..., 0].T,
                                a["L0_tok_B_ri"][..., 1].T], 1)),
        "ident": np.eye(P, dtype=np.float32),
        "eye64": np.tile(np.eye(CHUNK, dtype=np.float32), (2, 1)),
        "mask": mask,
        "A_log": a["L0_attn_A_log"],
        "dt_bias": a["L0_attn_dt_bias"],
        "w_bc": lay(np.concatenate([tiles(bc)[0], tiles(bc)[1],
                                    dtw.reshape(HEADS, KE, P).transpose(2, 1, 0).reshape(P, KE * HEADS)], 1)),
        "par_bc": par_bc,
        "w_mix": lay(np.concatenate([tiles(hidden), tiles(gate), par], 2)),
        "w_out": lay(a["L0_attn_W_out"].T.reshape(NJ // 2, 2, P, E)),
        "w_ffn": lay(np.concatenate([tiles(a["L0_ffn_w_gate"]), tiles(a["L0_ffn_w_up"])], 2)),
        "w_down": lay(a["L0_ffn_w_down"].T.reshape(NM // 2, 2, P, E)),
    }
    nc = bacc.Bacc("TRN2", target_bir_lowering=False, num_devices=1)
    d = {n: nc.dram_tensor("in_" + n, v.shape, F32, kind="ExternalInput").ap() for n, v in arrays.items()}
    d["decay"] = nc.dram_tensor("decay", (NJ, 2, NT, 2, CP * CHUNK), F32, kind="Internal").ap()
    d["dtz"] = nc.dram_tensor("dtz", (NJ, P, 2 * NT * 2 * CP), F32, kind="Internal").ap()
    out = nc.dram_tensor("out0", (NB, H, E), F32, kind="ExternalOutput").ap()
    build(nc, d, out)
    r = run_bass_kernel_spmd(nc, [{"in_" + n: v for n, v in arrays.items()}], core_ids=[0])
    return r.results[0]["out0"]
```

```python
from contextlib import ExitStack

import concourse.bass as bass
from concourse import mybir

F32 = mybir.dt.float32
F32R = mybir.dt.float32r
ALU = mybir.AluOpType
ACT = mybir.ActivationFunctionType

P = 128
NB, H, NS = 8, 256, 64
E = 512
TOK = NB * H
KE = E // P
INTER, HEADS, HD = 4096, 64, 64
NJ = INTER // P
TAPS = 4
CHUNK = 64
TBW = 512
NT = TOK // TBW
CP = TBW // P
TT = TOK // P
NM = 2048 // P
NPAR = 8
EPS = 1e-5
A_LO, A_HI, LB = 4, 4, 32


UNITS = NJ * NT
FUNITS = NM * NT
BODY = 8


class Shared:
    pass


def count(i, k, per=1, more=0):
    if isinstance(i, int):
        return per * (BODY * i + k) + more
    return i * (per * BODY) + (per * k + more)


def wait(eng, sem, value):
    if isinstance(value, int) and value <= 0:
        return
    eng.wait_ge(sem, value)


def values(eng, *v):
    return [x if isinstance(x, int) else eng.snap(x) for x in v]


def alive(i, k, units):
    return not isinstance(i, int) or 0 <= BODY * i + k < units


def steps(eng, step, units, tail):
    bodies = units // BODY
    for k in range(BODY):
        step(0, k)
    with eng.Fori(1, bodies - 1) as i:
        for k in range(BODY):
            step(i, k)
    for k in range(BODY):
        step(bodies - 1, k)
    for k in range(tail):
        step(bodies, k)


def phase_token(nc, d, g):
    with ExitStack() as ctx:
        def sb(name, shape, dt=F32):
            return ctx.enter_context(nc.sbuf_tensor(name, shape, dt))

        def sem(name):
            return ctx.enter_context(nc.semaphore(name))

        HH = H // 2
        GR = 16
        HG = GR // 2
        PAIRS = HH // GR
        QSTEPS = 6 * 5
        POW = 9
        x = sb("x", [P, H, NB])
        par = sb("tok_par", [P, 5, HH])
        w = sb("tok_w", [P, 8, HH])
        pw = sb("tok_pow", [P, POW, 2, HH])
        V = sb("V", [P, 2, HH, LB])
        Q = sb("Q", [P, 2, HH, A_LO, A_HI])
        tq = sb("tok_tq", [P, 2, HH * A_LO])
        Vs = sb("Vs", [P, 2, 2, GR, LB])
        Qs = sb("Qs", [P, 2, 2, GR, A_LO * A_HI])
        T = sb("T", [P, 4, 2, HG, A_LO * A_HI, NB])
        X2 = sb("X2", [P, 2, GR, A_HI, NB])
        Y = sb("Y", [P, 2, 4, P])
        W = lambda i: w[:, i, :]
        tv = T[:].rearrange("p s r h a c -> p (s r h a c)")[:, 0:HH * LB].rearrange("p (i n) -> p i n", i=2)
        ps = [ctx.enter_context(nc.psum_tensor(f"tok_ps{i}", [P, 4, P], F32)) for i in range(2)]
        pt = [ctx.enter_context(nc.psum_tensor(f"tok_pt{i}", [P, GR, LB], F32)) for i in range(2)]
        s_in = sem("tok_in")
        s_exp = sem("tok_exp")
        s_dv = sem("tok_dv")
        s_pow = sem("tok_pow_s")
        s_q = sem("tok_q")
        s_v = sem("tok_v")
        s_vs = sem("tok_vs")
        s_qs = sem("tok_qs")
        s_T = sem("tok_T")
        s_mm = sem("tok_mm")
        s_y = sem("tok_y")
        s_tr = sem("tok_tr")
        s_x2 = sem("tok_x2")
        s_hi = sem("tok_hi")
        s_lo = sem("tok_lo")
        block = ctx.enter_context(nc.Block())

        def group(i, k):
            return i * 2 + k

        def tokens(i, k):
            return i * GR + (GR * (k // 2) + HH * (k % 2))

        def there(i, k):
            return not isinstance(i, int) or 0 <= group(i, k) < 2 * PAIRS

        def pairs(eng, step):
            step(0, 0)
            step(0, 1)
            with eng.Fori(1, PAIRS - 1) as i:
                step(i, 0)
                step(i, 1)
            step(PAIRS - 1, 0)
            step(PAIRS - 1, 1)
            step(PAIRS, 0)
            step(PAIRS, 1)

        def of_group(t, i, k):
            return t.rearrange("p k (c h) -> p k c h", c=NB)[:, :, :, bass.ds(tokens(i, k), GR)]

        @block.sync
        def _(sp):
            for half in range(2):
                rows = slice(64 * half, 64 * half + 64)
                sp.dma_start(par[rows, 0, :], d["log_dt"][HH * half:HH * half + HH].partition_broadcast(64)).then_inc(s_in, 16)
            sp.dma_start(par[:, 1:5, :], d["tokpar"]).then_inc(s_in, 16)
            sp.dma_start(x[:], d["x"]).then_inc(s_in, 16)

        @block.scalar
        def _(act):
            act.wait_ge(s_in, 64)
            nc.scalar.activation(W(0), par[:, 0, :], ACT.Exp).then_inc(s_exp, 1)
            nc.scalar.activation(W(1), par[:, 1, :], ACT.Exp).then_inc(s_exp, 1)

            def spread(i, k):
                n, slot = group(i, k), k % 2
                half = slice(64 * slot, 64 * slot + 64)
                h = bass.ds(i * GR + GR * (k // 2), GR)
                wait(act, s_T, n * 4 - 4)
                for rows in (slice(0, 64), slice(64, 128)):
                    nc.scalar.activation(Qs[rows, slot], Q[half, :, h].rearrange("p r h a b -> p r h (a b)"),
                                         ACT.Copy).then_inc(s_qs, 1)
                wait(act, s_mm, n * 2 - 2)
                for rows, part, src, sign in ((slice(0, 64), 0, 0, 1.0), (slice(64, 128), 0, 1, -1.0),
                                              (slice(0, 64), 1, 1, -1.0), (slice(64, 128), 1, 0, -1.0)):
                    nc.scalar.activation(Vs[rows, slot, part], V[half, src, h, :], ACT.Copy, scale=sign).then_inc(s_vs, 1)

            act.wait_ge(s_v, 1)
            act.wait_ge(s_q, QSTEPS)
            spread(0, 0)
            spread(0, 1)

            def step(i, k):
                n = group(i, k)
                if there(i, k - 2):
                    act.wait_ge(s_x2, n - 1)
                    nc.scalar.activation(of_group(g.hhi[:], i, k - 2), X2[:, k % 2].rearrange("p h k c -> p k c h"),
                                         ACT.Copy).then_inc(s_hi, 1)
                if there(i, k):
                    act.wait_ge(s_mm, n * 2 + 2)
                    wait(act, s_tr, n - 1)
                    nc.scalar.activation(Y[:, k % 2], ps[k % 2][:], ACT.Copy).then_inc(s_y, 1)
                if there(i, k + 2):
                    spread(i, k + 2)

            pairs(act, step)

        def grow(tt, s, start, t, re, im, out_re, out_im, m, wait_for):
            dims = [int(v) for v in re.shape[1:]]
            size = dims[0] * (dims[1] if len(dims) > 1 else 1)
            t0, t1 = [t[:, i, 0:size].rearrange("p (h b) -> p h b", h=dims[0]) for i in range(2)]
            r, i = [pw[:, m, q, :].unsqueeze(2).to_broadcast([P] + dims) for q in range(2)]
            tt(out_re, re, r, ALU.mult).then_inc(s, 1)
            tt(t0, im, i, ALU.mult).then_inc(s, 1)
            tt(out_im, im, r, ALU.mult).then_inc(s, 1)
            tt(t1, re, i, ALU.mult).then_inc(s, 1)
            wait_for(start + 4)
            tt(out_re, out_re, t0, ALU.subtract).then_inc(s, 1)
            tt(out_im, out_im, t1, ALU.add).then_inc(s, 1)
            wait_for(start + 6)
            return start + 6

        @block.gpsimd
        def _(pool):
            tt = nc.gpsimd.tensor_tensor
            pool.wait_ge(s_pow, 1)
            q = lambda lo, hi: (Q[:, 0, :, lo, hi], Q[:, 1, :, lo, hi])
            at = 0

            def more(src, dst, m):
                return grow(tt, s_q, at, tq, *src, *dst, m, lambda v: pool.wait_ge(s_q, v))

            at = more(q(slice(0, 1), 0), q(slice(1, 2), 0), 5)
            at = more(q(slice(0, 2), 0), q(slice(2, 4), 0), 6)
            at = more(q(slice(0, 4), 0), q(slice(0, 4), 1), 7)
            for hi in range(2):
                at = more(q(slice(0, 4), hi), q(slice(0, 4), 2 + hi), 8)
            assert at == QSTEPS

            def step(i, k):
                if there(i, k - 1):
                    n = group(i, k)
                    pool.wait_ge(s_hi, n)
                    tt(of_group(g.hlo[:], i, k - 1), X2[:, (k - 1) % 2].rearrange("p h k c -> p k c h"),
                       of_group(g.hhi[:].bitcast(F32), i, k - 1), ALU.subtract).then_inc(s_lo, 1)

            pairs(pool, step)

        @block.vector
        def _(dve):
            chain = [0]

            def after(ins):
                chain[0] += 1
                ins.then_inc(s_dv, 1)
                dve.wait_ge(s_dv, chain[0])

            tt = nc.vector.tensor_tensor
            ts = nc.vector.tensor_scalar
            stt = nc.vector.scalar_tensor_tensor
            dve.wait_ge(s_exp, 2)
            after(stt(W(2), W(1), -0.5, W(0), ALU.mult, ALU.mult))
            after(stt(W(3), par[:, 2, :], 0.5, W(0), ALU.mult, ALU.mult))
            after(ts(W(4), W(2), -1.0, 1.0, ALU.mult, ALU.add))
            after(tt(W(5), W(3), W(3), ALU.mult))
            after(tt(W(6), W(4), W(4), ALU.mult))
            after(tt(W(6), W(6), W(5), ALU.add))
            after(nc.vector.reciprocal(W(6), W(6)))
            after(stt(W(0), W(0), 2.0, W(6), ALU.mult, ALU.mult))
            after(tt(W(1), par[:, 3, :], W(4), ALU.mult))
            after(tt(W(7), par[:, 4, :], W(3), ALU.mult))
            after(tt(W(1), W(1), W(7), ALU.subtract))
            after(tt(Q[:, 0, :, 0, 0], W(1), W(0), ALU.mult))
            after(tt(W(1), par[:, 3, :], W(3), ALU.mult))
            after(tt(W(7), par[:, 4, :], W(4), ALU.mult))
            after(tt(W(1), W(1), W(7), ALU.add))
            after(tt(Q[:, 1, :, 0, 0], W(1), W(0), ALU.mult))
            after(stt(W(1), W(2), 1.0, W(4), ALU.add, ALU.mult))
            after(tt(W(1), W(1), W(5), ALU.subtract))
            after(tt(pw[:, 0, 0, :], W(1), W(6), ALU.mult))
            after(stt(pw[:, 0, 1, :], W(3), 2.0, W(6), ALU.mult, ALU.mult))
            for m in range(1, POW):
                re, im = pw[:, m - 1, 0, :], pw[:, m - 1, 1, :]
                tt(W(4), re, re, ALU.mult).then_inc(s_dv, 1)
                tt(W(5), im, im, ALU.mult).then_inc(s_dv, 1)
                chain[0] += 2
                after(stt(pw[:, m, 1, :], re, 2.0, im, ALU.mult, ALU.mult))
                after(tt(pw[:, m, 0, :], W(4), W(5), ALU.subtract))
            nc.vector.memset(V[:, 0, :, 0], 1.0).then_inc(s_pow, 1)
            after(nc.vector.memset(V[:, 1, :, 0], 0.0))
            dve.wait_ge(s_pow, 1)
            for m in range(5):
                b = 2 ** m
                chain[0] = grow(tt, s_dv, chain[0], tv, V[:, 0, :, 0:b], V[:, 1, :, 0:b], V[:, 0, :, b:2 * b],
                                V[:, 1, :, b:2 * b], m, lambda v: dve.wait_ge(s_dv, v))
            nc.vector.memset(W(7)[:, 0:1], 0.0).then_inc(s_v, 1)

            def products(i, k, half):
                n, slot = group(i, k), 2 * (k % 2) + half
                dve.wait_ge(s_qs, n * 2 + 2)
                wait(dve, s_mm, n * 2 - 3 + half)
                h = bass.ds(tokens(i, k) + HG * half, HG)
                for r in range(2):
                    tt(T[:, slot, r], x[:, h, :].unsqueeze(2).to_broadcast([P, HG, A_LO * A_HI, NB]),
                       Qs[:, k % 2, r, HG * half:HG * half + HG, :].unsqueeze(3).to_broadcast([P, HG, A_LO * A_HI, NB]),
                       ALU.mult).then_inc(s_T, 1)

            for k in range(2):
                for half in range(2):
                    products(0, k, half)

            def step(i, k):
                if there(i, k + 2):
                    products(i, k + 2, 0)
                if there(i, k - 1):
                    n = group(i, k)
                    dve.wait_ge(s_tr, n)
                    wait(dve, s_hi, n - 2)
                    wait(dve, s_lo, n - 2)
                    nc.vector.transpose(X2[:, (k - 1) % 2].rearrange("p h k c -> p h (k c)"), pt[(k - 1) % 2][:]).then_inc(s_x2, 1)
                if there(i, k + 2):
                    products(i, k + 2, 1)

            pairs(dve, step)

        @block.tensor
        def _(pe):
            def sums(i, k):
                n, slot = group(i, k), k % 2
                pe.wait_ge(s_vs, n * 4 + 4)
                wait(pe, s_y, n - 1)
                for half in range(2):
                    pe.wait_ge(s_T, n * 4 + (2 * half + 2))
                    for m in range(HG):
                        at = half * HG + m
                        q = at % 4
                        for r in range(2):
                            mm = nc.tensor.matmul(ps[slot][32 * q:32 * q + 32, at // 4, :], Vs[:, slot, r, at, :],
                                                  T[:, 2 * slot + half, r, m].rearrange("p a c -> p (a c)"),
                                                  start=(r == 0), stop=(r == 1), skip_group_check=True)
                    mm.then_inc(s_mm, 1)

            sums(0, 0)

            def step(i, k):
                if there(i, k + 1):
                    sums(i, k + 1)
                if there(i, k):
                    n = group(i, k)
                    pe.wait_ge(s_y, n + 1)
                    wait(pe, s_x2, n - 1)
                    for m in range(4):
                        mm = nc.tensor.transpose(pt[k % 2][:, 4 * m:4 * m + 4, :].rearrange("p h b -> p (h b)"),
                                                 Y[:, k % 2, m, :], g.ident[:])
                    mm.then_inc(s_tr, 1)

            pairs(pe, step)


def phase_constants(nc, d, g):
    with ExitStack() as ctx:
        s_in = ctx.enter_context(nc.semaphore("const_in"))
        s_r = ctx.enter_context(nc.semaphore("const_r"))
        block = ctx.enter_context(nc.Block())

        @block.sync
        def _(sp):
            sp.dma_start(g.ident[:], d["ident"]).then_inc(s_in, 16)
            sp.wait_ge(s_in, 16)

        @block.scalar
        def _(act):
            act.wait_ge(s_in, 16)
            nc.scalar.activation(g.identr[:], g.ident[:], ACT.Copy).then_inc(s_r, 1)


def split_matmuls(nc, out, whi, wlo, g, w_of, h_of):
    for k in range(KE):
        mm = None
        for n, (w, h) in enumerate(((whi, g.hhi), (whi, g.hlo), (wlo, g.hhi))):
            mm = nc.tensor.matmul(out, w_of(w, k), h_of(h, k), start=(k == 0 and n == 0),
                                  stop=(k == KE - 1 and n == 2))
    return mm


def phase_decays(nc, d, g):
    with ExitStack() as ctx:
        def sb(name, shape, dt=F32):
            return ctx.enter_context(nc.sbuf_tensor(name, shape, dt))

        def sem(name):
            return ctx.enter_context(nc.semaphore(name))

        w = sb("bc_w", [P, 2 * E + HEADS * KE])
        whi = sb("bc_whi", [P, 2 * E + HEADS * KE], F32R)
        wlo = sb("bc_wlo", [P, 2 * E + HEADS * KE], F32R)
        par = sb("bc_par", [P, 2, NPAR])
        hd = sb("hd_par", [P, 2, HEADS])
        msk = sb("msk", [P, P + 1])
        names = ["xb", "ex", "un", "ln", "dt", "a", "z0"]
        t = {n: sb("dc_" + n, [P, TT, HEADS]) for n in names}
        packed = sb("packed", [P, NJ, 2, NT, 2, CP])
        eT = sb("eT", [HEADS, 2, NT, CP, CHUNK])
        raw = sb("bc_raw", [P, 2, 3 + H])
        cv = sb("bc_cv", [P, 2, H])
        BC = sb("BC", [P, 2, TOK])
        pd = [ctx.enter_context(nc.psum_tensor(f"pd{i}", [P, 8, HEADS], F32)) for i in range(2)]
        ph = [ctx.enter_context(nc.psum_tensor(f"pb{i}", [P, TBW], F32)) for i in range(2)]
        pm = [ctx.enter_context(nc.psum_tensor(f"pm{i}", [P, 8, HEADS], F32)) for i in range(2)]
        pe_t = [ctx.enter_context(nc.psum_tensor(f"pet{i}", [P, TBW], F32)) for i in range(2)]
        s_w = sem("bc_in_w")
        s_in = sem("bc_in")
        s_hi = sem("bc_hi")
        s_lo = sem("bc_lo")
        s_pd = sem("bc_pd")
        s_ph = sem("bc_ph")
        s_raw = sem("bc_raw_s")
        s_pad = sem("bc_pad")
        s_cv0 = sem("bc_cv0")
        s_conv = sem("bc_conv")
        s_bc = sem("bc_bc")
        s_d = sem("bc_d")
        s_x = sem("bc_x")
        s_pm = sem("bc_pm")
        s_pt = sem("bc_pt")
        s_eT = sem("bc_eT")
        s_neg = sem("bc_neg")
        s_zero = sem("bc_zero")
        s_G = sem("bc_G")
        s_Gc = sem("bc_Gc")
        s_out = sem("bc_out")
        block = ctx.enter_context(nc.Block())
        wk = lambda x, i, k: x[:, E * i + P * k:E * i + P * (k + 1)]
        wd = lambda x, k: x[:, 2 * E + HEADS * k:2 * E + HEADS * (k + 1)]

        @block.sync
        def _(sp):
            sp.dma_start(w[:], d["w_bc"]).then_inc(s_w, 16)
            sp.dma_start(par[:], d["par_bc"]).then_inc(s_in, 16)
            sp.dma_start(hd[:, 0, :], d["A_log"].partition_broadcast(P)).then_inc(s_in, 16)
            sp.dma_start(hd[:, 1, :], d["dt_bias"].partition_broadcast(P)).then_inc(s_in, 16)
            sp.dma_start(msk[:], d["mask"]).then_inc(s_in, 16)
            sp.wait_ge(s_zero, 1)
            for h2 in range(2):
                for q in range(2):
                    sp.dma_start(d["decay"][:, q, :, h2, :], eT[h2:HEADS:2, q].rearrange("j t c l -> j t (c l)")).then_inc(s_out, 16)
            sp.wait_ge(s_d, 14)
            sp.dma_start(d["dtz"].rearrange("j p n -> p j n"), packed[:].rearrange("p j a t h c -> p j (a t h c)")).then_inc(s_out, 16)
            sp.wait_ge(s_out, 80)

        @block.scalar
        def _(act):
            act.wait_ge(s_w, 16)
            nc.scalar.activation(whi[:], w[:], ACT.Copy).then_inc(s_hi, 1)
            act.wait_ge(s_in, 64)
            nc.scalar.activation(hd[:, 0, :], hd[:, 0, :], ACT.Exp).then_inc(s_x, 1)
            act.wait_ge(s_d, 3)
            nc.scalar.activation(t["ex"][:], t["un"][:], ACT.Exp).then_inc(s_x, 1)
            act.wait_ge(s_d, 4)
            nc.scalar.activation(t["ln"][:], t["un"][:], ACT.Ln).then_inc(s_x, 1)
            act.wait_ge(s_d, 10)
            nc.scalar.activation(t["ex"][:], t["a"][:], ACT.Exp).then_inc(s_x, 1)
            for n in range(2):
                act.wait_ge(s_pm, n + 1)
                nc.scalar.activation(t["z0"][:, 8 * n:8 * n + 8, :], pm[n][:], ACT.Exp).then_inc(s_x, 1)
            for tb in range(NT):
                act.wait_ge(s_pt, tb + 1)
                nc.scalar.activation(eT[:, :, tb], pe_t[tb % 2][0:HEADS, :].rearrange("p (c q l) -> p q c l", c=CP, q=2),
                                     ACT.Copy).then_inc(s_eT, 1)
            act.wait_ge(s_pad, 1)
            for n in range(2 * NT):
                i, tb = n // NT, n % NT
                act.wait_ge(s_ph, n + 1)
                if n:
                    act.wait_ge(s_conv, 3 * n)
                nc.scalar.activation(raw[:, :, 3:], ph[n % 2][:].rearrange("p (c h) -> p c h", c=2), ACT.Copy).then_inc(s_raw, 1)
                if n:
                    act.wait_ge(s_bc, n)
                nc.scalar.activation(cv[:].rearrange("p c h -> p (c h)"), ph[n % 2][:], ACT.Identity,
                                     bias=par[:, i, 4:5], scale=par[:, i, 3:4]).then_inc(s_cv0, 1)
                act.wait_ge(s_conv, 3 * n + 3)
                nc.scalar.activation(BC[:, i, TBW * tb:TBW * tb + TBW], cv[:].rearrange("p c h -> p (c h)"), ACT.Silu).then_inc(s_bc, 1)

        @block.vector
        def _(dve):
            tt = nc.vector.tensor_tensor
            stt = nc.vector.scalar_tensor_tensor
            ts = nc.vector.tensor_scalar
            nc.vector.memset(raw[:, :, 0:3], 0.0).then_inc(s_pad, 1)
            nc.vector.memset(g.G[:], 0.0).then_inc(s_pad, 1)
            dve.wait_ge(s_hi, 1)
            tt(wlo[:], w[:], whi[:].bitcast(F32), ALU.subtract).then_inc(s_lo, 1)
            dve.wait_ge(s_in, 64)
            for n in range(2):
                dve.wait_ge(s_pd, n + 1)
                tt(t["xb"][:, 8 * n:8 * n + 8, :], pd[n][:], hd[:, 1:2, :].to_broadcast([P, 8, HEADS]), ALU.add).then_inc(s_d, 1)
            dve.wait_ge(s_x, 1)
            ts(hd[:, 0, :], hd[:, 0, :], -1.0, None, ALU.mult).then_inc(s_neg, 1)
            dve.wait_ge(s_d, 2)
            stt(t["un"][:], t["xb"][:], -1.0, t["xb"][:], ALU.mult, ALU.min).then_inc(s_d, 1)
            dve.wait_ge(s_x, 2)
            ts(t["un"][:], t["ex"][:], 1.0, None, ALU.add).then_inc(s_d, 1)
            dve.wait_ge(s_d, 4)
            stt(t["dt"][:], t["un"][:], -1.0, t["ex"][:], ALU.add, ALU.subtract).then_inc(s_d, 1)
            dve.wait_ge(s_x, 3)
            nc.vector.reciprocal(t["un"][:], t["un"][:]).then_inc(s_d, 1)
            dve.wait_ge(s_d, 6)
            tt(t["dt"][:], t["dt"][:], t["un"][:], ALU.mult).then_inc(s_d, 1)
            dve.wait_ge(s_d, 7)
            tt(t["ln"][:], t["ln"][:], t["dt"][:], ALU.subtract).then_inc(s_d, 1)
            dve.wait_ge(s_d, 8)
            stt(t["dt"][:], t["xb"][:], 0.0, t["ln"][:], ALU.max, ALU.add).then_inc(s_d, 1)
            dve.wait_ge(s_d, 9)
            dve.wait_ge(s_neg, 1)
            stt(t["a"][:], t["dt"][:], 0.0,
                hd[:, 0:1, :].to_broadcast([P, TT, HEADS]), ALU.max, ALU.mult).then_inc(s_d, 1)
            for h2 in range(2):
                ts(packed[:, :, 0, :, h2, :], t["dt"][:].rearrange("p (t c) (j h) -> p j t c h", t=NT, h=2)[:, :, :, :, h2],
                   0.0, None, ALU.max).then_inc(s_d, 1)
            dve.wait_ge(s_x, 6)
            for h2 in range(2):
                ts(packed[:, :, 1, :, h2, :], t["z0"][:].rearrange("p (t c) (j h) -> p j t c h", t=NT, h=2)[:, :, :, :, h2],
                   msk[:, P:P + 1], None, ALU.add).then_inc(s_d, 1)
            dve.wait_ge(s_eT, NT)
            nc.vector.memset(eT[:, :, :, :, 0], 0.0).then_inc(s_zero, 1)
            for n in range(2 * NT):
                i = n // NT
                dve.wait_ge(s_raw, n + 1)
                dve.wait_ge(s_cv0, n + 1)
                for tap in range(3):
                    if tap:
                        dve.wait_ge(s_conv, 3 * n + tap)
                    stt(cv[:], raw[:, :, tap:tap + H], par[:, i, tap:tap + 1], cv[:], ALU.mult, ALU.add).then_inc(s_conv, 1)
            dve.wait_ge(s_pad, 2)
            for n in range(CP):
                dve.wait_ge(s_G, n + 1)
                for q in range(2):
                    rows = slice(64 * q, 64 * q + 64)
                    nc.vector.tensor_copy(g.G[rows, CP * n:CP * n + CP, q, :],
                                          ph[n % 2][:].rearrange("p (c m) -> p c m", c=CP)[rows, :, 64 * q:64 * q + 64]).then_inc(s_Gc, 1)

        @block.tensor
        def _(pe):
            pe.wait_ge(s_hi, 1)
            pe.wait_ge(s_lo, 1)
            for n in range(TT):
                for k in range(KE):
                    for m, (h, x) in enumerate(((g.hhi, whi), (g.hlo, whi), (g.hhi, wlo))):
                        mm = nc.tensor.matmul(pd[n // 8][:, n % 8, :], h[:, k, P * n:P * n + P], wd(x, k),
                                              start=(k == 0 and m == 0), stop=(k == KE - 1 and m == 2))
                if n % 8 == 7:
                    mm.then_inc(s_pd, 1)

            def project(n):
                i, tb = n // NT, n % NT
                if n >= 2:
                    pe.wait_ge(s_cv0, n - 1)
                    pe.wait_ge(s_raw, n - 1)
                split_matmuls(nc, ph[n % 2][:], whi, wlo, g, lambda x, k: wk(x, i, k),
                              lambda h, k: h[:, k, TBW * tb:TBW * tb + TBW]).then_inc(s_ph, 1)

            project(0)
            project(1)
            pe.wait_ge(s_d, 10)
            pe.wait_ge(s_in, 64)
            for n in range(2):
                nc.tensor.matmul(pm[n][:].rearrange("p t h -> p (t h)"), msk[:, 0:P],
                                 t["a"][:, 8 * n:8 * n + 8, :].rearrange("p t h -> p (t h)"), start=True, stop=True).then_inc(s_pm, 1)
            pe.wait_ge(s_x, 4)
            for tb in range(NT):
                if tb >= 2:
                    pe.wait_ge(s_eT, tb - 1)
                for c in range(CP):
                    mm = nc.tensor.transpose(pe_t[tb % 2][0:HEADS, P * c:P * c + P], t["ex"][:, CP * tb + c, :], g.ident[:])
                mm.then_inc(s_pt, 1)
            for n in range(2, 2 * NT):
                project(n)
            pe.wait_ge(s_bc, 2 * NT)
            for n in range(CP):
                if n >= 2:
                    pe.wait_ge(s_Gc, 2 * n - 2)
                for c in range(CP):
                    at = slice(P * (CP * n + c), P * (CP * n + c + 1))
                    mm = nc.tensor.matmul(ph[n % 2][:, P * c:P * c + P], BC[:, 0, at], BC[:, 1, at], start=True, stop=True)
                mm.then_inc(s_G, 1)


def phase_mixer(nc, d, g):
    with ExitStack() as ctx:
        def sb(name, shape, dt=F32):
            return ctx.enter_context(nc.sbuf_tensor(name, shape, dt))

        def sem(name):
            return ctx.enter_context(nc.semaphore(name))

        def bank(name):
            return ctx.enter_context(nc.psum_tensor(name, [P, TBW], F32))

        wst = sb("wst", [P, 2 * E + NPAR])
        whi = sb("whi", [P, 2, 2 * E], F32R)
        wlo = sb("wlo", [P, 2, 2 * E], F32R)
        par = sb("par_j", [P, 2, NPAR])
        wost = sb("wost", [P, 2, E])
        wohi = sb("wohi", [P, 2, E], F32R)
        wolo = sb("wolo", [P, 2, E], F32R)
        dtz = sb("dtz_j", [P, 2, 2, NT, 2 * CP])
        raw = sb("raw", [P, 2, 3 + H])
        cv = sb("cv", [P, 2, H])
        hs = sb("hs", [P, 2, TBW])
        sg = sb("sg", [P, 2, TBW])
        Hdt = sb("Hdt", [P, 2, CP, 2, HD])
        dec = sb("dec", [P, 2, TBW])
        one = sb("one", [P, 2 * CP, CHUNK])
        Z = sb("Z", [P, 2, CP, CHUNK])
        M = sb("M", [P, 2, CP, 2, CHUNK])
        y = sb("y", [P, 2, TBW])
        ye = [sb(f"ye{i}", [P, NT, TBW], F32R) for i in range(2)]
        yo = [sb(f"yo{i}", [P, 2, TBW], F32R) for i in range(2)]
        sq = sb("sq", [P, TBW])
        ph = [bank(f"ph{i}") for i in range(2)]
        pg = [bank(f"pg{i}") for i in range(2)]
        tr, Yp = bank("tr"), bank("Yp")
        po = [bank(f"po{i}") for i in range(2)]
        s = {n: sem("mx_" + n) for n in (
            "w", "wo", "dtz", "dec0", "dec1", "init", "whi", "wlo", "par", "wohi", "wolo", "Ah", "Ag", "raw", "cv0",
            "conv", "hs", "sg", "tr", "Hdt", "one", "Z", "M", "Y", "y", "yhi", "ylo", "sq", "sqa", "po", "acc", "pat")}
        block = ctx.enter_context(nc.Block())
        flat = lambda x: x.rearrange("p c h -> p (c h)")

        def y_of(k, part):
            return ye[part][:, k % NT, :] if (k // NT) % 2 == 0 else yo[part][:, k % 2, :]

        def y_free(i, k):
            tb = k % NT
            pair = i if k >= 0 else i - 1
            return count(pair, 0, 2, 4 * tb - (12 if (k // NT) % 2 == 0 else 4))

        @block.sync
        def _(sp):
            def load_w(j):
                sp.dma_start(wst[:], d["w_mix"][bass.ds(j, 1)].rearrange("a p n -> (a p) n")).then_inc(s["w"], 16)

            def load_dtz(j, slot):
                sp.dma_start(dtz[:, slot].rearrange("p a t n -> p (a t n)"), d["dtz"][bass.ds(j, 1)].rearrange("a p n -> (a p) n")).then_inc(s["dtz"], 16)

            def load_wo(pair):
                sp.dma_start(wost[:], d["w_out"][bass.ds(pair, 1)].rearrange("a m p n -> p (a m) n")).then_inc(s["wo"], 16)

            def load_dec(j, tb, slot):
                for q in range(2):
                    sp.dma_start(dec[64 * q:64 * q + 64, slot, :],
                                 d["decay"][bass.ds(j, 1), q, tb].rearrange("a h n -> a (h n)").to_broadcast([64, TBW])).then_inc(s[f"dec{slot}"], 16)

            sp.dma_start(one[:, 0, :], d["eye64"]).then_inc(s["pat"], 16)
            load_w(0)
            load_dtz(0, 0)
            load_dec(0, 0, 0)
            load_wo(0)

            def step(i, k):
                done, j, next_j, before, landed, pair = values(sp, count(i, k), i * 2 + (k + 1) // NT, i * 2 + (k // NT + 1),
                                                               count(i, k - 1), count(i, k - 1, 4, 16), i + 1)
                if alive(i, k + 1, UNITS):
                    wait(sp, s["Z"], done)
                    load_dec(j, (k + 1) % NT, (k + 1) % 2)
                if k % NT == 0 and alive(i, k + NT, UNITS):
                    sp.wait_ge(s["whi"], next_j)
                    sp.wait_ge(s["wlo"], next_j)
                    sp.wait_ge(s["par"], next_j)
                    load_w(next_j)
                if k % NT == 1 and alive(i, k + NT, UNITS):
                    wait(sp, s["dtz"], landed)
                    wait(sp, s["Hdt"], before)
                    wait(sp, s["Z"], before)
                    load_dtz(next_j, (k // NT + 1) % 2)
                if k == 4 and alive(i, BODY, UNITS):
                    both = values(sp, i * 2 + 2)[0]
                    sp.wait_ge(s["wohi"], both)
                    sp.wait_ge(s["wolo"], both)
                    load_wo(pair)

            steps(sp, step, UNITS, 0)

        @block.scalar
        def _(act):
            def split_w(j, slot):
                act.wait_ge(s["w"], j * 16 + 16)
                nc.scalar.activation(whi[:, slot], wst[:, 0:2 * E], ACT.Copy).then_inc(s["whi"], 1)
                nc.scalar.activation(par[:, slot], wst[:, 2 * E:], ACT.Copy).then_inc(s["par"], 1)

            split_w(0, 0)

            def step(i, k):
                u = k - 2
                if alive(i, u, UNITS):
                    wait(act, s["y"], count(i, u, 2, 2))
                    wait(act, s["po"], y_free(i, u))
                    nc.scalar.activation(y_of(u, 0), y[:, u % 2, :], ACT.Copy).then_inc(s["yhi"], 1)
                    wait(act, s["sqa"], count(i, u))
                    nc.scalar.activation(sq[:], y[:, u % 2, :], ACT.Square).then_inc(s["sq"], 1)
                if not alive(i, k, UNITS):
                    return
                wait(act, s["Ah"], count(i, k, 1, 1))
                wait(act, s["conv"], count(i, k, 3))
                if isinstance(i, int) and i == 0 and k == 0:
                    act.wait_ge(s["init"], 4)
                nc.scalar.activation(raw[:, :, 3:], ph[k % 2][:].rearrange("p (c h) -> p c h", c=2), ACT.Copy).then_inc(s["raw"], 1)
                wait(act, s["hs"], count(i, k))
                wait(act, s["par"], i * 2 + (k // NT + 1))
                nc.scalar.activation(flat(cv[:]), ph[k % 2][:], ACT.Identity, bias=par[:, k // NT, 4:5],
                                     scale=par[:, k // NT, 3:4]).then_inc(s["cv0"], 1)
                if k % NT == 1 and alive(i, k + NT, UNITS):
                    wait(act, s["Ag"], count(i, k - 1))
                    wait(act, s["y"], count(i, k - 1, 2))
                    split_w(i * 2 + (k // NT + 1), (k // NT + 1) % 2)
                if k in (2, 3):
                    act.wait_ge(s["wo"], i * 16 + 16)
                    wait(act, s["po"], count(i, 0, 2))
                    nc.scalar.activation(wohi[:, k - 2], wost[:, k - 2], ACT.Copy, scale=par[:, k - 2, 5:6]).then_inc(s["wohi"], 1)
                wait(act, s["conv"], count(i, k, 3, 3))
                wait(act, s["tr"], count(i, k, 1, -1))
                wait(act, s["y"], count(i, k, 2, -2))
                nc.scalar.activation(hs[:, k % 2, :], flat(cv[:]), ACT.Silu).then_inc(s["hs"], 1)
                wait(act, s["Ag"], count(i, k, 1, 1))
                nc.scalar.activation(sg[:, k % 2, :], pg[k % 2][:], ACT.Silu).then_inc(s["sg"], 1)

            steps(act, step, UNITS, 2)

        @block.vector
        def _(dve):
            tt = nc.vector.tensor_tensor
            stt = nc.vector.scalar_tensor_tensor
            nc.vector.memset(raw[:, :, 0:3], 0.0).then_inc(s["init"], 1)
            nc.vector.memset(g.acc[:], 0.0).then_inc(s["init"], 1)
            nc.vector.memset(g.sqa[:], 0.0).then_inc(s["init"], 1)
            dve.wait_ge(s["pat"], 16)
            nc.vector.tensor_copy(one[:, 1:, :], one[:, 0:1, :].to_broadcast([P, 2 * CP - 1, CHUNK])).then_inc(s["init"], 1)
            dve.wait_ge(s["init"], 4)

            def step(i, k):
                v = k - 1
                if alive(i, v, UNITS):
                    jv = v // NT
                    dve.wait_ge(s["dtz"], (i * 32 + (16 * jv + 16)))
                    wait(dve, s["Z"], count(i, v))
                    nc.vector.tensor_copy(one[:, :, 0], dtz[:, jv % 2, 1, v % NT, :]).then_inc(s["one"], 1)
                    dve.wait_ge(s[f"dec{v % 2}"], count(i, v - v % 2, 16, 32))
                    wait(dve, s["M"], count(i, v, 2))
                    dve.wait_ge(s["one"], count(i, v, 1, 1))
                    nc.vector.tensor_tensor_scan(Z[:].rearrange("p h c l -> p (h c l)"), dec[:, v % 2, :],
                                                 one[:].rearrange("p n l -> p (n l)"), 0.0, ALU.mult, ALU.add).then_inc(s["Z"], 1)
                    dve.wait_ge(s["tr"], count(i, v, 1, 1))
                    wait(dve, s["Y"], count(i, v, 1, -1))
                    tt(Hdt[:, v % 2], tr[:].rearrange("p (c h d) -> p c h d", c=CP, h=2),
                       dtz[:, jv % 2, 0, v % NT, :].rearrange("p (h c) -> p c h", h=2).unsqueeze(3).to_broadcast([P, CP, 2, HD]),
                       ALU.mult).then_inc(s["Hdt"], 1)
                u = k - 2
                if alive(i, u, UNITS):
                    dve.wait_ge(s["yhi"], count(i, u, 1, 1))
                    wait(dve, s["po"], y_free(i, u))
                    tt(y_of(u, 1), y[:, u % 2, :], y_of(u, 0).bitcast(F32), ALU.subtract).then_inc(s["ylo"], 1)
                if alive(i, k, UNITS):
                    dve.wait_ge(s["raw"], count(i, k, 1, 1))
                    dve.wait_ge(s["cv0"], count(i, k, 1, 1))
                    for tap in range(3):
                        if tap:
                            dve.wait_ge(s["conv"], count(i, k, 3, tap))
                        stt(cv[:], raw[:, :, tap:tap + H], par[:, k // NT, tap:tap + 1], cv[:], ALU.mult, ALU.add).then_inc(s["conv"], 1)
                if k in (2, 3) and alive(i, k, UNITS):
                    dve.wait_ge(s["wohi"], i * 2 + (k - 1))
                    wait(dve, s["po"], count(i, 0, 2))
                    stt(wolo[:, k - 2], wost[:, k - 2], par[:, k - 2, 5:6], wohi[:, k - 2].bitcast(F32),
                        ALU.mult, ALU.subtract).then_inc(s["wolo"], 1)
                if alive(i, v, UNITS):
                    dve.wait_ge(s["Y"], count(i, v, 1, 1))
                    wait(dve, s["yhi"], count(i, v, 1, -1))
                    wait(dve, s["sq"], count(i, v, 1, -1))
                    wait(dve, s["ylo"], count(i, v, 1, -1))
                    stt(y[:, v % 2, :], hs[:, v % 2, :], par[:, (v // NT) % 2, 6:7], Yp[:], ALU.mult, ALU.add).then_inc(s["y"], 1)
                    dve.wait_ge(s["sg"], count(i, v, 1, 1))
                    dve.wait_ge(s["y"], count(i, v, 2, 1))
                    tt(y[:, v % 2, :], y[:, v % 2, :], sg[:, v % 2, :], ALU.mult).then_inc(s["y"], 1)
                if alive(i, u, UNITS) and (u // NT) % 2 == 1:
                    pair = i if u >= 0 else i - 1
                    for m in range(CP):
                        n = 4 * (u % NT) + m
                        dve.wait_ge(s["po"], count(pair, 0, 2, n + 1))
                        wait(dve, s["acc"], count(pair, 0, 2, n - 7))
                        tt(g.acc[:, n, :], g.acc[:, n, :], po[n % 2][:], ALU.add).then_inc(s["acc"], 1)

            steps(dve, step, UNITS, 2)

        @block.gpsimd
        def _(pool):
            tt = nc.gpsimd.tensor_tensor

            def split_w(j, slot):
                pool.wait_ge(s["whi"], j + 1)
                tt(wlo[:, slot], wst[:, 0:2 * E], whi[:, slot].bitcast(F32), ALU.subtract).then_inc(s["wlo"], 1)

            split_w(0, 0)
            pool.wait_ge(s["init"], 4)

            def step(i, k):
                v = k - 1
                if alive(i, v, UNITS):
                    pool.wait_ge(s["Z"], count(i, v, 1, 1))
                    wait(pool, s["Y"], count(i, v))
                    for q in range(2):
                        tt(M[:, :, :, q, :], Z[:],
                           g.G[:, CP * (v % NT):CP * (v % NT) + CP, q, :].unsqueeze(1).to_broadcast([P, 2, CP, CHUNK]),
                           ALU.mult).then_inc(s["M"], 1)
                u = k - 2
                if alive(i, u, UNITS):
                    pool.wait_ge(s["sq"], count(i, u, 1, 1))
                    wait(pool, s["sqa"], count(i, u, 1, -3))
                    tt(g.sqa[:, u % NT, :], g.sqa[:, u % NT, :], sq[:], ALU.add).then_inc(s["sqa"], 1)
                if k % NT == 1 and alive(i, k + NT, UNITS) and alive(i, k, UNITS):
                    split_w(i * 2 + (k // NT + 1), (k // NT + 1) % 2)

            steps(pool, step, UNITS, 2)

        @block.tensor
        def _(pe):
            def project(i, k, part, out):
                tb, slot = k % NT, k // NT
                return split_matmuls(nc, out, whi, wlo, g, lambda x, c: x[:, slot, E * part + P * c:E * part + P * (c + 1)],
                                     lambda h, c: h[:, c, TBW * tb:TBW * tb + TBW])

            def step(i, k):
                if alive(i, k, UNITS):
                    if k % NT == 0:
                        pe.wait_ge(s["whi"], i * 2 + (k // NT + 1))
                        pe.wait_ge(s["wlo"], i * 2 + (k // NT + 1))
                    wait(pe, s["raw"], count(i, k, 1, -1))
                    wait(pe, s["cv0"], count(i, k, 1, -1))
                    project(i, k, 0, ph[k % 2][:]).then_inc(s["Ah"], 1)
                v = k - 1
                if alive(i, v, UNITS):
                    pe.wait_ge(s["hs"], count(i, v, 1, 1))
                    wait(pe, s["Hdt"], count(i, v))
                    for c in range(CP):
                        mm = nc.tensor.transpose(tr[:, P * c:P * c + P], hs[:, v % 2, P * c:P * c + P], g.ident[:])
                    mm.then_inc(s["tr"], 1)
                if alive(i, k, UNITS):
                    wait(pe, s["sg"], count(i, k, 1, -1))
                    project(i, k, 1, pg[k % 2][:]).then_inc(s["Ag"], 1)
                if alive(i, v, UNITS):
                    pe.wait_ge(s["Hdt"], count(i, v, 1, 1))
                    pe.wait_ge(s["M"], count(i, v, 2, 2))
                    wait(pe, s["y"], count(i, v, 2, -1))
                    for c in range(CP):
                        for h in range(2):
                            mm = nc.tensor.matmul(Yp[64 * h:64 * h + 64, P * c:P * c + P], Hdt[:, v % 2, c, h, :],
                                                  M[:, h, c].rearrange("p q l -> p (q l)"), start=True, stop=True)
                    mm.then_inc(s["Y"], 1)
                u = k - 2
                if alive(i, u, UNITS) and (u // NT) % 2 == 1:
                    pair = i if u >= 0 else i - 1
                    pe.wait_ge(s["yhi"], count(i, u, 1, 1))
                    pe.wait_ge(s["ylo"], count(i, u, 1, 1))
                    pe.wait_ge(s["wohi"], pair * 2 + 2)
                    pe.wait_ge(s["wolo"], pair * 2 + 2)
                    for m in range(CP):
                        n = 4 * (u % NT) + m
                        wait(pe, s["acc"], count(pair, 0, 2, n - 1))
                        mm = None
                        for tile in range(2):
                            kk = u - NT + NT * tile
                            cols = slice(P * m, P * m + P)
                            for a, b in ((0, wohi), (1, wohi), (0, wolo)):
                                mm = nc.tensor.matmul(po[n % 2][:], y_of(kk, a)[:, cols], b[:, tile, :],
                                                      start=(tile == 0 and a == 0 and b is wohi), stop=(tile == 1 and b is wolo))
                        mm.then_inc(s["po"], 1)

            steps(pe, step, UNITS, 2)


def phase_norm(nc, d, g):
    with ExitStack() as ctx:
        def sb(name, shape, dt=F32):
            return ctx.enter_context(nc.sbuf_tensor(name, shape, dt))

        def sem(name):
            return ctx.enter_context(nc.semaphore(name))

        ones = sb("nm_ones", [P, 2])
        var = sb("nm_var", [P, TT])
        root = sb("nm_root", [P, TT])
        inv = sb("nm_inv", [P, TT])
        st = sb("nm_st", [P, TT, 6])
        mv = sb("nm_mv", [P, TT, 2])
        rs = sb("nm_rs", [P, TT])
        mrs = sb("nm_mrs", [P, TT])
        pv = ctx.enter_context(nc.psum_tensor("nm_pv", [P, TT, 2], F32))
        ph = [ctx.enter_context(nc.psum_tensor(f"nm_h{i}", [P, E], F32)) for i in range(3)]
        pt = [ctx.enter_context(nc.psum_tensor(f"nm_t{i}", [P, KE, P], F32)) for i in range(3)]
        s_one, s_pv, s_rms, s_root, s_h, s_x, s_st, s_mv, s_c, s_n, s_t, s_hi, s_lo = [
            sem("nm_" + n) for n in ("one", "pv_s", "rms", "root_s", "h", "x", "st_s", "mv_s", "c", "n", "t", "hi", "lo")]
        block = ctx.enter_context(nc.Block())

        @block.tensor
        def _(pe):
            pe.wait_ge(s_one, 1)
            for n in range(TT):
                mm = nc.tensor.matmul(pv[:, n, :], g.sqa[:].rearrange("p t n -> p (t n)")[:, P * n:P * n + P], ones[:],
                                      start=True, stop=True)
            mm.then_inc(s_pv, 1)
            for n in range(TT):
                if n >= 3:
                    pe.wait_ge(s_x, n - 2)
                for k in range(KE):
                    for m, h in enumerate((g.hhi, g.hlo)):
                        mm = nc.tensor.matmul(ph[n % 3][:, P * k:P * k + P], h[:, k, P * n:P * n + P], g.identr[:],
                                              start=(m == 0), stop=(m == 1))
                mm.then_inc(s_h, 1)
            for n in range(TT):
                pe.wait_ge(s_n, n + 1)
                if n >= 3:
                    pe.wait_ge(s_hi, n - 2)
                    pe.wait_ge(s_lo, n - 2)
                for k in range(KE):
                    mm = nc.tensor.transpose(pt[n % 3][:, k, :], g.acc[:, n, P * k:P * k + P], g.ident[:])
                mm.then_inc(s_t, 1)

        @block.scalar
        def _(act):
            act.wait_ge(s_rms, 1)
            nc.scalar.activation(root[:], var[:], ACT.Sqrt).then_inc(s_root, 1)
            act.wait_ge(s_mv, TT + 1)
            nc.scalar.activation(root[:], var[:], ACT.Sqrt).then_inc(s_root, 1)
            for n in range(TT):
                act.wait_ge(s_t, n + 1)
                nc.scalar.activation(g.hhi[:, :, P * n:P * n + P], pt[n % 3][:], ACT.Copy).then_inc(s_hi, 1)

        @block.vector
        def _(dve):
            tt = nc.vector.tensor_tensor
            stt = nc.vector.scalar_tensor_tensor
            ts = nc.vector.tensor_scalar
            chain = [0]

            def after(ins):
                chain[0] += 1
                ins.then_inc(s_c, 1)
                dve.wait_ge(s_c, chain[0])

            def rsqrt(out):
                after(nc.vector.reciprocal(inv[:], root[:]))
                after(tt(inv[:], inv[:], var[:], ALU.mult))
                after(tt(inv[:], inv[:], root[:], ALU.add))
                after(ts(inv[:], inv[:], 0.5, None, ALU.mult))
                after(nc.vector.reciprocal(out, inv[:]))

            nc.vector.memset(ones[:], 1.0).then_inc(s_one, 1)
            dve.wait_ge(s_pv, 1)
            ts(var[:], pv[:, :, 0], 1.0 / INTER, EPS, ALU.mult, ALU.add).then_inc(s_rms, 1)
            dve.wait_ge(s_root, 1)
            rsqrt(rs[:])
            for n in range(TT):
                dve.wait_ge(s_h, n + 1)
                stt(g.acc[:, n, :], g.acc[:, n, :], rs[:, n:n + 1], ph[n % 3][:], ALU.mult, ALU.add).then_inc(s_x, 1)
                dve.wait_ge(s_x, n + 1)
                nc.vector.bn_stats(st[:, n, :], g.acc[:, n, :]).then_inc(s_st, 1)
                dve.wait_ge(s_st, n + 1)
                nc.vector.bn_aggr(mv[:, n, :], st[:, n, :]).then_inc(s_mv, 1)
            dve.wait_ge(s_mv, TT)
            ts(var[:], mv[:, :, 1], EPS, None, ALU.add).then_inc(s_mv, 1)
            dve.wait_ge(s_root, 2)
            rsqrt(rs[:])
            after(stt(mrs[:], mv[:, :, 0], -1.0, rs[:], ALU.mult, ALU.mult))
            for n in range(TT):
                ts(g.acc[:, n, :], g.acc[:, n, :], rs[:, n:n + 1], mrs[:, n:n + 1], ALU.mult, ALU.add).then_inc(s_n, 1)
                if n >= 2:
                    dve.wait_ge(s_hi, n - 1)
                    tt(g.hlo[:, :, P * (n - 2):P * (n - 1)], pt[(n - 2) % 3][:], g.hhi[:, :, P * (n - 2):P * (n - 1)].bitcast(F32),
                       ALU.subtract).then_inc(s_lo, 1)
            for n in range(TT - 2, TT):
                dve.wait_ge(s_hi, n + 1)
                tt(g.hlo[:, :, P * n:P * n + P], pt[n % 3][:], g.hhi[:, :, P * n:P * n + P].bitcast(F32),
                   ALU.subtract).then_inc(s_lo, 1)


def phase_ffn(nc, d, g):
    with ExitStack() as ctx:
        def sb(name, shape, dt=F32):
            return ctx.enter_context(nc.sbuf_tensor(name, shape, dt))

        def sem(name):
            return ctx.enter_context(nc.semaphore(name))

        def bank(name):
            return ctx.enter_context(nc.psum_tensor(name, [P, TBW], F32))

        wst = sb("f_wst", [P, 2 * E])
        whi = sb("f_whi", [P, 2, 2 * E], F32R)
        wlo = sb("f_wlo", [P, 2, 2 * E], F32R)
        wost = sb("f_wost", [P, 2, E])
        wohi = sb("f_wohi", [P, 2, E], F32R)
        wolo = sb("f_wolo", [P, 2, E], F32R)
        sg = sb("f_sg", [P, 2, TBW])
        y = sb("f_y", [P, 2, TBW])
        ye = [sb(f"f_ye{i}", [P, NT, TBW], F32R) for i in range(2)]
        yo = [sb(f"f_yo{i}", [P, 2, TBW], F32R) for i in range(2)]
        pg = [bank(f"f_pg{i}") for i in range(2)]
        pu = [bank(f"f_pu{i}") for i in range(2)]
        po = [bank(f"f_po{i}") for i in range(4)]
        s = {n: sem("ff_" + n) for n in ("w", "wo", "whi", "wlo", "wohi", "wolo", "Ag", "Au", "sg", "y", "yhi", "ylo", "po", "acc")}
        block = ctx.enter_context(nc.Block())

        def y_of(k, part):
            return ye[part][:, k % NT, :] if (k // NT) % 2 == 0 else yo[part][:, k % 2, :]

        def y_free(i, k):
            pair = i if k >= 0 else i - 1
            return count(pair, 0, 2, 4 * (k % NT) - (12 if (k // NT) % 2 == 0 else 4))

        @block.sync
        def _(sp):
            def load_w(m):
                sp.dma_start(wst[:], d["w_ffn"][bass.ds(m, 1)].rearrange("a p n -> (a p) n")).then_inc(s["w"], 16)

            def load_wo(pair):
                sp.dma_start(wost[:], d["w_down"][bass.ds(pair, 1)].rearrange("a m p n -> p (a m) n")).then_inc(s["wo"], 16)

            load_w(0)
            load_wo(0)

            def step(i, k):
                next_m, both, pair = values(sp, i * 2 + (k // NT + 1), i * 2 + 2, i + 1)
                if k % NT == 0 and alive(i, k + NT, FUNITS):
                    sp.wait_ge(s["whi"], next_m)
                    sp.wait_ge(s["wlo"], next_m)
                    load_w(next_m)
                if k == 4 and alive(i, BODY, FUNITS):
                    sp.wait_ge(s["wohi"], both)
                    sp.wait_ge(s["wolo"], both)
                    load_wo(pair)

            steps(sp, step, FUNITS, 0)

        @block.scalar
        def _(act):
            def split_w(m, slot):
                act.wait_ge(s["w"], m * 16 + 16)
                nc.scalar.activation(whi[:, slot], wst[:], ACT.Copy).then_inc(s["whi"], 1)

            split_w(0, 0)

            def step(i, k):
                u = k - 1
                if alive(i, u, FUNITS):
                    act.wait_ge(s["y"], count(i, u, 1, 1))
                    wait(act, s["po"], y_free(i, u))
                    nc.scalar.activation(y_of(u, 0), y[:, u % 2, :], ACT.Copy).then_inc(s["yhi"], 1)
                if not alive(i, k, FUNITS):
                    return
                if k % NT == 1 and alive(i, k + NT, FUNITS):
                    wait(act, s["Au"], count(i, k - 1))
                    split_w(i * 2 + (k // NT + 1), (k // NT + 1) % 2)
                if k in (2, 3):
                    act.wait_ge(s["wo"], i * 16 + 16)
                    wait(act, s["po"], count(i, 0, 2))
                    nc.scalar.activation(wohi[:, k - 2], wost[:, k - 2], ACT.Copy).then_inc(s["wohi"], 1)
                act.wait_ge(s["Ag"], count(i, k, 1, 1))
                wait(act, s["y"], count(i, k, 1, -1))
                nc.scalar.activation(sg[:, k % 2, :], pg[k % 2][:], ACT.Silu).then_inc(s["sg"], 1)

            steps(act, step, FUNITS, 2)

        @block.vector
        def _(dve):
            tt = nc.vector.tensor_tensor

            def step(i, k):
                v = k - 1
                if alive(i, v, FUNITS):
                    dve.wait_ge(s["yhi"], count(i, v, 1, 1))
                    wait(dve, s["po"], y_free(i, v))
                    tt(y_of(v, 1), y[:, v % 2, :], y_of(v, 0).bitcast(F32), ALU.subtract).then_inc(s["ylo"], 1)
                if k in (2, 3) and alive(i, k, FUNITS):
                    dve.wait_ge(s["wohi"], i * 2 + (k - 1))
                    wait(dve, s["po"], count(i, 0, 2))
                    tt(wolo[:, k - 2], wost[:, k - 2], wohi[:, k - 2].bitcast(F32), ALU.subtract).then_inc(s["wolo"], 1)
                if alive(i, k, FUNITS):
                    dve.wait_ge(s["Au"], count(i, k, 1, 1))
                    dve.wait_ge(s["sg"], count(i, k, 1, 1))
                    wait(dve, s["yhi"], count(i, k, 1, -1))
                    wait(dve, s["ylo"], count(i, k, 1, -1))
                    tt(y[:, k % 2, :], sg[:, k % 2, :], pu[k % 2][:], ALU.mult).then_inc(s["y"], 1)
                if alive(i, v, FUNITS) and (v // NT) % 2 == 1:
                    pair = i if v >= 0 else i - 1
                    for m in range(CP):
                        n = 4 * (v % NT) + m
                        dve.wait_ge(s["po"], count(pair, 0, 2, n + 1))
                        wait(dve, s["acc"], count(pair, 0, 2, n - 7))
                        tt(g.acc[:, n, :], g.acc[:, n, :], po[n % 4][:], ALU.add).then_inc(s["acc"], 1)

            steps(dve, step, FUNITS, 1)

        @block.gpsimd
        def _(pool):
            def split_w(m, slot):
                pool.wait_ge(s["whi"], m + 1)
                nc.gpsimd.tensor_tensor(wlo[:, slot], wst[:], whi[:, slot].bitcast(F32), ALU.subtract).then_inc(s["wlo"], 1)

            split_w(0, 0)

            def step(i, k):
                if k % NT == 1 and alive(i, k + NT, FUNITS) and alive(i, k, FUNITS):
                    split_w(i * 2 + (k // NT + 1), (k // NT + 1) % 2)

            steps(pool, step, FUNITS, 0)

        @block.tensor
        def _(pe):
            def project(i, k, part, out):
                tb, slot = k % NT, k // NT
                return split_matmuls(nc, out, whi, wlo, g, lambda x, c: x[:, slot, E * part + P * c:E * part + P * (c + 1)],
                                     lambda h, c: h[:, c, TBW * tb:TBW * tb + TBW])

            def step(i, k):
                if alive(i, k, FUNITS):
                    if k % NT == 0:
                        pe.wait_ge(s["whi"], i * 2 + (k // NT + 1))
                        pe.wait_ge(s["wlo"], i * 2 + (k // NT + 1))
                    wait(pe, s["sg"], count(i, k, 1, -1))
                    project(i, k, 0, pg[k % 2][:]).then_inc(s["Ag"], 1)
                    wait(pe, s["y"], count(i, k, 1, -1))
                    project(i, k, 1, pu[k % 2][:]).then_inc(s["Au"], 1)
                u = k - 1
                if alive(i, u, FUNITS) and (u // NT) % 2 == 1:
                    pair = i if u >= 0 else i - 1
                    pe.wait_ge(s["yhi"], count(i, u, 1, 1))
                    pe.wait_ge(s["ylo"], count(i, u, 1, 1))
                    pe.wait_ge(s["wohi"], pair * 2 + 2)
                    pe.wait_ge(s["wolo"], pair * 2 + 2)
                    for m in range(CP):
                        n = 4 * (u % NT) + m
                        wait(pe, s["acc"], count(pair, 0, 2, n - 3))
                        mm = None
                        for tile in range(2):
                            kk = u - NT + NT * tile
                            cols = slice(P * m, P * m + P)
                            for a, b in ((0, wohi), (1, wohi), (0, wolo)):
                                mm = nc.tensor.matmul(po[n % 4][:], y_of(kk, a)[:, cols], b[:, tile, :],
                                                      start=(tile == 0 and a == 0 and b is wohi), stop=(tile == 1 and b is wolo))
                        mm.then_inc(s["po"], 1)

            steps(pe, step, FUNITS, 1)


def phase_out(nc, d, g, out):
    with ExitStack() as ctx:
        def sb(name, shape, dt=F32):
            return ctx.enter_context(nc.sbuf_tensor(name, shape, dt))

        def sem(name):
            return ctx.enter_context(nc.semaphore(name))

        var = sb("o_var", [P, TT])
        root = sb("o_root", [P, TT])
        inv = sb("o_inv", [P, TT])
        st = sb("o_st", [P, TT, 6])
        mv = sb("o_mv", [P, TT, 2])
        rs = sb("o_rs", [P, TT])
        mrs = sb("o_mrs", [P, TT])
        s_st, s_mv, s_root, s_c, s_n, s_out = [sem("o_" + n) for n in ("st_s", "mv_s", "root_s", "c", "n", "out")]
        block = ctx.enter_context(nc.Block())

        @block.vector
        def _(dve):
            tt = nc.vector.tensor_tensor
            ts = nc.vector.tensor_scalar
            chain = [0]

            def after(ins):
                chain[0] += 1
                ins.then_inc(s_c, 1)
                dve.wait_ge(s_c, chain[0])

            for n in range(TT):
                nc.vector.bn_stats(st[:, n, :], g.acc[:, n, :]).then_inc(s_st, 1)
            for n in range(TT):
                dve.wait_ge(s_st, n + 1)
                nc.vector.bn_aggr(mv[:, n, :], st[:, n, :]).then_inc(s_mv, 1)
            dve.wait_ge(s_mv, TT)
            ts(var[:], mv[:, :, 1], EPS, None, ALU.add).then_inc(s_mv, 1)
            dve.wait_ge(s_root, 1)
            after(nc.vector.reciprocal(inv[:], root[:]))
            after(tt(inv[:], inv[:], var[:], ALU.mult))
            after(tt(inv[:], inv[:], root[:], ALU.add))
            after(ts(inv[:], inv[:], 0.5, None, ALU.mult))
            after(nc.vector.reciprocal(rs[:], inv[:]))
            after(nc.vector.scalar_tensor_tensor(mrs[:], mv[:, :, 0], -1.0, rs[:], ALU.mult, ALU.mult))
            for n in range(TT):
                ts(g.acc[:, n, :], g.acc[:, n, :], rs[:, n:n + 1], mrs[:, n:n + 1], ALU.mult, ALU.add).then_inc(s_n, 1)

        @block.scalar
        def _(act):
            act.wait_ge(s_mv, TT + 1)
            nc.scalar.activation(root[:], var[:], ACT.Sqrt).then_inc(s_root, 1)

        @block.sync
        def _(sp):
            o = out.rearrange("b (t p) e -> p (b t) e", p=P)
            for n in range(0, TT, 4):
                sp.wait_ge(s_n, n + 4)
                sp.dma_start(o[:, n:n + 4, :], g.acc[:, n:n + 4, :]).then_inc(s_out, 16)
            sp.wait_ge(s_out, 16 * (TT // 4))


def build(nc, d, out, stop=None):
    with ExitStack() as ctx:
        g = Shared()
        g.hhi = ctx.enter_context(nc.sbuf_tensor("hhi", [P, KE, TOK], F32R))
        g.hlo = ctx.enter_context(nc.sbuf_tensor("hlo", [P, KE, TOK], F32R))
        g.ident = ctx.enter_context(nc.sbuf_tensor("ident", [P, P], F32))
        g.identr = ctx.enter_context(nc.sbuf_tensor("identr", [P, P], F32R))
        phase_constants(nc, d, g)
        phase_token(nc, d, g)
        g.acc = ctx.enter_context(nc.sbuf_tensor("acc", [P, TT, E], F32))
        with ExitStack() as mixer:
            g.G = mixer.enter_context(nc.sbuf_tensor("G", [P, TT, 2, CHUNK], F32))
            phase_decays(nc, d, g)
            g.sqa = mixer.enter_context(nc.sbuf_tensor("sqa", [P, NT, TBW], F32))
            phase_mixer(nc, d, g)
            phase_norm(nc, d, g)
        phase_ffn(nc, d, g)
        phase_out(nc, d, g, out)


def kernel(**inputs):
    import numpy as np
    import concourse.bacc as bacc
    from concourse.bass_utils import run_bass_kernel_spmd

    a = {k: np.asarray(v) for k, v in inputs.items()}
    lay = np.ascontiguousarray

    def tiles(w):
        r = w.shape[0] // P
        return w.reshape(r, P, KE, P).transpose(0, 3, 2, 1).reshape(r, P, E)

    W_in = a["L0_attn_W_in"]
    gate, hidden, bc, dtw = W_in[:INTER], W_in[INTER:2 * INTER], W_in[2 * INTER:2 * INTER + 2 * P], W_in[2 * INTER + 2 * P:]
    cw, cb = a["L0_attn_conv_w"], a["L0_attn_conv_b"]
    par = np.zeros((NJ, P, NPAR), np.float32)
    par[:, :, 0:4] = cw[:INTER].reshape(NJ, P, TAPS)
    par[:, :, 4] = cb[:INTER].reshape(NJ, P)
    par[:, :, 5] = a["L0_attn_norm_w"].reshape(NJ, P)
    par[:, :, 6] = np.repeat(a["L0_attn_D"], HD).reshape(NJ, P)
    par_bc = np.zeros((P, 2, NPAR), np.float32)
    par_bc[:, :, 0:4] = cw[INTER:].reshape(2, P, TAPS).transpose(1, 0, 2)
    par_bc[:, :, 4] = cb[INTER:].reshape(2, P).T
    k, s_ = np.arange(P)[:, None], np.arange(P)[None, :]
    mask = np.zeros((P, P + 1), np.float32)
    mask[:, :P] = (k // CHUNK == s_ // CHUNK) & ((k > s_) | (k % CHUNK == 0))
    mask[:, P] = np.arange(P) % CHUNK == 0
    arrays = {
        "x": lay(a["x"].transpose(3, 2, 1, 0).reshape(P, H, NB)),
        "log_dt": a["L0_tok_log_dt"],
        "tokpar": lay(np.stack([a["L0_tok_inv_A_real"], a["L0_tok_A_imag"], a["L0_tok_B_ri"][..., 0],
                                a["L0_tok_B_ri"][..., 1]]).reshape(4, 2, H // 2, NS).transpose(1, 3, 0, 2).reshape(P, 4, H // 2)),
        "ident": np.eye(P, dtype=np.float32),
        "eye64": np.tile(np.eye(CHUNK, dtype=np.float32), (2, 1)),
        "mask": mask,
        "A_log": a["L0_attn_A_log"],
        "dt_bias": a["L0_attn_dt_bias"],
        "w_bc": lay(np.concatenate([tiles(bc)[0], tiles(bc)[1],
                                    dtw.reshape(HEADS, KE, P).transpose(2, 1, 0).reshape(P, KE * HEADS)], 1)),
        "par_bc": par_bc,
        "w_mix": lay(np.concatenate([tiles(hidden), tiles(gate), par], 2)),
        "w_out": lay(a["L0_attn_W_out"].T.reshape(NJ // 2, 2, P, E)),
        "w_ffn": lay(np.concatenate([tiles(a["L0_ffn_w_gate"]), tiles(a["L0_ffn_w_up"])], 2)),
        "w_down": lay(a["L0_ffn_w_down"].T.reshape(NM // 2, 2, P, E)),
    }
    nc = bacc.Bacc("TRN2", target_bir_lowering=False, num_devices=1)
    d = {n: nc.dram_tensor("in_" + n, v.shape, F32, kind="ExternalInput").ap() for n, v in arrays.items()}
    d["decay"] = nc.dram_tensor("decay", (NJ, 2, NT, 2, CP * CHUNK), F32, kind="Internal").ap()
    d["dtz"] = nc.dram_tensor("dtz", (NJ, P, 2 * NT * 2 * CP), F32, kind="Internal").ap()
    out = nc.dram_tensor("out0", (NB, H, E), F32, kind="ExternalOutput").ap()
    build(nc, d, out)
    r = run_bass_kernel_spmd(nc, [{"in_" + n: v for n, v in arrays.items()}], core_ids=[0])
    return r.results[0]["out0"]
```

```python
from contextlib import ExitStack

import concourse.bass as bass
from concourse import mybir

F32 = mybir.dt.float32
F32R = mybir.dt.float32r
ALU = mybir.AluOpType
ACT = mybir.ActivationFunctionType

P = 128
NB, H, NS = 8, 256, 64
E = 512
TOK = NB * H
KE = E // P
INTER, HEADS, HD = 4096, 64, 64
NJ = INTER // P
TAPS = 4
CHUNK = 64
TBW = 512
NT = TOK // TBW
CP = TBW // P
TT = TOK // P
NM = 2048 // P
NPAR = 8
EPS = 1e-5
A_LO, A_HI, LB = 4, 4, 32
BCW = 2 * E + HEADS * KE
UNITS = NJ * NT
FUNITS = NM * NT
BODY = 8


class Shared:
    pass


def count(i, k, per=1, more=0):
    if isinstance(i, int):
        return per * (BODY * i + k) + more
    return i * (per * BODY) + (per * k + more)


def wait(eng, sem, value):
    if isinstance(value, int) and value <= 0:
        return
    eng.wait_ge(sem, value)


def values(eng, *v):
    return [x if isinstance(x, int) else eng.snap(x) for x in v]


def alive(i, k, units):
    return not isinstance(i, int) or 0 <= BODY * i + k < units


def steps(eng, step, units, tail):
    bodies = units // BODY
    for k in range(BODY):
        step(0, k)
    with eng.Fori(1, bodies - 1) as i:
        for k in range(BODY):
            step(i, k)
    for k in range(BODY):
        step(bodies - 1, k)
    for k in range(tail):
        step(bodies, k)


def phase_token(nc, d, g):
    with ExitStack() as ctx:
        def sb(name, shape, dt=F32):
            return ctx.enter_context(nc.sbuf_tensor(name, shape, dt))

        def sem(name):
            return ctx.enter_context(nc.semaphore(name))

        HH = H // 2
        GR = 16
        HG = GR // 2
        PAIRS = HH // GR
        QSTEPS = 6 * 5
        POW = 9
        x = sb("x", [P, H, NB])
        par = sb("tok_par", [P, 5, HH])
        w = sb("tok_w", [P, 8, HH])
        pw = sb("tok_pow", [P, POW, 2, HH])
        V = sb("V", [P, 2, HH, LB])
        Q = sb("Q", [P, 2, HH, A_LO, A_HI])
        tq = sb("tok_tq", [P, 2, HH * A_LO])
        Vs = sb("Vs", [P, 2, 2, GR, LB])
        Qs = sb("Qs", [P, 2, 2, GR, A_LO * A_HI])
        T = sb("T", [P, 4, 2, HG, A_LO * A_HI, NB])
        X2 = sb("X2", [P, 2, GR, A_HI, NB])
        Y = sb("Y", [P, 2, 4, P])
        W = lambda i: w[:, i, :]
        tv = T[:].rearrange("p s r h a c -> p (s r h a c)")[:, 0:HH * LB].rearrange("p (i n) -> p i n", i=2)
        ps = [ctx.enter_context(nc.psum_tensor(f"tok_ps{i}", [P, 4, P], F32)) for i in range(2)]
        pt = [ctx.enter_context(nc.psum_tensor(f"tok_pt{i}", [P, GR, LB], F32)) for i in range(2)]
        s_in = sem("tok_in")
        s_inx = sem("tok_inx")
        s_ident = sem("tok_ident")
        s_bcw = sem("tok_bcw")
        s_bchi = sem("tok_bchi")
        s_bclo = sem("tok_bclo")
        s_exp = sem("tok_exp")
        s_dv = sem("tok_dv")
        s_pow = sem("tok_pow_s")
        s_q = sem("tok_q")
        s_v = sem("tok_v")
        s_vs = sem("tok_vs")
        s_qs = sem("tok_qs")
        s_T = sem("tok_T")
        s_Tp = sem("tok_Tp")
        s_mm = sem("tok_mm")
        s_y = sem("tok_y")
        s_tr = sem("tok_tr")
        s_x2 = sem("tok_x2")
        s_hi = sem("tok_hi")
        s_lo = sem("tok_lo")
        block = ctx.enter_context(nc.Block())

        def group(i, k):
            return i * 2 + k

        def tokens(i, k):
            return i * GR + (GR * (k // 2) + HH * (k % 2))

        def there(i, k):
            return not isinstance(i, int) or 0 <= group(i, k) < 2 * PAIRS

        def pairs(eng, step):
            step(0, 0)
            step(0, 1)
            with eng.Fori(1, PAIRS - 1) as i:
                step(i, 0)
                step(i, 1)
            step(PAIRS - 1, 0)
            step(PAIRS - 1, 1)
            step(PAIRS, 0)
            step(PAIRS, 1)

        def of_group(t, i, k):
            return t.rearrange("p k (c h) -> p k c h", c=NB)[:, :, :, bass.ds(tokens(i, k), GR)]

        def of_half_tokens(i, k):
            return bass.ds(i * GR + GR * (k // 2), GR)

        def of_half(i, k, half):
            return (bass.ds(tokens(i, k) + HG * half, HG), [P, HG, A_LO * A_HI, NB],
                    lambda r: Qs[:, k % 2, r, HG * half:HG * half + HG, :].unsqueeze(3))

        @block.sync
        def _(sp):
            for half in range(2):
                rows = slice(64 * half, 64 * half + 64)
                sp.dma_start(par[rows, 0, :], d["log_dt"][HH * half:HH * half + HH].partition_broadcast(64)).then_inc(s_in, 16)
            sp.dma_start(par[:, 1:5, :], d["tokpar"]).then_inc(s_in, 16)
            sp.dma_start(g.stage[:], d["w_bc"]).then_inc(s_bcw, 16)
            sp.dma_start(x[:], d["x"]).then_inc(s_inx, 16)
            sp.dma_start(g.ident[:], d["ident"]).then_inc(s_ident, 16)

        @block.scalar
        def _(act):
            act.wait_ge(s_in, 48)
            nc.scalar.activation(W(0), par[:, 0, :], ACT.Exp).then_inc(s_exp, 1)
            nc.scalar.activation(W(1), par[:, 1, :], ACT.Exp).then_inc(s_exp, 1)
            act.wait_ge(s_bcw, 16)
            nc.scalar.activation(g.w2hi[:], g.stage[:], ACT.Copy).then_inc(s_bchi, 1)

            def spread_q(i, k):
                n, slot = group(i, k), k % 2
                wait(act, s_T, n * 3 - 3)
                wait(act, s_Tp, n - 1)
                for rows in (slice(0, 64), slice(64, 128)):
                    q = Q[64 * slot:64 * slot + 64, :, of_half_tokens(i, k)]
                    nc.scalar.activation(Qs[rows, slot], q.rearrange("p r h a b -> p r h (a b)"), ACT.Copy).then_inc(s_qs, 1)

            def spread_v(i, k):
                n, slot = group(i, k), k % 2
                wait(act, s_mm, n * 2 - 2)
                for rows, part, src, sign in ((slice(0, 64), 0, 0, 1.0), (slice(64, 128), 0, 1, -1.0),
                                              (slice(0, 64), 1, 1, -1.0), (slice(64, 128), 1, 0, -1.0)):
                    nc.scalar.activation(Vs[rows, slot, part], V[64 * slot:64 * slot + 64, src, of_half_tokens(i, k), :],
                                         ACT.Copy, scale=sign).then_inc(s_vs, 1)

            act.wait_ge(s_v, 1)
            act.wait_ge(s_q, QSTEPS)
            for k in range(2):
                spread_q(0, k)
            for k in range(2):
                spread_v(0, k)

            def step(i, k):
                n = group(i, k)
                if there(i, k + 2):
                    spread_q(i, k + 2)
                if there(i, k - 2):
                    act.wait_ge(s_x2, n - 1)
                    nc.scalar.activation(of_group(g.hhi[:], i, k - 2), X2[:, k % 2].rearrange("p h k c -> p k c h"),
                                         ACT.Copy).then_inc(s_hi, 1)
                if there(i, k):
                    act.wait_ge(s_mm, n * 2 + 2)
                    wait(act, s_tr, n - 1)
                    nc.scalar.activation(Y[:, k % 2], ps[k % 2][:], ACT.Copy).then_inc(s_y, 1)
                if there(i, k + 2):
                    spread_v(i, k + 2)

            pairs(act, step)

        def grow(tt, s, start, t, re, im, out_re, out_im, m, wait_for):
            dims = [int(v) for v in re.shape[1:]]
            size = dims[0] * (dims[1] if len(dims) > 1 else 1)
            t0, t1 = [t[:, i, 0:size].rearrange("p (h b) -> p h b", h=dims[0]) for i in range(2)]
            r, i = [pw[:, m, q, :].unsqueeze(2).to_broadcast([P] + dims) for q in range(2)]
            tt(out_re, re, r, ALU.mult).then_inc(s, 1)
            tt(t0, im, i, ALU.mult).then_inc(s, 1)
            tt(out_im, im, r, ALU.mult).then_inc(s, 1)
            tt(t1, re, i, ALU.mult).then_inc(s, 1)
            wait_for(start + 4)
            tt(out_re, out_re, t0, ALU.subtract).then_inc(s, 1)
            tt(out_im, out_im, t1, ALU.add).then_inc(s, 1)
            wait_for(start + 6)
            return start + 6

        @block.gpsimd
        def _(pool):
            tt = nc.gpsimd.tensor_tensor
            pool.wait_ge(s_bchi, 1)
            tt(g.w2lo[:], g.stage[:], g.w2hi[:].bitcast(F32), ALU.subtract).then_inc(s_bclo, 1)
            pool.wait_ge(s_pow, 1)
            q = lambda lo, hi: (Q[:, 0, :, lo, hi], Q[:, 1, :, lo, hi])
            at = 0

            def more(src, dst, m):
                return grow(tt, s_q, at, tq, *src, *dst, m, lambda v: pool.wait_ge(s_q, v))

            at = more(q(slice(0, 1), 0), q(slice(1, 2), 0), 5)
            at = more(q(slice(0, 2), 0), q(slice(2, 4), 0), 6)
            at = more(q(slice(0, 4), 0), q(slice(0, 4), 1), 7)
            for hi in range(2):
                at = more(q(slice(0, 4), hi), q(slice(0, 4), 2 + hi), 8)
            assert at == QSTEPS

            def product(i, k):
                n = group(i, k)
                pool.wait_ge(s_qs, n * 2 + 2)
                wait(pool, s_mm, n * 2 - 2)
                h, src, q = of_half(i, k, 1)
                tt(T[:, 2 * (k % 2) + 1, 1], x[:, h, :].unsqueeze(2).to_broadcast(src), q(1).to_broadcast(src),
                   ALU.mult).then_inc(s_Tp, 1)

            pool.wait_ge(s_inx, 16)
            product(0, 0)
            product(0, 1)

            def step(i, k):
                if there(i, k - 2) and not (isinstance(i, int) and group(i, k) == 2 * PAIRS + 1):
                    n = group(i, k)
                    pool.wait_ge(s_hi, n - 1)
                    tt(of_group(g.hlo[:], i, k - 2), X2[:, k % 2].rearrange("p h k c -> p k c h"),
                       of_group(g.hhi[:].bitcast(F32), i, k - 2), ALU.subtract).then_inc(s_lo, 1)
                if there(i, k + 2):
                    product(i, k + 2)

            pairs(pool, step)

        @block.vector
        def _(dve):
            chain = [0]

            def after(ins):
                chain[0] += 1
                ins.then_inc(s_dv, 1)
                dve.wait_ge(s_dv, chain[0])

            tt = nc.vector.tensor_tensor
            ts = nc.vector.tensor_scalar
            stt = nc.vector.scalar_tensor_tensor
            dve.wait_ge(s_exp, 2)
            after(stt(W(2), W(1), -0.5, W(0), ALU.mult, ALU.mult))
            after(stt(W(3), par[:, 2, :], 0.5, W(0), ALU.mult, ALU.mult))
            after(ts(W(4), W(2), -1.0, 1.0, ALU.mult, ALU.add))
            after(tt(W(5), W(3), W(3), ALU.mult))
            after(tt(W(6), W(4), W(4), ALU.mult))
            after(tt(W(6), W(6), W(5), ALU.add))
            after(nc.vector.reciprocal(W(6), W(6)))
            after(stt(W(0), W(0), 2.0, W(6), ALU.mult, ALU.mult))
            after(tt(W(1), par[:, 3, :], W(4), ALU.mult))
            after(tt(W(7), par[:, 4, :], W(3), ALU.mult))
            after(tt(W(1), W(1), W(7), ALU.subtract))
            after(tt(Q[:, 0, :, 0, 0], W(1), W(0), ALU.mult))
            after(tt(W(1), par[:, 3, :], W(3), ALU.mult))
            after(tt(W(7), par[:, 4, :], W(4), ALU.mult))
            after(tt(W(1), W(1), W(7), ALU.add))
            after(tt(Q[:, 1, :, 0, 0], W(1), W(0), ALU.mult))
            after(stt(W(1), W(2), 1.0, W(4), ALU.add, ALU.mult))
            after(tt(W(1), W(1), W(5), ALU.subtract))
            after(tt(pw[:, 0, 0, :], W(1), W(6), ALU.mult))
            after(stt(pw[:, 0, 1, :], W(3), 2.0, W(6), ALU.mult, ALU.mult))
            for m in range(1, POW):
                re, im = pw[:, m - 1, 0, :], pw[:, m - 1, 1, :]
                tt(W(4), re, re, ALU.mult).then_inc(s_dv, 1)
                tt(W(5), im, im, ALU.mult).then_inc(s_dv, 1)
                chain[0] += 2
                after(stt(pw[:, m, 1, :], re, 2.0, im, ALU.mult, ALU.mult))
                after(tt(pw[:, m, 0, :], W(4), W(5), ALU.subtract))
            nc.vector.memset(V[:, 0, :, 0], 1.0).then_inc(s_pow, 1)
            after(nc.vector.memset(V[:, 1, :, 0], 0.0))
            dve.wait_ge(s_pow, 1)
            for m in range(5):
                b = 2 ** m
                chain[0] = grow(tt, s_dv, chain[0], tv, V[:, 0, :, 0:b], V[:, 1, :, 0:b], V[:, 0, :, b:2 * b],
                                V[:, 1, :, b:2 * b], m, lambda v: dve.wait_ge(s_dv, v))
            nc.vector.memset(W(7)[:, 0:1], 0.0).then_inc(s_v, 1)

            def products(i, k, half):
                n, slot = group(i, k), 2 * (k % 2) + half
                dve.wait_ge(s_qs, n * 2 + 2)
                wait(dve, s_mm, n * 2 - 3 + half)
                h, src, q = of_half(i, k, half)
                for r in range(2 - half):
                    tt(T[:, slot, r], x[:, h, :].unsqueeze(2).to_broadcast(src), q(r).to_broadcast(src), ALU.mult).then_inc(s_T, 1)

            dve.wait_ge(s_inx, 16)
            for k in range(2):
                for half in range(2):
                    products(0, k, half)

            def step(i, k):
                if there(i, k + 2):
                    products(i, k + 2, 0)
                if there(i, k - 1):
                    n = group(i, k)
                    dve.wait_ge(s_tr, n)
                    wait(dve, s_hi, n - 2)
                    wait(dve, s_lo, n - 2)
                    nc.vector.transpose(X2[:, (k - 1) % 2].rearrange("p h k c -> p h (k c)"), pt[(k - 1) % 2][:]).then_inc(s_x2, 1)
                if there(i, k + 2):
                    products(i, k + 2, 1)

            pairs(dve, step)
            dve.wait_ge(s_hi, 2 * PAIRS)
            tt(of_group(g.hlo[:], PAIRS, -1), X2[:, 1].rearrange("p h k c -> p k c h"),
               of_group(g.hhi[:].bitcast(F32), PAIRS, -1), ALU.subtract).then_inc(s_lo, 1)

        @block.tensor
        def _(pe):
            def sums(i, k):
                n, slot = group(i, k), k % 2
                pe.wait_ge(s_vs, n * 4 + 4)
                wait(pe, s_y, n - 1)
                for half in range(2):
                    pe.wait_ge(s_T, n * 3 + (half + 2))
                    if half:
                        pe.wait_ge(s_Tp, n + 1)
                    for four in range(HG // 4):
                        for r in range(2):
                            for q in range(4):
                                m = 4 * four + q
                                at = half * HG + m
                                mm = nc.tensor.matmul(ps[slot][32 * q:32 * q + 32, at // 4, :], Vs[:, slot, r, at, :],
                                                      T[:, 2 * slot + half, r, m].rearrange("p a c -> p (a c)"),
                                                      start=(r == 0), stop=(r == 1), skip_group_check=True)
                    mm.then_inc(s_mm, 1)

            pe.wait_ge(s_ident, 16)
            sums(0, 0)

            def step(i, k):
                if there(i, k + 1):
                    sums(i, k + 1)
                if there(i, k):
                    n = group(i, k)
                    pe.wait_ge(s_y, n + 1)
                    wait(pe, s_x2, n - 1)
                    for m in range(4):
                        mm = nc.tensor.transpose(pt[k % 2][:, 4 * m:4 * m + 4, :].rearrange("p h b -> p (h b)"),
                                                 Y[:, k % 2, m, :], g.ident[:])
                    mm.then_inc(s_tr, 1)

            pairs(pe, step)


def split_matmuls(nc, out, whi, wlo, g, w_of, h_of):
    for k in range(KE):
        mm = None
        for n, (w, h) in enumerate(((whi, g.hhi), (whi, g.hlo), (wlo, g.hhi))):
            mm = nc.tensor.matmul(out, w_of(w, k), h_of(h, k), start=(k == 0 and n == 0),
                                  stop=(k == KE - 1 and n == 2))
    return mm


def phase_decays(nc, d, g):
    with ExitStack() as ctx:
        def sb(name, shape, dt=F32):
            return ctx.enter_context(nc.sbuf_tensor(name, shape, dt))

        def sem(name):
            return ctx.enter_context(nc.semaphore(name))

        whi, wlo = g.w2hi, g.w2lo
        par = sb("bc_par", [P, 2, NPAR])
        A = sb("dc_A", [P, HEADS])
        bias = sb("dc_bias", [HEADS, 1])
        msk = sb("msk", [P, P + 1])
        xT = sb("dc_xT", [HEADS, NT, TBW])
        t = {n: sb("dc_" + n, [P, TT, HEADS]) for n in ("xb", "ex", "un", "ln", "dt", "a", "z0")}
        packed = sb("packed", [P, NJ, 2, NT, 2, CP])
        eT = sb("eT", [HEADS, 2, NT, CP, CHUNK])
        raw = sb("bc_raw", [P, 2, 2, 3 + H])
        BC = sb("BC", [P, 2, TOK])
        pd = [ctx.enter_context(nc.psum_tensor(f"pd{i}", [P, TBW], F32)) for i in range(2)]
        ph = [ctx.enter_context(nc.psum_tensor(f"pb{i}", [P, TBW], F32)) for i in range(2)]
        pm = [ctx.enter_context(nc.psum_tensor(f"pm{i}", [P, TT // 2, HEADS], F32)) for i in range(2)]
        pe_t = [ctx.enter_context(nc.psum_tensor(f"pet{i}", [P, TBW], F32)) for i in range(2)]
        s_par = sem("bc_in_par")
        s_A = sem("dc_in_A")
        s_bias = sem("dc_in_bias")
        s_msk = sem("dc_in_msk")
        s_pd = sem("dc_pd")
        s_xT = sem("dc_xT_s")
        s_tx = sem("dc_tx")
        s_ph = sem("bc_ph")
        s_raw = sem("bc_raw_s")
        s_pad = sem("bc_pad")
        s_cv0 = sem("bc_cv0")
        s_conv = sem("bc_conv")
        s_bc = sem("bc_bc")
        s_d = sem("dc_d")
        s_x = sem("dc_x")
        s_pm = sem("dc_pm")
        s_pt = sem("dc_pt")
        s_eT = sem("dc_eT")
        s_neg = sem("dc_neg")
        s_zero = sem("dc_zero")
        s_G = sem("bc_G")
        s_Gc = sem("bc_Gc")
        s_out = sem("dc_out")
        s_stage = sem("dc_stage")
        s_acc = sem("dc_acc")
        A_READY = 7
        PACKED = A_READY + 4
        block = ctx.enter_context(nc.Block())
        wk = lambda x, i, k: x[:, E * i + P * k:E * i + P * (k + 1)]
        wd = lambda x, k: x[:, 2 * E + HEADS * k:2 * E + HEADS * (k + 1)]

        def cells(n):
            return BC[:, n % 2, TBW * (n // 2):TBW * (n // 2) + TBW].rearrange("p (c h) -> p c h", c=2)

        @block.sync
        def _(sp):
            sp.dma_start(bias[:], d["dt_bias"]).then_inc(s_bias, 16)
            sp.dma_start(A[:], d["A_log"].partition_broadcast(P)).then_inc(s_A, 16)
            sp.dma_start(par[:], d["par_bc"]).then_inc(s_par, 16)
            sp.dma_start(msk[:], d["mask"]).then_inc(s_msk, 16)
            sp.dma_start(g.stage[:, 0:2 * E + NPAR], d["w_mix"][0]).then_inc(s_stage, 16)
            sp.wait_ge(s_d, PACKED)
            sp.dma_start(d["dtz"].rearrange("j p n -> p j n"), packed[:].rearrange("p j a t h c -> p j (a t h c)")).then_inc(s_out, 16)
            sp.wait_ge(s_zero, 1)
            for h2 in range(2):
                for q in range(2):
                    sp.dma_start(d["decay"][:, q, :, h2, :], eT[h2:HEADS:2, q].rearrange("j t c l -> j t (c l)")).then_inc(s_out, 16)
            sp.wait_ge(s_out, 80)
            sp.wait_ge(s_stage, 16)

        @block.scalar
        def _(act):
            act.wait_ge(s_A, 16)
            nc.scalar.activation(A[:], A[:], ACT.Exp).then_inc(s_x, 1)
            act.wait_ge(s_bias, 16)
            for tb in range(NT):
                act.wait_ge(s_pd, tb + 1)
                nc.scalar.activation(xT[:, tb], pd[tb % 2][0:HEADS, :], ACT.Identity, bias=bias[:]).then_inc(s_xT, 1)
            act.wait_ge(s_par, 16)
            act.wait_ge(s_pad, 1)

            def take(n):
                act.wait_ge(s_ph, n + 1)
                wait(act, s_conv, 3 * n - 3)
                nc.scalar.activation(raw[:, n % 2, :, 3:], ph[n % 2][:].rearrange("p (c h) -> p c h", c=2), ACT.Copy).then_inc(s_raw, 1)
                nc.scalar.activation(cells(n), ph[n % 2][:].rearrange("p (c h) -> p c h", c=2), ACT.Identity,
                                     bias=par[:, n % 2, 4:5], scale=par[:, n % 2, 3:4]).then_inc(s_cv0, 1)

            take(0)
            take(1)
            for i in range(2):
                act.wait_ge(s_tx, 2 * i + 2)
                nc.scalar.activation(t["xb"][:, 8 * i:8 * i + 8, :], pm[i][:], ACT.Copy).then_inc(s_x, 1)
            take(2)
            act.wait_ge(s_d, 1)
            nc.scalar.activation(t["ex"][:], t["un"][:], ACT.Exp).then_inc(s_x, 1)
            take(3)
            act.wait_ge(s_d, 2)
            nc.scalar.activation(t["ln"][:], t["un"][:], ACT.Ln).then_inc(s_x, 1)
            act.wait_ge(s_x, 5)
            nc.scalar.activation(t["z0"][:], t["ln"][:], ACT.Exp, scale=-1.0).then_inc(s_x, 1)
            take(4)
            take(5)
            act.wait_ge(s_d, A_READY)
            nc.scalar.activation(t["ex"][:], t["a"][:], ACT.Exp).then_inc(s_x, 1)
            for n in range(2):
                act.wait_ge(s_pm, n + 1)
                nc.scalar.activation(t["z0"][:, 8 * n:8 * n + 8, :], pm[n][:], ACT.Exp).then_inc(s_x, 1)
            for tb in range(NT):
                act.wait_ge(s_pt, tb + 1)
                nc.scalar.activation(eT[:, :, tb], pe_t[tb % 2][0:HEADS, :].rearrange("p (c q l) -> p q c l", c=CP, q=2),
                                     ACT.Copy).then_inc(s_eT, 1)
            take(6)
            take(7)
            for n in range(2 * NT):
                act.wait_ge(s_conv, 3 * n + 3)
                nc.scalar.activation(cells(n), cells(n), ACT.Silu).then_inc(s_bc, 1)

        @block.vector
        def _(dve):
            tt = nc.vector.tensor_tensor
            stt = nc.vector.scalar_tensor_tensor
            ts = nc.vector.tensor_scalar
            nc.vector.memset(raw[:, :, :, 0:3], 0.0).then_inc(s_pad, 1)
            nc.vector.memset(g.G[:], 0.0).then_inc(s_pad, 1)
            dve.wait_ge(s_x, 1)
            ts(A[:], A[:], -1.0, None, ALU.mult).then_inc(s_neg, 1)
            dve.wait_ge(s_par, 16)
            dve.wait_ge(s_pad, 1)

            def conv(n):
                dve.wait_ge(s_raw, n + 1)
                dve.wait_ge(s_cv0, n + 1)
                for tap in range(3):
                    if tap:
                        dve.wait_ge(s_conv, 3 * n + tap)
                    stt(cells(n), raw[:, n % 2, :, tap:tap + H], par[:, n % 2, tap:tap + 1], cells(n), ALU.mult, ALU.add).then_inc(s_conv, 1)

            conv(0)
            dve.wait_ge(s_x, 3)
            stt(t["un"][:], t["xb"][:], -1.0, t["xb"][:], ALU.mult, ALU.min).then_inc(s_d, 1)
            conv(1)
            dve.wait_ge(s_x, 4)
            ts(t["un"][:], t["ex"][:], 1.0, None, ALU.add).then_inc(s_d, 1)
            dve.wait_ge(s_d, 2)
            stt(t["dt"][:], t["un"][:], -1.0, t["ex"][:], ALU.add, ALU.subtract).then_inc(s_d, 1)
            conv(2)
            conv(3)
            dve.wait_ge(s_x, 6)
            dve.wait_ge(s_d, 3)
            tt(t["dt"][:], t["dt"][:], t["z0"][:], ALU.mult).then_inc(s_d, 1)
            dve.wait_ge(s_d, 4)
            tt(t["ln"][:], t["ln"][:], t["dt"][:], ALU.subtract).then_inc(s_d, 1)
            dve.wait_ge(s_d, 5)
            stt(t["dt"][:], t["xb"][:], 0.0, t["ln"][:], ALU.max, ALU.add).then_inc(s_d, 1)
            dve.wait_ge(s_d, 6)
            dve.wait_ge(s_neg, 1)
            stt(t["a"][:], t["dt"][:], 0.0, A[:].unsqueeze(1).to_broadcast([P, TT, HEADS]), ALU.max, ALU.mult).then_inc(s_d, 1)
            conv(4)
            for h2 in range(2):
                ts(packed[:, :, 0, :, h2, :], t["dt"][:].rearrange("p (t c) (j h) -> p j t c h", t=NT, h=2)[:, :, :, :, h2],
                   0.0, None, ALU.max).then_inc(s_d, 1)
            dve.wait_ge(s_x, 9)
            dve.wait_ge(s_msk, 16)
            for h2 in range(2):
                ts(packed[:, :, 1, :, h2, :], t["z0"][:].rearrange("p (t c) (j h) -> p j t c h", t=NT, h=2)[:, :, :, :, h2],
                   msk[:, P:P + 1], None, ALU.add).then_inc(s_d, 1)
            conv(5)
            dve.wait_ge(s_eT, NT)
            nc.vector.memset(eT[:, :, :, :, 0], 0.0).then_inc(s_zero, 1)
            conv(6)
            conv(7)
            dve.wait_ge(s_pad, 2)
            for n in range(NT):
                dve.wait_ge(s_G, n + 1)
                for q in range(2):
                    rows = slice(64 * q, 64 * q + 64)
                    nc.vector.tensor_copy(g.G[rows, CP * n:CP * n + CP, q, :],
                                          ph[n % 2][:].rearrange("p (c m) -> p c m", c=CP)[rows, :, 64 * q:64 * q + 64]).then_inc(s_Gc, 1)

        @block.gpsimd
        def _(pool):
            nc.gpsimd.memset(g.acc[:], 0.0).then_inc(s_acc, 1)

        @block.tensor
        def _(pe):
            for tb in range(NT):
                wait(pe, s_xT, tb - 1)
                split_matmuls(nc, pd[tb % 2][0:HEADS, :], whi, wlo, g, wd,
                              lambda h, k: h[:, k, TBW * tb:TBW * tb + TBW]).then_inc(s_pd, 1)

            def project(n):
                i, tb = n % 2, n // 2
                wait(pe, s_cv0, n - 1)
                wait(pe, s_raw, n - 1)
                split_matmuls(nc, ph[n % 2][:], whi, wlo, g, lambda x, k: wk(x, i, k),
                              lambda h, k: h[:, k, TBW * tb:TBW * tb + TBW]).then_inc(s_ph, 1)

            project(0)
            for tb in range(NT):
                pe.wait_ge(s_xT, tb + 1)
                for c in range(CP):
                    mm = nc.tensor.transpose(pm[tb // 2][:, CP * (tb % 2) + c, :], xT[:, tb, P * c:P * c + P],
                                             g.ident[0:HEADS, 0:HEADS])
                mm.then_inc(s_tx, 1)
            for n in range(1, 2 * NT):
                project(n)
            pe.wait_ge(s_d, A_READY)
            pe.wait_ge(s_msk, 16)
            for n in range(2):
                nc.tensor.matmul(pm[n][:].rearrange("p t h -> p (t h)"), msk[:, 0:P],
                                 t["a"][:, 8 * n:8 * n + 8, :].rearrange("p t h -> p (t h)"), start=True, stop=True).then_inc(s_pm, 1)
            pe.wait_ge(s_x, 7)
            for tb in range(NT):
                wait(pe, s_eT, tb - 1)
                for c in range(CP):
                    mm = nc.tensor.transpose(pe_t[tb % 2][0:HEADS, P * c:P * c + P], t["ex"][:, CP * tb + c, :], g.ident[:])
                mm.then_inc(s_pt, 1)
            pe.wait_ge(s_cv0, 2 * NT)
            for n in range(NT):
                pe.wait_ge(s_bc, 2 * n + 2)
                wait(pe, s_Gc, 2 * n - 2)
                for c in range(CP):
                    at = slice(P * (CP * n + c), P * (CP * n + c + 1))
                    mm = nc.tensor.matmul(ph[n % 2][:, P * c:P * c + P], BC[:, 0, at], BC[:, 1, at], start=True, stop=True)
                mm.then_inc(s_G, 1)


def phase_mixer(nc, d, g):
    with ExitStack() as ctx:
        def sb(name, shape, dt=F32):
            return ctx.enter_context(nc.sbuf_tensor(name, shape, dt))

        def sem(name):
            return ctx.enter_context(nc.semaphore(name))

        def bank(name):
            return ctx.enter_context(nc.psum_tensor(name, [P, TBW], F32))

        wst = g.stage[:, 0:2 * E + NPAR]
        whi = sb("whi", [P, 2, 2 * E], F32R)
        wlo = sb("wlo", [P, 2, 2 * E], F32R)
        par = sb("par_j", [P, 2, NPAR])
        wost = sb("wost", [P, 2, E])
        wohi, wolo = [x[:, 0:2 * E].rearrange("p (m n) -> p m n", m=2) for x in (g.w2hi, g.w2lo)]
        dtz = sb("dtz_j", [P, 2, 2, NT, 2 * CP])
        raw = sb("raw", [P, 2, 3 + H])
        cv = sb("cv", [P, 2, H])
        hs = sb("hs", [P, 2, TBW])
        sg = sb("sg", [P, 2, TBW])
        Hdt = sb("Hdt", [P, 2, CP, 2, HD])
        dec = sb("dec", [P, 2, TBW])
        one = sb("one", [P, 2 * CP, CHUNK])
        Z = sb("Z", [P, 2, CP, CHUNK])
        M = sb("M", [P, 2, CP, 2, CHUNK])
        y = sb("y", [P, 2, TBW])
        ye = [sb(f"ye{i}", [P, NT, TBW], F32R) for i in range(2)]
        yo = [sb(f"yo{i}", [P, 2, TBW], F32R) for i in range(2)]
        sq = sb("sq", [P, TBW])
        ph = [bank(f"ph{i}") for i in range(2)]
        pg = [bank(f"pg{i}") for i in range(2)]
        tr, Yp = bank("tr"), bank("Yp")
        po = [bank(f"po{i}") for i in range(2)]
        s = {n: sem("mx_" + n) for n in (
            "w", "wo", "dtz", "dec0", "dec1", "eye",
            "init", "sqa0",
            "whi", "wlo", "par", "wohi", "wolo",
            "Ah", "Ag",
            "raw", "cv0", "conv",
            "hs", "sg",
            "tr", "Hdt",
            "one", "Z", "M",
            "Y", "y", "yhi", "ylo",
            "sq", "sqa",
            "po", "acc")}
        block = ctx.enter_context(nc.Block())
        flat = lambda x: x.rearrange("p c h -> p (c h)")

        def y_of(k, part):
            return ye[part][:, k % NT, :] if (k // NT) % 2 == 0 else yo[part][:, k % 2, :]

        def y_free(i, k):
            tb = k % NT
            pair = i if k >= 0 else i - 1
            return count(pair, 0, 2, 4 * tb - (12 if (k // NT) % 2 == 0 else 4))

        @block.sync
        def _(sp):
            def load_w(j):
                sp.dma_start(wst, d["w_mix"][bass.ds(j, 1)].rearrange("a p n -> (a p) n")).then_inc(s["w"], 16)

            def load_dtz(j, slot):
                sp.dma_start(dtz[:, slot].rearrange("p a t n -> p (a t n)"),
                             d["dtz"][bass.ds(j, 1)].rearrange("a p n -> (a p) n")).then_inc(s["dtz"], 16)

            def load_wo(pair):
                sp.dma_start(wost[:], d["w_out"][bass.ds(pair, 1)].rearrange("a m p n -> p (a m) n")).then_inc(s["wo"], 16)

            def load_dec(j, tb, slot):
                for q in range(2):
                    sp.dma_start(dec[64 * q:64 * q + 64, slot, :],
                                 d["decay"][bass.ds(j, 1), q, tb].rearrange("a h n -> a (h n)").to_broadcast([64, TBW])).then_inc(s[f"dec{slot}"], 16)

            sp.dma_start(one[:, 0, :], d["eye64"]).then_inc(s["eye"], 16)
            load_dtz(0, 0)
            load_dec(0, 0, 0)
            load_wo(0)

            def step(i, k):
                done, j, next_j, before, landed, pair = values(sp, count(i, k), i * 2 + (k + 1) // NT, i * 2 + (k // NT + 1),
                                                               count(i, k - 1), count(i, k - 1, 4, 16), i + 1)
                if alive(i, k + 1, UNITS):
                    wait(sp, s["Z"], done)
                    load_dec(j, (k + 1) % NT, (k + 1) % 2)
                if k % NT == 0 and alive(i, k + NT, UNITS):
                    sp.wait_ge(s["whi"], next_j)
                    sp.wait_ge(s["wlo"], next_j)
                    sp.wait_ge(s["par"], next_j)
                    load_w(next_j)
                if k % NT == 1 and alive(i, k + NT, UNITS):
                    wait(sp, s["dtz"], landed)
                    wait(sp, s["Hdt"], before)
                    wait(sp, s["Z"], before)
                    load_dtz(next_j, (k // NT + 1) % 2)
                if k == 4 and alive(i, BODY, UNITS):
                    both = values(sp, i * 2 + 2)[0]
                    sp.wait_ge(s["wohi"], both)
                    sp.wait_ge(s["wolo"], both)
                    load_wo(pair)

            steps(sp, step, UNITS, 0)

        @block.scalar
        def _(act):
            def split_w(j, slot):
                wait(act, s["w"], j * 16)
                nc.scalar.activation(whi[:, slot], wst[:, 0:2 * E], ACT.Copy).then_inc(s["whi"], 1)
                nc.scalar.activation(par[:, slot], wst[:, 2 * E:], ACT.Copy).then_inc(s["par"], 1)

            split_w(0, 0)

            def step(i, k):
                u = k - 2
                if alive(i, u, UNITS):
                    wait(act, s["y"], count(i, u, 2, 2))
                    wait(act, s["po"], y_free(i, u))
                    nc.scalar.activation(y_of(u, 0), y[:, u % 2, :], ACT.Copy).then_inc(s["yhi"], 1)
                    wait(act, s["sqa"], count(i, u))
                    nc.scalar.activation(sq[:], y[:, u % 2, :], ACT.Square).then_inc(s["sq"], 1)
                if not alive(i, k, UNITS):
                    return
                wait(act, s["Ah"], count(i, k, 1, 1))
                wait(act, s["conv"], count(i, k, 3))
                if isinstance(i, int) and i == 0 and k == 0:
                    act.wait_ge(s["init"], 2)
                nc.scalar.activation(raw[:, :, 3:], ph[k % 2][:].rearrange("p (c h) -> p c h", c=2), ACT.Copy).then_inc(s["raw"], 1)
                wait(act, s["hs"], count(i, k))
                wait(act, s["par"], i * 2 + (k // NT + 1))
                nc.scalar.activation(flat(cv[:]), ph[k % 2][:], ACT.Identity, bias=par[:, k // NT, 4:5],
                                     scale=par[:, k // NT, 3:4]).then_inc(s["cv0"], 1)
                if k % NT == 1 and alive(i, k + NT, UNITS):
                    wait(act, s["Ag"], count(i, k - 1))
                    wait(act, s["y"], count(i, k - 1, 2))
                    split_w(i * 2 + (k // NT + 1), (k // NT + 1) % 2)
                if k in (2, 3):
                    act.wait_ge(s["wo"], i * 16 + 16)
                    wait(act, s["po"], count(i, 0, 2))
                    nc.scalar.activation(wohi[:, k - 2], wost[:, k - 2], ACT.Copy, scale=par[:, k - 2, 5:6]).then_inc(s["wohi"], 1)
                wait(act, s["conv"], count(i, k, 3, 3))
                wait(act, s["tr"], count(i, k, 1, -1))
                wait(act, s["y"], count(i, k, 2, -2))
                nc.scalar.activation(hs[:, k % 2, :], flat(cv[:]), ACT.Silu).then_inc(s["hs"], 1)
                wait(act, s["Ag"], count(i, k, 1, 1))
                nc.scalar.activation(sg[:, k % 2, :], pg[k % 2][:], ACT.Silu).then_inc(s["sg"], 1)

            steps(act, step, UNITS, 2)

        @block.vector
        def _(dve):
            tt = nc.vector.tensor_tensor
            stt = nc.vector.scalar_tensor_tensor
            nc.vector.memset(raw[:, :, 0:3], 0.0).then_inc(s["init"], 1)
            dve.wait_ge(s["whi"], 1)
            tt(wlo[:, 0], wst[:, 0:2 * E], whi[:, 0].bitcast(F32), ALU.subtract).then_inc(s["wlo"], 1)
            dve.wait_ge(s["eye"], 16)
            nc.vector.tensor_copy(one[:, 1:, :], one[:, 0:1, :].to_broadcast([P, 2 * CP - 1, CHUNK])).then_inc(s["init"], 1)
            dve.wait_ge(s["init"], 2)

            def step(i, k):
                v = k - 1
                if alive(i, v, UNITS):
                    jv = v // NT
                    dve.wait_ge(s["dtz"], (i * 32 + (16 * jv + 16)))
                    wait(dve, s["Z"], count(i, v))
                    nc.vector.tensor_copy(one[:, :, 0], dtz[:, jv % 2, 1, v % NT, :]).then_inc(s["one"], 1)
                    dve.wait_ge(s[f"dec{v % 2}"], count(i, v - v % 2, 16, 32))
                    wait(dve, s["M"], count(i, v, 2))
                    dve.wait_ge(s["one"], count(i, v, 1, 1))
                    nc.vector.tensor_tensor_scan(Z[:].rearrange("p h c l -> p (h c l)"), dec[:, v % 2, :],
                                                 one[:].rearrange("p n l -> p (n l)"), 0.0, ALU.mult, ALU.add).then_inc(s["Z"], 1)
                    dve.wait_ge(s["tr"], count(i, v, 1, 1))
                    wait(dve, s["Y"], count(i, v, 1, -1))
                    tt(Hdt[:, v % 2], tr[:].rearrange("p (c h d) -> p c h d", c=CP, h=2),
                       dtz[:, jv % 2, 0, v % NT, :].rearrange("p (h c) -> p c h", h=2).unsqueeze(3).to_broadcast([P, CP, 2, HD]),
                       ALU.mult).then_inc(s["Hdt"], 1)
                u = k - 2
                if alive(i, u, UNITS):
                    dve.wait_ge(s["yhi"], count(i, u, 1, 1))
                    wait(dve, s["po"], y_free(i, u))
                    tt(y_of(u, 1), y[:, u % 2, :], y_of(u, 0).bitcast(F32), ALU.subtract).then_inc(s["ylo"], 1)
                if alive(i, k, UNITS):
                    dve.wait_ge(s["raw"], count(i, k, 1, 1))
                    dve.wait_ge(s["cv0"], count(i, k, 1, 1))
                    for tap in range(3):
                        if tap:
                            dve.wait_ge(s["conv"], count(i, k, 3, tap))
                        stt(cv[:], raw[:, :, tap:tap + H], par[:, k // NT, tap:tap + 1], cv[:], ALU.mult, ALU.add).then_inc(s["conv"], 1)
                if k in (2, 3) and alive(i, k, UNITS):
                    dve.wait_ge(s["wohi"], i * 2 + (k - 1))
                    wait(dve, s["po"], count(i, 0, 2))
                    stt(wolo[:, k - 2], wost[:, k - 2], par[:, k - 2, 5:6], wohi[:, k - 2].bitcast(F32),
                        ALU.mult, ALU.subtract).then_inc(s["wolo"], 1)
                if alive(i, v, UNITS):
                    dve.wait_ge(s["Y"], count(i, v, 1, 1))
                    wait(dve, s["yhi"], count(i, v, 1, -1))
                    wait(dve, s["sq"], count(i, v, 1, -1))
                    wait(dve, s["ylo"], count(i, v, 1, -1))
                    stt(y[:, v % 2, :], hs[:, v % 2, :], par[:, (v // NT) % 2, 6:7], Yp[:], ALU.mult, ALU.add).then_inc(s["y"], 1)
                    dve.wait_ge(s["sg"], count(i, v, 1, 1))
                    dve.wait_ge(s["y"], count(i, v, 2, 1))
                    tt(y[:, v % 2, :], y[:, v % 2, :], sg[:, v % 2, :], ALU.mult).then_inc(s["y"], 1)
                if alive(i, u, UNITS) and (u // NT) % 2 == 1:
                    pair = i if u >= 0 else i - 1
                    for m in range(CP):
                        n = 4 * (u % NT) + m
                        dve.wait_ge(s["po"], count(pair, 0, 2, n + 1))
                        wait(dve, s["acc"], count(pair, 0, 2, n - 7))
                        tt(g.acc[:, n, :], g.acc[:, n, :], po[n % 2][:], ALU.add).then_inc(s["acc"], 1)

            steps(dve, step, UNITS, 2)

        @block.gpsimd
        def _(pool):
            tt = nc.gpsimd.tensor_tensor

            def split_w(j, slot):
                pool.wait_ge(s["whi"], j + 1)
                tt(wlo[:, slot], wst[:, 0:2 * E], whi[:, slot].bitcast(F32), ALU.subtract).then_inc(s["wlo"], 1)

            nc.gpsimd.memset(g.sqa[:], 0.0).then_inc(s["sqa0"], 1)
            pool.wait_ge(s["sqa0"], 1)
            pool.wait_ge(s["init"], 2)

            def step(i, k):
                v = k - 1
                if alive(i, v, UNITS):
                    pool.wait_ge(s["Z"], count(i, v, 1, 1))
                    wait(pool, s["Y"], count(i, v))
                    for q in range(2):
                        tt(M[:, :, :, q, :], Z[:],
                           g.G[:, CP * (v % NT):CP * (v % NT) + CP, q, :].unsqueeze(1).to_broadcast([P, 2, CP, CHUNK]),
                           ALU.mult).then_inc(s["M"], 1)
                u = k - 2
                if alive(i, u, UNITS):
                    pool.wait_ge(s["sq"], count(i, u, 1, 1))
                    wait(pool, s["sqa"], count(i, u, 1, -3))
                    tt(g.sqa[:, u % NT, :], g.sqa[:, u % NT, :], sq[:], ALU.add).then_inc(s["sqa"], 1)
                if k % NT == 1 and alive(i, k + NT, UNITS) and alive(i, k, UNITS):
                    split_w(i * 2 + (k // NT + 1), (k // NT + 1) % 2)

            steps(pool, step, UNITS, 2)

        @block.tensor
        def _(pe):
            def project(i, k, part, out):
                tb, slot = k % NT, k // NT
                return split_matmuls(nc, out, whi, wlo, g, lambda x, c: x[:, slot, E * part + P * c:E * part + P * (c + 1)],
                                     lambda h, c: h[:, c, TBW * tb:TBW * tb + TBW])

            def step(i, k):
                if alive(i, k, UNITS):
                    if k % NT == 0:
                        pe.wait_ge(s["whi"], i * 2 + (k // NT + 1))
                        pe.wait_ge(s["wlo"], i * 2 + (k // NT + 1))
                    wait(pe, s["raw"], count(i, k, 1, -1))
                    wait(pe, s["cv0"], count(i, k, 1, -1))
                    project(i, k, 0, ph[k % 2][:]).then_inc(s["Ah"], 1)
                v = k - 1
                if alive(i, v, UNITS):
                    pe.wait_ge(s["hs"], count(i, v, 1, 1))
                    wait(pe, s["Hdt"], count(i, v))
                    for c in range(CP):
                        mm = nc.tensor.transpose(tr[:, P * c:P * c + P], hs[:, v % 2, P * c:P * c + P], g.ident[:])
                    mm.then_inc(s["tr"], 1)
                if alive(i, k, UNITS):
                    wait(pe, s["sg"], count(i, k, 1, -1))
                    project(i, k, 1, pg[k % 2][:]).then_inc(s["Ag"], 1)
                if alive(i, v, UNITS):
                    pe.wait_ge(s["Hdt"], count(i, v, 1, 1))
                    pe.wait_ge(s["M"], count(i, v, 2, 2))
                    wait(pe, s["y"], count(i, v, 2, -1))
                    for c in range(CP):
                        for h in range(2):
                            mm = nc.tensor.matmul(Yp[64 * h:64 * h + 64, P * c:P * c + P], Hdt[:, v % 2, c, h, :],
                                                  M[:, h, c].rearrange("p q l -> p (q l)"), start=True, stop=True)
                    mm.then_inc(s["Y"], 1)
                u = k - 2
                if alive(i, u, UNITS) and (u // NT) % 2 == 1:
                    pair = i if u >= 0 else i - 1
                    pe.wait_ge(s["yhi"], count(i, u, 1, 1))
                    pe.wait_ge(s["ylo"], count(i, u, 1, 1))
                    pe.wait_ge(s["wohi"], pair * 2 + 2)
                    pe.wait_ge(s["wolo"], pair * 2 + 2)
                    for m in range(CP):
                        n = 4 * (u % NT) + m
                        wait(pe, s["acc"], count(pair, 0, 2, n - 1))
                        mm = None
                        for tile in range(2):
                            kk = u - NT + NT * tile
                            cols = slice(P * m, P * m + P)
                            for a, b in ((0, wohi), (1, wohi), (0, wolo)):
                                mm = nc.tensor.matmul(po[n % 2][:], y_of(kk, a)[:, cols], b[:, tile, :],
                                                      start=(tile == 0 and a == 0 and b is wohi), stop=(tile == 1 and b is wolo))
                        mm.then_inc(s["po"], 1)

            steps(pe, step, UNITS, 2)


def inverse_root(eng, after, out, var, root, inv):
    after(eng.reciprocal(inv, root))
    after(eng.tensor_tensor(inv, inv, var, ALU.mult))
    after(eng.tensor_tensor(inv, inv, root, ALU.add))
    after(eng.tensor_scalar(inv, inv, 0.5, None, ALU.mult))
    after(eng.reciprocal(out, inv))


def phase_norm(nc, d, g):
    with ExitStack() as ctx:
        def sb(name, shape, dt=F32):
            return ctx.enter_context(nc.sbuf_tensor(name, shape, dt))

        def sem(name):
            return ctx.enter_context(nc.semaphore(name))

        ones = sb("nm_ones", [P, 2])
        hsum = sb("nm_hsum", [P, 8, KE, P])
        rvar, rroot, rinv, rrs = [sb("nm_r" + n, [P, TT]) for n in ("var", "root", "inv", "rs")]
        var, root, inv, rs, mrs = [sb("nm_" + n, [P, TT]) for n in ("var", "root", "inv", "rs", "mrs")]
        turned = sb("nm_turned", [P, 2, KE, P])
        st = sb("nm_st", [P, TT, 6])
        mv = sb("nm_mv", [P, TT, 2])
        pv = ctx.enter_context(nc.psum_tensor("nm_pv", [P, TT, 2], F32))
        ph = [ctx.enter_context(nc.psum_tensor(f"nm_h{i}", [P, E], F32)) for i in range(3)]
        pt = [ctx.enter_context(nc.psum_tensor(f"nm_t{i}", [P, KE, P], F32)) for i in range(4)]
        s_one = sem("nm_one")
        s_pv = sem("nm_pv_s")
        s_rms, s_rroot = sem("nm_rms"), sem("nm_rroot_s")
        s_sum, s_h, s_x = sem("nm_sum"), sem("nm_h"), sem("nm_x")
        s_st, s_mv = sem("nm_st_s"), sem("nm_mv_s")
        s_var, s_root, s_rs = sem("nm_var_s"), sem("nm_root_s"), sem("nm_rs_s")
        s_c = sem("nm_c")
        s_n, s_t = sem("nm_n"), sem("nm_t")
        s_hi, s_loe, s_loo, s_turned = sem("nm_hi"), sem("nm_lo_even"), sem("nm_lo_odd"), sem("nm_turned_s")
        s_stage, s_whi, s_wlo = sem("nm_stage"), sem("nm_whi"), sem("nm_wlo")
        block = ctx.enter_context(nc.Block())
        tile = lambda x, n: x[:, :, P * n:P * n + P]
        groups = TT // 4

        def ahead(grp):
            return range(4 * grp + 3 if grp else 0, min(4 * grp + 7, TT))

        @block.sync
        def _(sp):
            sp.dma_start(g.stage[:, 0:2 * E], d["w_ffn"][0]).then_inc(s_stage, 16)
            sp.wait_ge(s_stage, 16)

        @block.gpsimd
        def _(pool):
            def sums(grp):
                for n in range(4 * grp + 7 if grp else 0, min(4 * grp + 11, TT)):
                    wait(pool, s_h, n - 7)
                    nc.gpsimd.tensor_tensor(hsum[:, n % 8], tile(g.hhi, n).bitcast(F32), tile(g.hlo, n).bitcast(F32),
                                            ALU.add).then_inc(s_sum, 1)

            for grp in range(groups):
                sums(grp)
                for n in range(4 * grp + 1, 4 * grp + 4, 2):
                    pool.wait_ge(s_hi, n + 1)
                    pool.wait_ge(s_turned, (n + 1) // 2)
                    nc.gpsimd.tensor_tensor(tile(g.hlo, n), turned[:, n // 2 % 2], tile(g.hhi, n).bitcast(F32),
                                            ALU.subtract).then_inc(s_loo, 1)

        @block.tensor
        def _(pe):
            pe.wait_ge(s_one, 1)
            for n in range(TT):
                mm = nc.tensor.matmul(pv[:, n, :], g.sqa[:].rearrange("p t n -> p (t n)")[:, P * n:P * n + P], ones[:],
                                      start=True, stop=True)
            mm.then_inc(s_pv, 1)

            def old(grp):
                for n in ahead(grp):
                    pe.wait_ge(s_sum, n + 1)
                    wait(pe, s_x, n - 2)
                    for k in range(KE):
                        mm = nc.tensor.transpose(ph[n % 3][:, P * k:P * k + P], hsum[:, n % 8, k, :], g.ident[:])
                    mm.then_inc(s_h, 1)

            for grp in range(groups):
                old(grp)
                for n in range(4 * grp, 4 * grp + 4):
                    pe.wait_ge(s_n, n + 1)
                    wait(pe, s_hi, n - 3)
                    wait(pe, s_loe, (n - 4) // 2 + 1)
                    wait(pe, s_turned, (n - 3) // 2)
                    for k in range(KE):
                        mm = nc.tensor.transpose(pt[n % 4][:, k, :], g.acc[:, n, P * k:P * k + P], g.ident[:])
                    mm.then_inc(s_t, 1)

        @block.scalar
        def _(act):
            act.wait_ge(s_stage, 16)
            nc.scalar.activation(g.fhi[:, 0], g.stage[:, 0:2 * E], ACT.Copy).then_inc(s_whi, 1)
            act.wait_ge(s_rms, 1)
            nc.scalar.activation(rroot[:], rvar[:], ACT.Sqrt).then_inc(s_rroot, 1)

            for grp in range(groups):
                at = slice(4 * grp, 4 * grp + 4)
                act.wait_ge(s_var, grp + 1)
                nc.scalar.activation(root[:, at], var[:, at], ACT.Sqrt).then_inc(s_root, 1)
                act.wait_ge(s_rs, grp + 1)
                for n in range(4 * grp, 4 * grp + 4):
                    nc.scalar.activation(g.acc[:, n, :], g.acc[:, n, :], ACT.Identity, bias=mrs[:, n:n + 1],
                                         scale=rs[:, n:n + 1]).then_inc(s_n, 1)
                for n in range(4 * grp, 4 * grp + 4):
                    act.wait_ge(s_t, n + 1)
                    nc.scalar.activation(tile(g.hhi, n), pt[n % 4][:], ACT.Copy).then_inc(s_hi, 1)
                    if n % 2:
                        wait(act, s_loo, n // 2 - 1)
                        nc.scalar.activation(turned[:, n // 2 % 2], pt[n % 4][:], ACT.Copy).then_inc(s_turned, 1)

        @block.vector
        def _(dve):
            stt = nc.vector.scalar_tensor_tensor
            ts = nc.vector.tensor_scalar
            chain = [0]

            def after(ins):
                chain[0] += 1
                ins.then_inc(s_c, 1)
                dve.wait_ge(s_c, chain[0])

            nc.vector.memset(ones[:], 1.0).then_inc(s_one, 1)
            dve.wait_ge(s_whi, 1)
            nc.vector.tensor_tensor(g.flo[:, 0], g.stage[:, 0:2 * E], g.fhi[:, 0].bitcast(F32), ALU.subtract).then_inc(s_wlo, 1)
            dve.wait_ge(s_pv, 1)
            ts(rvar[:], pv[:, :, 0], 1.0 / INTER, EPS, ALU.mult, ALU.add).then_inc(s_rms, 1)
            dve.wait_ge(s_rms, 1)
            dve.wait_ge(s_rroot, 1)
            inverse_root(nc.vector, after, rrs[:], rvar[:], rroot[:], rinv[:])

            def low(grp):
                for n in range(4 * grp, 4 * grp + 4, 2):
                    dve.wait_ge(s_hi, n + 1)
                    nc.vector.tensor_tensor(tile(g.hlo, n), pt[n % 4][:], tile(g.hhi, n).bitcast(F32),
                                            ALU.subtract).then_inc(s_loe, 1)

            for grp in range(groups):
                at = slice(4 * grp, 4 * grp + 4)

                def stats(n):
                    dve.wait_ge(s_x, n + 1)
                    nc.vector.bn_stats(st[:, n, :], g.acc[:, n, :]).then_inc(s_st, 1)

                for n in range(4 * grp, 4 * grp + 4):
                    dve.wait_ge(s_h, n + 1)
                    stt(g.acc[:, n, :], g.acc[:, n, :], rrs[:, n:n + 1], ph[n % 3][:], ALU.mult, ALU.add).then_inc(s_x, 1)
                    if n % 4:
                        stats(n - 1)
                stats(4 * grp + 3)
                for n in range(4 * grp, 4 * grp + 4):
                    dve.wait_ge(s_st, n + 1)
                    nc.vector.bn_aggr(mv[:, n, :], st[:, n, :]).then_inc(s_mv, 1)
                dve.wait_ge(s_mv, 4 * grp + 4)
                ts(var[:, at], mv[:, at, 1], EPS, None, ALU.add).then_inc(s_var, 1)
                dve.wait_ge(s_var, grp + 1)
                dve.wait_ge(s_root, grp + 1)
                inverse_root(nc.vector, after, rs[:, at], var[:, at], root[:, at], inv[:, at])
                stt(mrs[:, at], mv[:, at, 0], -1.0, rs[:, at], ALU.mult, ALU.mult).then_inc(s_rs, 1)
                if grp:
                    low(grp - 1)
            low(groups - 1)


def phase_ffn(nc, d, g):
    with ExitStack() as ctx:
        def sb(name, shape, dt=F32):
            return ctx.enter_context(nc.sbuf_tensor(name, shape, dt))

        def sem(name):
            return ctx.enter_context(nc.semaphore(name))

        def bank(name):
            return ctx.enter_context(nc.psum_tensor(name, [P, TBW], F32))

        wst = g.stage[:, 0:2 * E]
        whi, wlo = g.fhi, g.flo
        wost = sb("f_wost", [P, 2, E])
        wohi, wolo = [x[:, 0:2 * E].rearrange("p (m n) -> p m n", m=2) for x in (g.w2hi, g.w2lo)]
        sg = sb("f_sg", [P, 2, TBW])
        y = sb("f_y", [P, 2, TBW])
        ye = [sb(f"f_ye{i}", [P, NT, TBW], F32R) for i in range(2)]
        yo = [sb(f"f_yo{i}", [P, 2, TBW], F32R) for i in range(2)]
        pg = [bank(f"f_pg{i}") for i in range(2)]
        pu = [bank(f"f_pu{i}") for i in range(2)]
        po = [bank(f"f_po{i}") for i in range(4)]
        s = {n: sem("ff_" + n) for n in (
            "w", "wo", "whi", "wlo", "wohi", "wolo",
            "Ag", "Au",
            "sg", "y", "yhi", "ylo",
            "po", "acc")}
        block = ctx.enter_context(nc.Block())

        def y_of(k, part):
            return ye[part][:, k % NT, :] if (k // NT) % 2 == 0 else yo[part][:, k % 2, :]

        def y_free(i, k):
            pair = i if k >= 0 else i - 1
            return count(pair, 0, 2, 4 * (k % NT) - (12 if (k // NT) % 2 == 0 else 4))

        @block.sync
        def _(sp):
            def load_w(m):
                sp.dma_start(wst, d["w_ffn"][bass.ds(m, 1)].rearrange("a p n -> (a p) n")).then_inc(s["w"], 16)

            def load_wo(pair):
                sp.dma_start(wost[:], d["w_down"][bass.ds(pair, 1)].rearrange("a m p n -> p (a m) n")).then_inc(s["wo"], 16)

            load_wo(0)

            def step(i, k):
                next_m, m, both, pair = values(sp, i * 2 + (k // NT + 1), i * 2 + k // NT, i * 2 + 2, i + 1)
                if k % NT == 0 and alive(i, k + NT, FUNITS):
                    wait(sp, s["whi"], m)
                    wait(sp, s["wlo"], m)
                    load_w(next_m)
                if k == 4 and alive(i, BODY, FUNITS):
                    sp.wait_ge(s["wohi"], both)
                    sp.wait_ge(s["wolo"], both)
                    load_wo(pair)

            steps(sp, step, FUNITS, 0)

        @block.scalar
        def _(act):
            def split_w(m, slot):
                act.wait_ge(s["w"], m * 16)
                nc.scalar.activation(whi[:, slot], wst, ACT.Copy).then_inc(s["whi"], 1)

            def step(i, k):
                u = k - 1
                if alive(i, u, FUNITS):
                    act.wait_ge(s["y"], count(i, u, 1, 1))
                    wait(act, s["po"], y_free(i, u))
                    nc.scalar.activation(y_of(u, 0), y[:, u % 2, :], ACT.Copy).then_inc(s["yhi"], 1)
                if not alive(i, k, FUNITS):
                    return
                if k % NT == 1 and alive(i, k + NT, FUNITS):
                    wait(act, s["Au"], count(i, k - 1))
                    split_w(i * 2 + (k // NT + 1), (k // NT + 1) % 2)
                if k in (2, 3):
                    act.wait_ge(s["wo"], i * 16 + 16)
                    wait(act, s["po"], count(i, 0, 2))
                    nc.scalar.activation(wohi[:, k - 2], wost[:, k - 2], ACT.Copy).then_inc(s["wohi"], 1)
                act.wait_ge(s["Ag"], count(i, k, 1, 1))
                wait(act, s["y"], count(i, k, 1, -1))
                nc.scalar.activation(sg[:, k % 2, :], pg[k % 2][:], ACT.Silu).then_inc(s["sg"], 1)

            steps(act, step, FUNITS, 2)

        @block.vector
        def _(dve):
            tt = nc.vector.tensor_tensor

            def step(i, k):
                v = k - 1
                if alive(i, v, FUNITS):
                    dve.wait_ge(s["yhi"], count(i, v, 1, 1))
                    wait(dve, s["po"], y_free(i, v))
                    tt(y_of(v, 1), y[:, v % 2, :], y_of(v, 0).bitcast(F32), ALU.subtract).then_inc(s["ylo"], 1)
                if k in (2, 3) and alive(i, k, FUNITS):
                    dve.wait_ge(s["wohi"], i * 2 + (k - 1))
                    wait(dve, s["po"], count(i, 0, 2))
                    tt(wolo[:, k - 2], wost[:, k - 2], wohi[:, k - 2].bitcast(F32), ALU.subtract).then_inc(s["wolo"], 1)
                if alive(i, k, FUNITS):
                    dve.wait_ge(s["Au"], count(i, k, 1, 1))
                    dve.wait_ge(s["sg"], count(i, k, 1, 1))
                    wait(dve, s["yhi"], count(i, k, 1, -1))
                    wait(dve, s["ylo"], count(i, k, 1, -1))
                    tt(y[:, k % 2, :], sg[:, k % 2, :], pu[k % 2][:], ALU.mult).then_inc(s["y"], 1)
                if alive(i, v, FUNITS) and (v // NT) % 2 == 1:
                    pair = i if v >= 0 else i - 1
                    for m in range(CP):
                        n = 4 * (v % NT) + m
                        dve.wait_ge(s["po"], count(pair, 0, 2, n + 1))
                        wait(dve, s["acc"], count(pair, 0, 2, n - 7))
                        tt(g.acc[:, n, :], g.acc[:, n, :], po[n % 4][:], ALU.add).then_inc(s["acc"], 1)

            steps(dve, step, FUNITS, 1)

        @block.gpsimd
        def _(pool):
            def split_w(m, slot):
                pool.wait_ge(s["whi"], m)
                nc.gpsimd.tensor_tensor(wlo[:, slot], wst, whi[:, slot].bitcast(F32), ALU.subtract).then_inc(s["wlo"], 1)

            def step(i, k):
                if k % NT == 1 and alive(i, k + NT, FUNITS) and alive(i, k, FUNITS):
                    split_w(i * 2 + (k // NT + 1), (k // NT + 1) % 2)

            steps(pool, step, FUNITS, 0)

        @block.tensor
        def _(pe):
            def project(i, k, part, out):
                tb, slot = k % NT, k // NT
                return split_matmuls(nc, out, whi, wlo, g, lambda x, c: x[:, slot, E * part + P * c:E * part + P * (c + 1)],
                                     lambda h, c: h[:, c, TBW * tb:TBW * tb + TBW])

            def step(i, k):
                if alive(i, k, FUNITS):
                    if k % NT == 0:
                        wait(pe, s["whi"], i * 2 + k // NT)
                        wait(pe, s["wlo"], i * 2 + k // NT)
                    wait(pe, s["sg"], count(i, k, 1, -1))
                    project(i, k, 0, pg[k % 2][:]).then_inc(s["Ag"], 1)
                    wait(pe, s["y"], count(i, k, 1, -1))
                    project(i, k, 1, pu[k % 2][:]).then_inc(s["Au"], 1)
                u = k - 1
                if alive(i, u, FUNITS) and (u // NT) % 2 == 1:
                    pair = i if u >= 0 else i - 1
                    pe.wait_ge(s["yhi"], count(i, u, 1, 1))
                    pe.wait_ge(s["ylo"], count(i, u, 1, 1))
                    pe.wait_ge(s["wohi"], pair * 2 + 2)
                    pe.wait_ge(s["wolo"], pair * 2 + 2)
                    for m in range(CP):
                        n = 4 * (u % NT) + m
                        wait(pe, s["acc"], count(pair, 0, 2, n - 3))
                        mm = None
                        for tile in range(2):
                            kk = u - NT + NT * tile
                            cols = slice(P * m, P * m + P)
                            for a, b in ((0, wohi), (1, wohi), (0, wolo)):
                                mm = nc.tensor.matmul(po[n % 4][:], y_of(kk, a)[:, cols], b[:, tile, :],
                                                      start=(tile == 0 and a == 0 and b is wohi), stop=(tile == 1 and b is wolo))
                        mm.then_inc(s["po"], 1)

            steps(pe, step, FUNITS, 1)


def phase_out(nc, d, g, out):
    with ExitStack() as ctx:
        def sb(name, shape, dt=F32):
            return ctx.enter_context(nc.sbuf_tensor(name, shape, dt))

        def sem(name):
            return ctx.enter_context(nc.semaphore(name))

        var, root, inv, rs, mrs = [sb("o_" + n, [P, TT]) for n in ("var", "root", "inv", "rs", "mrs")]
        st = sb("o_st", [P, TT, 6])
        mv = sb("o_mv", [P, TT, 2])
        s_st, s_mv, s_var, s_root, s_rs, s_c, s_n, s_out = [
            sem("o_" + n) for n in ("st_s", "mv_s", "var_s", "root_s", "rs_s", "c", "n", "out")]
        block = ctx.enter_context(nc.Block())
        groups = TT // 4
        LAST_ON_VECTOR = (TT - 2, TT - 1)

        @block.vector
        def _(dve):
            chain = [0]

            def after(ins):
                chain[0] += 1
                ins.then_inc(s_c, 1)
                dve.wait_ge(s_c, chain[0])

            def stats(grp):
                at = slice(4 * grp, 4 * grp + 4)
                for n in range(4 * grp, 4 * grp + 4):
                    nc.vector.bn_stats(st[:, n, :], g.acc[:, n, :]).then_inc(s_st, 1)
                for n in range(4 * grp, 4 * grp + 4):
                    dve.wait_ge(s_st, n + 1)
                    nc.vector.bn_aggr(mv[:, n, :], st[:, n, :]).then_inc(s_mv, 1)
                dve.wait_ge(s_mv, 4 * grp + 4)
                nc.vector.tensor_scalar(var[:, at], mv[:, at, 1], EPS, None, ALU.add).then_inc(s_var, 1)

            stats(0)
            for grp in range(groups):
                at = slice(4 * grp, 4 * grp + 4)
                dve.wait_ge(s_var, grp + 1)
                dve.wait_ge(s_root, grp + 1)
                inverse_root(nc.vector, after, rs[:, at], var[:, at], root[:, at], inv[:, at])
                nc.vector.scalar_tensor_tensor(mrs[:, at], mv[:, at, 0], -1.0, rs[:, at], ALU.mult, ALU.mult).then_inc(s_rs, 1)
                if grp + 1 < groups:
                    stats(grp + 1)
            dve.wait_ge(s_rs, groups)
            for n in LAST_ON_VECTOR:
                nc.vector.tensor_scalar(g.acc[:, n, :], g.acc[:, n, :], rs[:, n:n + 1], mrs[:, n:n + 1],
                                        ALU.mult, ALU.add).then_inc(s_n, 1)

        @block.scalar
        def _(act):
            for grp in range(groups):
                at = slice(4 * grp, 4 * grp + 4)
                act.wait_ge(s_var, grp + 1)
                nc.scalar.activation(root[:, at], var[:, at], ACT.Sqrt).then_inc(s_root, 1)
                act.wait_ge(s_rs, grp + 1)
                for n in [n for n in range(4 * grp, 4 * grp + 4) if n not in LAST_ON_VECTOR]:
                    nc.scalar.activation(g.acc[:, n, :], g.acc[:, n, :], ACT.Identity, bias=mrs[:, n:n + 1],
                                         scale=rs[:, n:n + 1]).then_inc(s_n, 1)

        @block.sync
        def _(sp):
            o = out.rearrange("b (t p) e -> p (b t) e", p=P)
            for n in range(0, TT, 4):
                sp.wait_ge(s_n, n + 4)
                sp.dma_start(o[:, n:n + 4, :], g.acc[:, n:n + 4, :]).then_inc(s_out, 16)
            sp.wait_ge(s_out, 16 * (TT // 4))


def build(nc, d, out):
    with ExitStack() as ctx:
        g = Shared()

        def shared(stack, name, shape, dt=F32):
            return stack.enter_context(nc.sbuf_tensor(name, shape, dt))

        g.hhi = shared(ctx, "hhi", [P, KE, TOK], F32R)
        g.hlo = shared(ctx, "hlo", [P, KE, TOK], F32R)
        g.ident = shared(ctx, "ident", [P, P])
        g.stage = shared(ctx, "stage", [P, BCW])
        g.w2hi = shared(ctx, "w2hi", [P, BCW], F32R)
        g.w2lo = shared(ctx, "w2lo", [P, BCW], F32R)
        phase_token(nc, d, g)
        g.acc = shared(ctx, "acc", [P, TT, E])
        g.G = shared(ctx, "G", [P, TT, 2, CHUNK])
        phase_decays(nc, d, g)
        g.sqa = shared(ctx, "sqa", [P, NT, TBW])
        phase_mixer(nc, d, g)
        g.fhi = shared(ctx, "fhi", [P, 2, 2 * E], F32R)
        g.flo = shared(ctx, "flo", [P, 2, 2 * E], F32R)
        phase_norm(nc, d, g)
        phase_ffn(nc, d, g)
        phase_out(nc, d, g, out)


def kernel(**inputs):
    import numpy as np
    import concourse.bacc as bacc
    from concourse.bass_utils import run_bass_kernel_spmd

    a = {k: np.asarray(v) for k, v in inputs.items()}
    lay = np.ascontiguousarray

    def tiles(w):
        r = w.shape[0] // P
        return w.reshape(r, P, KE, P).transpose(0, 3, 2, 1).reshape(r, P, E)

    W_in = a["L0_attn_W_in"]
    gate, hidden, bc, dtw = W_in[:INTER], W_in[INTER:2 * INTER], W_in[2 * INTER:2 * INTER + 2 * P], W_in[2 * INTER + 2 * P:]
    cw, cb = a["L0_attn_conv_w"], a["L0_attn_conv_b"]
    par = np.zeros((NJ, P, NPAR), np.float32)
    par[:, :, 0:4] = cw[:INTER].reshape(NJ, P, TAPS)
    par[:, :, 4] = cb[:INTER].reshape(NJ, P)
    par[:, :, 5] = a["L0_attn_norm_w"].reshape(NJ, P)
    par[:, :, 6] = np.repeat(a["L0_attn_D"], HD).reshape(NJ, P)
    par_bc = np.zeros((P, 2, NPAR), np.float32)
    par_bc[:, :, 0:4] = cw[INTER:].reshape(2, P, TAPS).transpose(1, 0, 2)
    par_bc[:, :, 4] = cb[INTER:].reshape(2, P).T
    k, s_ = np.arange(P)[:, None], np.arange(P)[None, :]
    mask = np.zeros((P, P + 1), np.float32)
    mask[:, :P] = (k // CHUNK == s_ // CHUNK) & ((k > s_) | (k % CHUNK == 0))
    mask[:, P] = np.arange(P) % CHUNK == 0
    arrays = {
        "x": lay(a["x"].transpose(3, 2, 1, 0).reshape(P, H, NB)),
        "log_dt": a["L0_tok_log_dt"],
        "tokpar": lay(np.stack([a["L0_tok_inv_A_real"], a["L0_tok_A_imag"], a["L0_tok_B_ri"][..., 0],
                                a["L0_tok_B_ri"][..., 1]]).reshape(4, 2, H // 2, NS).transpose(1, 3, 0, 2).reshape(P, 4, H // 2)),
        "ident": np.eye(P, dtype=np.float32),
        "eye64": np.tile(np.eye(CHUNK, dtype=np.float32), (2, 1)),
        "mask": mask,
        "A_log": a["L0_attn_A_log"],
        "dt_bias": a["L0_attn_dt_bias"].reshape(HEADS, 1),
        "w_bc": lay(np.concatenate([tiles(bc)[0], tiles(bc)[1],
                                    dtw.reshape(HEADS, KE, P).transpose(2, 1, 0).reshape(P, KE * HEADS)], 1)),
        "par_bc": par_bc,
        "w_mix": lay(np.concatenate([tiles(hidden), tiles(gate), par], 2)),
        "w_out": lay(a["L0_attn_W_out"].T.reshape(NJ // 2, 2, P, E)),
        "w_ffn": lay(np.concatenate([tiles(a["L0_ffn_w_gate"]), tiles(a["L0_ffn_w_up"])], 2)),
        "w_down": lay(a["L0_ffn_w_down"].T.reshape(NM // 2, 2, P, E)),
    }
    nc = bacc.Bacc("TRN2", target_bir_lowering=False, num_devices=1)
    d = {n: nc.dram_tensor("in_" + n, v.shape, F32, kind="ExternalInput").ap() for n, v in arrays.items()}
    d["decay"] = nc.dram_tensor("decay", (NJ, 2, NT, 2, CP * CHUNK), F32, kind="Internal").ap()
    d["dtz"] = nc.dram_tensor("dtz", (NJ, P, 2 * NT * 2 * CP), F32, kind="Internal").ap()
    out = nc.dram_tensor("out0", (NB, H, E), F32, kind="ExternalOutput").ap()
    build(nc, d, out)
    r = run_bass_kernel_spmd(nc, [{"in_" + n: v for n, v in arrays.items()}], core_ids=[0])
    return r.results[0]["out0"]
```
